# Optimizing a Trainium2 kernel written in Bass

```python
import numpy as np
import jax
import jax.numpy as jnp

def _softmax(x, axis=-1):
    return jax.nn.softmax(x, axis=axis)

def _gelu(x):
    return jax.nn.gelu(x, approximate=True)

def _silu(x):
    return jax.nn.silu(x)

def _sigmoid(x):
    return jax.nn.sigmoid(x)

def _layernorm(x, axis=-1, eps=1e-05):
    m = jnp.mean(x, axis=axis, keepdims=True)
    v = jnp.var(x, axis=axis, keepdims=True)
    return (x - m) / jnp.sqrt(v + eps)

def _scatter_add(tgt, idx, src, axis=0):
    return tgt.at[idx].add(src)

def _segment_sum(src, seg, n):
    return jax.ops.segment_sum(src, seg, n)
kernel_name = 'mk_perceiver_d1_seqx_r2_a7460b'

def setup_inputs(seed: int=0):
    np.random.seed(seed)
    _w = jnp.asarray

    def _rec_inputs():
        import jax
        import jax.numpy as jnp
        _rk = jax.random.key(seed)
        x = -0.0002928 + 1 * jax.random.normal(jax.random.fold_in(_rk, 1), (32, 32, 512), jnp.float32)
        _lenS = 32 - jax.random.randint(jax.random.fold_in(_rk, 7), (32,), 0, max(1, 32 // 4) + 1, jnp.int32)
        _lenS2 = 257 - jax.random.randint(jax.random.fold_in(_rk, 8), (32,), 0, max(1, 257 // 4) + 1, jnp.int32)
        _ctx_1024P = jax.random.normal(jax.random.fold_in(_rk, 11), (32, 16, 512), jnp.float32)
        _ctx_1024c = jax.random.dirichlet(jax.random.fold_in(_rk, 511), 0.3 * jnp.ones((16,), jnp.float32), (32, 257))
        _ctx_1024t = jnp.einsum('bsk,bkd->bsd', _ctx_1024c, _ctx_1024P)
        _ctx_1024t = _ctx_1024t * jax.lax.rsqrt(jnp.mean(jnp.square(_ctx_1024t)) + 1e-12) * 0.953939
        ctx_1024 = -1.39393e-06 + 0.999914 * (_ctx_1024t + 0.3 * jax.random.normal(jax.random.fold_in(_rk, 611), (32, 257, 512), jnp.float32))
        _validS = jnp.arange(32)[None, :] < _lenS[:, None]
        _validS2 = jnp.arange(257)[None, :] < _lenS2[:, None]
        _causal = jnp.tril(jnp.ones((32, 32), dtype=bool))
        mask_1x1xSxS2_ff0 = jnp.where(jnp.ones((1, 1, 32, 257), dtype=bool), 0.0, -1000000000.0).astype(jnp.float32)
        return (x, ctx_1024, mask_1x1xSxS2_ff0)
    x, ctx_1024, mask_1x1xSxS2_ff0 = _rec_inputs()

    def _L0_xattn_setup():
        import jax, jax.numpy as jnp
        import numpy as np
        D_MODEL = 512
        N_HEADS = 16
        HEAD_DIM = D_MODEL // N_HEADS
        key = jax.random.key(seed)
        ks = jax.random.split(key, 12)
        B, S = (2, 1024)
        s = 1.0 / np.sqrt(D_MODEL)
        return {'Q': jax.random.normal(ks[0], (B, S, D_MODEL), jnp.float32), 'K': jax.random.normal(ks[1], (B, S, D_MODEL), jnp.float32), 'V': jax.random.normal(ks[2], (B, S, D_MODEL), jnp.float32), 'mask': jnp.zeros((1, 1, S, S), jnp.float32), 'Wq': jax.random.normal(ks[3], (D_MODEL, D_MODEL), jnp.float32) * s, 'bq': jnp.zeros((D_MODEL,), jnp.float32), 'Wk': jax.random.normal(ks[4], (D_MODEL, D_MODEL), jnp.float32) * s, 'bk': jnp.zeros((D_MODEL,), jnp.float32), 'Wv': jax.random.normal(ks[5], (D_MODEL, D_MODEL), jnp.float32) * s, 'bv': jnp.zeros((D_MODEL,), jnp.float32), 'Wo': jax.random.normal(ks[6], (D_MODEL, D_MODEL), jnp.float32) * s, 'bo': jnp.zeros((D_MODEL,), jnp.float32)}
    _L0_xattn_all = _L0_xattn_setup()
    _L0_xattn_in = {k: v for k, v in _L0_xattn_all.items() if k in ('Wq', 'bq', 'Wk', 'bk', 'Wv', 'bv', 'Wo', 'bo')}
    del _L0_xattn_all

    def _L0_attn_setup():
        import jax, jax.numpy as jnp
        import numpy as np
        D = 512
        H = 16
        HD = D // H
        EPS = 1e-06

        def rms_norm(x, w):
            xf = x.astype(jnp.float32)
            rms = jnp.sqrt(jnp.mean(xf * xf, axis=-1, keepdims=True) + EPS)
            return (xf / rms * w.astype(jnp.float32)).astype(x.dtype)
        key = jax.random.key(seed)
        ks = jax.random.split(key, 6)
        B, S = (2, 1024)
        x = jax.random.normal(ks[0], (B, S, D), dtype=jnp.float32)
        Wqkv = jax.random.normal(ks[1], (3 * D, D), dtype=jnp.float32) * (1.0 / np.sqrt(D))
        bqkv = jax.random.normal(ks[2], (3 * D,), dtype=jnp.float32) * 0.02
        Wproj = jax.random.normal(ks[3], (D, D), dtype=jnp.float32) * (1.0 / np.sqrt(D))
        bproj = jax.random.normal(ks[4], (D,), dtype=jnp.float32) * 0.02
        qn_w = jnp.ones((HD,), dtype=jnp.float32)
        kn_w = jnp.ones((HD,), dtype=jnp.float32)
        return {'x': x, 'Wqkv': Wqkv, 'bqkv': bqkv, 'Wproj': Wproj, 'bproj': bproj, 'qn_w': qn_w, 'kn_w': kn_w}
    _L0_attn_all = _L0_attn_setup()
    _L0_attn_in = {k: v for k, v in _L0_attn_all.items() if k in ('Wqkv', 'bqkv', 'Wproj', 'bproj', 'qn_w', 'kn_w')}
    del _L0_attn_all

    def _L0_ffn_setup():
        import jax, jax.numpy as jnp
        import numpy as np
        B, S, D = (4, 1024, 512)
        P = 9
        DM = D // 4
        EPS = 1e-05

        def _mix(x, mix_kernel):
            xp = jnp.pad(x, ((0, 0), (1, 1), (0, 0)))
            return mix_kernel[0] * xp[:, :-2] + mix_kernel[1] * xp[:, 1:-1] + mix_kernel[2] * xp[:, 2:]

        def _layernorm(h, gamma, beta):
            mu = jnp.mean(h, axis=-1, keepdims=True)
            var = jnp.var(h, axis=-1, keepdims=True)
            return (h - mu) * jax.lax.rsqrt(var + EPS) * gamma + beta
        key = jax.random.key(seed)
        ks = jax.random.split(key, 12)
        sc_in = 1.0 / np.sqrt(D)
        sc_mid = 1.0 / np.sqrt(DM)
        return {'x': jax.random.normal(ks[0], (B, S, D), dtype=jnp.float32), 'mix_kernel': jax.random.normal(ks[1], (3, D), dtype=jnp.float32) * 0.5, 'W1': jax.random.normal(ks[2], (P, D, DM), dtype=jnp.float32) * sc_in, 'b1': jnp.zeros((P, DM), dtype=jnp.float32), 'W2': jax.random.normal(ks[3], (P, DM, D), dtype=jnp.float32) * sc_mid, 'b2': jnp.zeros((P, D), dtype=jnp.float32), 'Wo1': jax.random.normal(ks[4], (D, DM), dtype=jnp.float32) * sc_in, 'bo1': jnp.zeros((DM,), dtype=jnp.float32), 'Wo2': jax.random.normal(ks[5], (DM, P), dtype=jnp.float32) * sc_mid, 'bo2': jnp.zeros((P,), dtype=jnp.float32), 'gamma': jnp.ones((D,), dtype=jnp.float32), 'beta': jnp.zeros((D,), dtype=jnp.float32)}
    _L0_ffn_all = _L0_ffn_setup()
    _L0_ffn_in = {k: v for k, v in _L0_ffn_all.items() if k in ('mix_kernel', 'W1', 'b1', 'W2', 'b2', 'Wo1', 'bo1', 'Wo2', 'bo2', 'gamma', 'beta')}
    del _L0_ffn_all
    return {'x': x, 'ctx_1024': ctx_1024, 'mask_1x1xSxS2_ff0': mask_1x1xSxS2_ff0, 'L0_xattn_Wq': _L0_xattn_in['Wq'], 'L0_xattn_bq': _L0_xattn_in['bq'], 'L0_xattn_Wk': _L0_xattn_in['Wk'], 'L0_xattn_bk': _L0_xattn_in['bk'], 'L0_xattn_Wv': _L0_xattn_in['Wv'], 'L0_xattn_bv': _L0_xattn_in['bv'], 'L0_xattn_Wo': _L0_xattn_in['Wo'], 'L0_xattn_bo': _L0_xattn_in['bo'], 'L0_attn_Wqkv': _L0_attn_in['Wqkv'], 'L0_attn_bqkv': _L0_attn_in['bqkv'], 'L0_attn_Wproj': _L0_attn_in['Wproj'], 'L0_attn_bproj': _L0_attn_in['bproj'], 'L0_attn_qn_w': _L0_attn_in['qn_w'], 'L0_attn_kn_w': _L0_attn_in['kn_w'], 'L0_ffn_mix_kernel': _L0_ffn_in['mix_kernel'], 'L0_ffn_W1': _L0_ffn_in['W1'], 'L0_ffn_b1': _L0_ffn_in['b1'], 'L0_ffn_W2': _L0_ffn_in['W2'], 'L0_ffn_b2': _L0_ffn_in['b2'], 'L0_ffn_Wo1': _L0_ffn_in['Wo1'], 'L0_ffn_bo1': _L0_ffn_in['bo1'], 'L0_ffn_Wo2': _L0_ffn_in['Wo2'], 'L0_ffn_bo2': _L0_ffn_in['bo2'], 'L0_ffn_gamma': _L0_ffn_in['gamma'], 'L0_ffn_beta': _L0_ffn_in['beta']}

def reference(x, ctx_1024, mask_1x1xSxS2_ff0, L0_xattn_Wq, L0_xattn_bq, L0_xattn_Wk, L0_xattn_bk, L0_xattn_Wv, L0_xattn_bv, L0_xattn_Wo, L0_xattn_bo, L0_attn_Wqkv, L0_attn_bqkv, L0_attn_Wproj, L0_attn_bproj, L0_attn_qn_w, L0_attn_kn_w, L0_ffn_mix_kernel, L0_ffn_W1, L0_ffn_b1, L0_ffn_W2, L0_ffn_b2, L0_ffn_Wo1, L0_ffn_bo1, L0_ffn_Wo2, L0_ffn_bo2, L0_ffn_gamma, L0_ffn_beta):
    import jax
    import jax.numpy as jnp

    def _L0_xattn_ref(Q, K, V, mask, Wq, bq, Wk, bk, Wv, bv, Wo, bo):
        import jax, jax.numpy as jnp
        import numpy as np
        D_MODEL = 512
        N_HEADS = 16
        HEAD_DIM = D_MODEL // N_HEADS
        B, Sq, _ = Q.shape
        Sk = K.shape[1]
        q = (Q @ Wq.T + bq).reshape(B, Sq, N_HEADS, HEAD_DIM).transpose(0, 2, 1, 3)
        k = (K @ Wk.T + bk).reshape(B, Sk, N_HEADS, HEAD_DIM).transpose(0, 2, 1, 3)
        v = (V @ Wv.T + bv).reshape(B, Sk, N_HEADS, HEAD_DIM).transpose(0, 2, 1, 3)
        scores = jnp.einsum('bhqd,bhkd->bhqk', q, k) / jnp.sqrt(jnp.asarray(HEAD_DIM, q.dtype))
        scores = scores + mask
        attn = jax.nn.softmax(scores, axis=-1)
        out = jnp.einsum('bhqk,bhkd->bhqd', attn, v)
        out = out.transpose(0, 2, 1, 3).reshape(B, Sq, D_MODEL)
        return out @ Wo.T + bo

    def _L0_attn_ref(x, Wqkv, bqkv, Wproj, bproj, qn_w, kn_w):
        import jax, jax.numpy as jnp
        import numpy as np
        D = 512
        H = 16
        HD = D // H
        EPS = 1e-06

        def rms_norm(x, w):
            xf = x.astype(jnp.float32)
            rms = jnp.sqrt(jnp.mean(xf * xf, axis=-1, keepdims=True) + EPS)
            return (xf / rms * w.astype(jnp.float32)).astype(x.dtype)
        B, S, _ = x.shape
        qkv = x @ Wqkv.T + bqkv
        qkv = qkv.reshape(B, S, 3, H, HD)
        q, k, v = (qkv[:, :, 0], qkv[:, :, 1], qkv[:, :, 2])
        q = rms_norm(q, qn_w)
        k = rms_norm(k, kn_w)
        q = q.transpose(0, 2, 1, 3)
        k = k.transpose(0, 2, 1, 3)
        v = v.transpose(0, 2, 1, 3)
        scale = 1.0 / np.sqrt(HD)
        scores = jnp.einsum('bhsd,bhtd->bhst', q, k) * scale
        attn = jax.nn.softmax(scores, axis=-1)
        out = jnp.einsum('bhst,bhtd->bhsd', attn, v)
        out = out.transpose(0, 2, 1, 3).reshape(B, S, D)
        return out @ Wproj.T + bproj

    def _L0_ffn_ref(x, mix_kernel, W1, b1, W2, b2, Wo1, bo1, Wo2, bo2, gamma, beta):
        import jax, jax.numpy as jnp
        import numpy as np
        B, S, D = (4, 1024, 512)
        P = 9
        DM = D // 4
        EPS = 1e-05

        def _mix(x, mix_kernel):
            xp = jnp.pad(x, ((0, 0), (1, 1), (0, 0)))
            return mix_kernel[0] * xp[:, :-2] + mix_kernel[1] * xp[:, 1:-1] + mix_kernel[2] * xp[:, 2:]

        def _layernorm(h, gamma, beta):
            mu = jnp.mean(h, axis=-1, keepdims=True)
            var = jnp.var(h, axis=-1, keepdims=True)
            return (h - mu) * jax.lax.rsqrt(var + EPS) * gamma + beta
        x_mixed = _mix(x, mix_kernel)
        h = jnp.einsum('bsd,pdm->bspm', x_mixed, W1) + b1
        stacked_paths = jnp.einsum('bspm,pmd->bspd', h, W2) + b2
        scores = jnp.tanh(x_mixed @ Wo1 + bo1) @ Wo2 + bo2
        idx = jnp.argmax(scores, axis=-1)
        weights = jax.nn.one_hot(idx, P, dtype=stacked_paths.dtype)
        collapsed = jnp.einsum('bspd,bsp->bsd', stacked_paths, weights)
        return _layernorm(x + collapsed, gamma, beta)
    x = x + _L0_xattn_ref(_layernorm(x, axis=-1), ctx_1024, ctx_1024, mask_1x1xSxS2_ff0, L0_xattn_Wq, L0_xattn_bq, L0_xattn_Wk, L0_xattn_bk, L0_xattn_Wv, L0_xattn_bv, L0_xattn_Wo, L0_xattn_bo)
    x = x + _L0_attn_ref(_layernorm(x, axis=-1), L0_attn_Wqkv, L0_attn_bqkv, L0_attn_Wproj, L0_attn_bproj, L0_attn_qn_w, L0_attn_kn_w)
    x = x + _L0_ffn_ref(_layernorm(x, axis=-1), L0_ffn_mix_kernel, L0_ffn_W1, L0_ffn_b1, L0_ffn_W2, L0_ffn_b2, L0_ffn_Wo1, L0_ffn_bo1, L0_ffn_Wo2, L0_ffn_bo2, L0_ffn_gamma, L0_ffn_beta)
    return x

_drawn_inputs = setup_inputs


def setup_inputs(seed=0):
    import zlib

    import numpy as np

    out = dict(_drawn_inputs(seed))
    spreads = {'L0_xattn_bq': (0.0, 0.1),
     'L0_xattn_bk': (0.0, 0.1),
     'L0_xattn_bv': (0.0, 0.1),
     'L0_xattn_bo': (0.0, 0.1),
     'L0_attn_qn_w': (1.0, 0.2),
     'L0_attn_kn_w': (1.0, 0.2),
     'L0_ffn_b1': (0.0, 0.1),
     'L0_ffn_b2': (0.0, 0.1),
     'L0_ffn_bo1': (0.0, 0.1),
     'L0_ffn_bo2': (0.0, 0.1),
     'L0_ffn_gamma': (1.0, 0.2),
     'L0_ffn_beta': (0.0, 0.1)}
    factors = {}
    for name, (base, spread) in spreads.items():
        noise = np.random.default_rng([zlib.crc32(name.encode()), seed]).standard_normal(out[name].shape)
        drawn = base * np.exp(spread * noise) if base else spread * noise
        out[name] = jnp.asarray(drawn.astype(out[name].dtype))
    for name, factor in factors.items():
        out[name] = (out[name] * factor).astype(out[name].dtype)
    return out
```

```python
import numpy as np
import concourse.bass as bass
from concourse import mybir
from contextlib import ExitStack

F32 = mybir.dt.float32
F32R = mybir.dt.float32r
I32 = mybir.dt.int32
ALU = mybir.AluOpType
ACT = mybir.ActivationFunctionType
AX = mybir.AxisListType

P = 128
D = 512
H, HD = 16, 32
B, S = 32, 32
T = B * S
NT = T // P
CT = D // P
SK = 257
SM = 256
NPAIR = B // 2
E = 9
DM = P
SCALE = 1.0 / float(np.sqrt(HD))
LN_EPS = 1e-5
RMS_EPS = 1e-6
BIG = 3.0e38


def need(eng, sem, value):
    if isinstance(value, (int, np.integer)) and value <= 0:
        return
    eng.wait_ge(sem, value)


class Chain:

    def __init__(self, eng, sem, start=0):
        self.eng, self.sem, self.start, self.k = eng, sem, start, 0

    def link(self, ins):
        self.k += 1
        ins.then_inc(self.sem, 1)
        self.eng.wait_ge(self.sem, self.start + self.k)


def rsqrt(eng, ch, y, v, t):
    ch.link(eng.tensor_scalar(t.bitcast(I32), v.bitcast(I32), 1, None, ALU.arith_shift_right))
    ch.link(eng.tensor_scalar(y.bitcast(I32), t.bitcast(I32), -1.0, 1597463007.0, ALU.mult, ALU.add))
    for _ in range(4):
        ch.link(eng.scalar_tensor_tensor(out=t, in0=y, scalar=-0.5, in1=y, op0=ALU.mult, op1=ALU.mult))
        ch.link(eng.tensor_tensor(t, t, v, ALU.mult))
        ch.link(eng.scalar_tensor_tensor(out=y, in0=t, scalar=1.5, in1=y, op0=ALU.add, op1=ALU.mult))


def build(nc, io, out):
    ctx = ExitStack()
    with ctx:
        def sb(name, shape, dt=F32, c=ctx):
            return c.enter_context(nc.sbuf_tensor(name, shape, dt))

        def sem(name, c=ctx):
            return c.enter_context(nc.semaphore(name))

        x_nat = sb("x_nat", [P, NT, D])
        ident = sb("ident", [P, P])
        ln3 = sb("ln3", [P, NT, 2])
        raw = sb("raw", [P, 2, CT * D])
        O_T = sb("O_T", [P, CT, T])
        w_in = [sem(f"w_in{i}") for i in range(2)]
        cross_attention(nc, io, x_nat, ident, O_T, raw, w_in)
        self_attention(nc, io, x_nat, ident, O_T, raw, w_in, ln3)
        experts(nc, io, out, x_nat, ident, ln3, O_T, raw)


def three(eng, out, a_hi, a_lo, b_hi, b_lo, first, last):
    eng.matmul(out, a_hi, b_hi, start=first, stop=False)
    eng.matmul(out, a_lo, b_hi, start=False, stop=False)
    return eng.matmul(out, a_hi, b_lo, start=False, stop=last)


def cross_attention(nc, io, x_nat, ident, O_T, raw, w_in):
    with ExitStack() as ctx:
        def sb(name, shape, dt=F32):
            return ctx.enter_context(nc.sbuf_tensor(name, shape, dt))

        def ps(name, shape):
            return ctx.enter_context(nc.psum_tensor(name, shape, F32))

        def sem(name):
            return ctx.enter_context(nc.semaphore(name))

        c_hi = [sb(f"c_hi{i}", [P, CT, D], F32R) for i in range(2)]
        c_lo = [sb(f"c_lo{i}", [P, CT, D], F32R) for i in range(2)]
        wk_hi, wk_lo = sb("wk_hi", [P, CT, D], F32R), sb("wk_lo", [P, CT, D], F32R)
        wv_hi, wv_lo = sb("wv_hi", [P, CT, D], F32R), sb("wv_lo", [P, CT, D], F32R)
        KW = SM + 2
        kf_hi, kf_lo = sb("kf_hi", [P, CT * 2 * KW], F32R), sb("kf_lo", [P, CT * 2 * KW], F32R)
        K_hi = kf_hi[:, :].rearrange("p (g j n) -> p g j n", g=CT, j=2)
        K_lo = kf_lo[:, :].rearrange("p (g j n) -> p g j n", g=CT, j=2)
        wq_hi = kf_hi[:, 0:CT * D].rearrange("p (c n) -> p c n", c=CT)
        wq_lo = kf_lo[:, 0:CT * D].rearrange("p (c n) -> p c n", c=CT)
        V = sb("V", [P, 4, D])
        masked = sb("masked", [P, 2, CT, SK])
        probs = sb("probs", [P, 2, CT, SK])
        P_T = sb("P_T", [P, 2, 2, D])
        Qd_hi = [sb(f"Qd_hi{j}", [P, CT, P], F32R) for j in range(2)]
        Qd_lo = [sb(f"Qd_lo{j}", [P, CT, P], F32R) for j in range(2)]
        Q_T = sb("Q_T", [P, CT, T])
        mask = sb("mask", [P, SK])
        bq, bk = sb("bq", [P, CT]), sb("bk", [P, CT])
        tail = sb("tail", [P, CT, B])
        t_hi, t_lo = sb("t_hi", [P, CT, B], F32R), sb("t_lo", [P, CT, B], F32R)
        tail_nat = sb("tail_nat", [B, 2, D])
        kt32 = sb("kt32", [P, CT, B])
        kt_hi, kt_lo = sb("kt_hi", [P, CT, B], F32R), sb("kt_lo", [P, CT, B], F32R)
        vt = sb("vt", [P, CT, B])
        same_head = sb("same_head", [P, P])
        same_q = sb("same_q", [P, S])
        q_b_hi, q_b_lo = sb("q_b_hi", [P, CT, S], F32R), sb("q_b_lo", [P, CT, S])
        stats, mv = sb("stats", [P, NT, 6]), sb("mv", [P, NT, 2])
        var, rstd, tmp8 = sb("var", [P, NT]), sb("rstd", [P, NT]), sb("tmp8", [P, NT])
        z = sb("z", [P, 2, D])
        nmax, psum_, rinv = sb("nmax", [P, 2, CT]), sb("psum_", [P, 2, CT]), sb("rinv", [P, 2, CT])
        dtail = sb("dtail", [P, CT, S])
        otail = sb("otail", [P, 2, CT, S])

        pj = [ps(f"pj{i}", [P, D]) for i in range(2)]
        sc = [ps(f"sc{i}", [P, D]) for i in range(2)]
        tp = ps("tp", [P, 2, D])
        sc = sc + [tp[:, 0, :], tp[:, 1, :]]
        po = ps("po", [P, D])
        pb = ps("pb", [P, D])

        x_in, wq_in, wv_in, wk_in, small_in = (sem(n) for n in ("x_in", "wq_in", "wv_in", "wk_in", "small_in"))
        ctx_in = [sem(f"ctx_in{i}") for i in range(2)]
        const_made, z_made, zT_done, zT_hi, zT_lo = (sem(n) for n in ("const_made", "z_made", "zT_done", "zT_hi", "zT_lo"))
        w_hi, w_lo, q_done, q_out = (sem(n) for n in ("w_hi", "w_lo", "q_done", "q_out"))
        tail_done, tail_out, tailT_done, tailT_out = (sem(n) for n in ("tail_done", "tail_out", "tailT_done", "tailT_out"))
        bias_made, dve_step = sem("bias_made"), sem("dve_step")
        ctx_hi, ctx_lo, kv_done, k_hi, k_lo, v_out = (sem(n) for n in ("ctx_hi", "ctx_lo", "kv_done", "k_hi", "k_lo", "v_out"))
        k_tail, q_hi, q_lo, qd_made = (sem(n) for n in ("k_tail", "q_hi", "q_lo", "qd_made"))
        ident_made, heads_made = sem("ident_made"), sem("heads_made")
        s_done, masked_made, exp_done, rinv_made, probs_made = (sem(n) for n in ("s_done", "masked_made", "exp_done", "rinv_made", "probs_made"))
        dt_made, pb_done, ot_made, tr_done, pt_act, pt_dve, pv_done, o_out = (
            sem(n) for n in ("dt_made", "pb_done", "ot_made", "tr_done", "pt_act", "pt_dve", "pv_done", "o_out"))

        s_seen, q_hi_seen = sem("s_seen"), sem("q_hi_seen")

        block = ctx.enter_context(nc.Block())

        @block.sync
        def _(eng):
            eng.dma_start(x_nat[:, :, :], io["x"]).then_inc(x_in, 16)
            eng.dma_start(raw[:, 0, :], io["wq"]).then_inc(wq_in, 16)
            eng.dma_start(bq[:, :], io["bq"]).then_inc(small_in, 16)
            eng.dma_start(bk[:, :], io["bk"]).then_inc(small_in, 16)
            eng.dma_start(tail[:, :, :], io["tail"]).then_inc(small_in, 16)
            for h in range(4):
                eng.dma_start(mask[h * S:(h + 1) * S, :], io["mask"]).then_inc(small_in, 16)
            eng.dma_start(raw[:, 1, :], io["wk"]).then_inc(wk_in, 16)
            eng.wait_ge(w_lo, 1)
            eng.dma_start(raw[:, 0, :], io["wv"]).then_inc(wv_in, 16)
            eng.wait_ge(w_lo, 2)
            eng.dma_start(raw[:, 1, :], io["ctx"][1]).then_inc(ctx_in[1], 16)
            eng.wait_ge(w_lo, 3)
            eng.dma_start(raw[:, 0, :], io["ctx"][0]).then_inc(ctx_in[0], 16)
            with eng.Fori(1, NT) as i:
                for p in range(2):
                    n = 2 * i + p
                    eng.wait_ge(ctx_lo, n - 1)
                    eng.dma_start(raw[:, p, :], io["ctx"][n]).then_inc(ctx_in[p], 16)
            for p in range(2):
                eng.wait_ge(ctx_lo, NPAIR - 1 + p)
                eng.dma_start(raw[:, p, :], io["w5"][p]).then_inc(w_in[p], 16)

        @block.gpsimd
        def _(eng):
            eng.memset(ident[:, :], 0.0).then_inc(const_made, 1)
            eng.wait_ge(const_made, 1)
            eng.affine_select(out=ident[:, :], in_=ident[:, :], compare_op=ALU.not_equal, fill=1.0,
                              base=0, pattern=[[-1, P]], channel_multiplier=1).then_inc(ident_made, 1)
            eng.wait_ge(heads_made, 9)
            eng.wait_ge(q_out, 8)

            def q_blocks(n, j):
                b = 2 * n + j
                cols = bass.ds(b * S, S)
                need(eng, qd_made, 2 * b)
                eng.tensor_copy(q_b_hi[:, :, :], Q_T[:, :, cols]).then_inc(q_hi, 1)
                eng.wait_ge(q_hi, b + 1)
                eng.sem_inc(q_hi_seen, 1)
                eng.tensor_tensor(q_b_lo[:, :, :], Q_T[:, :, cols], q_b_hi[:, :, :].bitcast(F32), ALU.subtract).then_inc(q_lo, 1)
                need(eng, s_done, 4 * (b - 1))
                eng.wait_ge(q_lo, b + 1)
                for Qd, q in ((Qd_hi, q_b_hi[:, :, :].bitcast(F32)), (Qd_lo, q_b_lo)):
                    eng.tensor_tensor(Qd[j][:, :, :].rearrange("p g (h s) -> p g h s", h=4),
                                      q[:, :, :].unsqueeze(2).broadcast_to([P, CT, 4, S]),
                                      same_head[:, :].rearrange("p (h s) -> p h s", h=4).unsqueeze(1).broadcast_to([P, CT, 4, S]),
                                      ALU.mult).then_inc(qd_made, 1)

            def pair(n):
                need(eng, s_done, 8 * n)
                if isinstance(n, int) and n == 0:
                    eng.wait_ge(tailT_out, 5)
                for j in range(2):
                    for K, kt in ((K_hi, kt_hi), (K_lo, kt_lo)):
                        eng.tensor_copy(K[:, :, j, SM:KW],
                                        kt[:, :, bass.ds(2 * n + j, 1)].broadcast_to([P, CT, 2])).then_inc(k_tail, 1)
                q_blocks(n, 0)
                q_blocks(n, 1)

            pair(0)
            pair(1)
            with eng.Fori(1, NT) as i:
                pair(2 * i)
                pair(2 * i + 1)

        @block.tensor
        def _(eng):
            def z_transposes(t):
                eng.wait_ge(z_made, t + 1)
                if t == 0:
                    eng.wait_ge(ident_made, 1)
                need(eng, zT_lo, t - 1)
                for c in range(CT):
                    mm = eng.transpose(tp[:, t % 2, c * P:(c + 1) * P], z[:, t % 2, c * P:(c + 1) * P], ident[:, :])
                mm.then_inc(zT_done, 1)

            def q_proj(hf):
                for g in range(CT):
                    k = CT * hf + g
                    if g == 0:
                        eng.wait_ge(zT_lo, 4 * (hf + 1))
                        eng.wait_ge(w_lo, 1)
                    need(eng, q_out, k - 1)
                    for c in range(CT):
                        mm = three(eng, pj[k % 2][:, :], wq_hi[:, c, g * P:(g + 1) * P], wq_lo[:, c, g * P:(g + 1) * P],
                                   c_hi[hf][:, c, :], c_lo[hf][:, c, :], c == 0, c == CT - 1)
                    mm.then_inc(q_done, 1)

            def tails():
                eng.wait_ge(w_lo, 4)
                for i, (hi, lo) in enumerate(((wk_hi, wk_lo), (wv_hi, wv_lo))):
                    for c in range(CT):
                        mm = three(eng, sc[i][0:B, :], t_hi[:, c, :], t_lo[:, c, :], hi[:, c, :], lo[:, c, :],
                                   c == 0, c == CT - 1)
                    mm.then_inc(tail_done, 1)
                for i in range(2):
                    eng.wait_ge(tail_out, i + 1)
                    for g in range(CT):
                        mm = eng.transpose(pb[:, (i * CT + g) * B:(i * CT + g + 1) * B],
                                           tail_nat[:, i, g * P:(g + 1) * P], ident[0:B, 0:B])
                mm.then_inc(tailT_done, 1)

            for t in range(4):
                z_transposes(t)
            q_proj(0)
            for t in range(4, NT):
                z_transposes(t)
            q_proj(1)
            tails()

            def k_tile(n, p, g):
                if g == 0:
                    eng.wait_ge(ctx_lo, n + 1)
                if g < 2:
                    need(eng, v_out, 4 * n - 1 + g)
                    if isinstance(n, int) and n == 0:
                        eng.wait_ge(q_out, 7 + g)
                else:
                    eng.wait_ge(k_lo, 4 * n + g - 1)
                for c in range(CT):
                    mm = three(eng, pj[g % 2][:, :], wk_hi[:, c, g * P:(g + 1) * P], wk_lo[:, c, g * P:(g + 1) * P],
                               c_hi[p][:, c, :], c_lo[p][:, c, :], c == 0, c == CT - 1)
                mm.then_inc(kv_done, 1)

            def v_tile(n, p, t):
                if t < 2:
                    eng.wait_ge(k_lo, 4 * n + 3 + t)
                else:
                    eng.wait_ge(v_out, 4 * n + t - 1)
                for c in range(CT):
                    mm = three(eng, pj[t % 2][:, :], c_hi[p][:, c, t * P:(t + 1) * P], c_lo[p][:, c, t * P:(t + 1) * P],
                               wv_hi[:, c, :], wv_lo[:, c, :], c == 0, c == CT - 1)
                mm.then_inc(kv_done, 1)

            def scores(n, j):
                eng.wait_ge(k_lo, 4 * n + 4)
                eng.wait_ge(k_tail, 4 * n + 2 * j + 2)
                eng.wait_ge(qd_made, 2 * (2 * n + j + 1))
                for g in range(CT):
                    need(eng, masked_made, 8 * n + 4 * (j - 1) + g + 1)
                    if g == 2 and j == 0:
                        need(eng, pt_act, 2 * n)
                        need(eng, pt_dve, 2 * n)
                    three(eng, sc[g][:, 0:KW], Qd_hi[j][:, g, :], Qd_lo[j][:, g, :],
                          K_hi[:, g, j, :], K_lo[:, g, j, :], True, True).then_inc(s_done, 1)

            def transposes(n, j):
                b = 2 * n + j
                eng.wait_ge(probs_made, 4 * (b + 1))
                eng.wait_ge(masked_made, 8 * (n + 1))
                need(eng, pt_act, b)
                need(eng, pt_dve, b)
                for k in range(2):
                    for g in range(CT):
                        mm = eng.transpose(tp[:, k, g * P:(g + 1) * P], probs[:, j, g, k * P:(k + 1) * P], ident[:, :])
                mm.then_inc(tr_done, 1)
                eng.wait_ge(dt_made, b + 1)
                need(eng, ot_made, b)
                eng.matmul(pb[:, 0:P], same_head[:, :], dtail[:, :, :].rearrange("p g s -> p (g s)"),
                           start=True, stop=True).then_inc(pb_done, 1)

            def weighted_sum(n, j):
                b = 2 * n + j
                eng.wait_ge(pt_act, b + 1)
                eng.wait_ge(pt_dve, b + 1)
                eng.wait_ge(v_out, 4 * (n + 1))
                need(eng, o_out, 4 * b)
                for g in range(CT):
                    for k in range(2):
                        mm = eng.matmul(po[:, g * P:(g + 1) * P], V[:, 2 * j + k, g * P:(g + 1) * P],
                                        P_T[:, j, k, g * P:(g + 1) * P], start=k == 0, stop=k == 1)
                mm.then_inc(pv_done, 1)

            def pair(n, p, first):
                k_tile(n, p, 0)
                if not first:
                    transposes(n - 1, 1)
                k_tile(n, p, 1)
                if not first:
                    weighted_sum(n - 1, 0)
                k_tile(n, p, 2)
                if not first:
                    weighted_sum(n - 1, 1)
                k_tile(n, p, 3)
                v_tile(n, p, 0)
                scores(n, 0)
                v_tile(n, p, 1)
                scores(n, 1)
                v_tile(n, p, 2)
                transposes(n, 0)
                v_tile(n, p, 3)

            pair(0, 0, True)
            pair(1, 1, False)
            with eng.Fori(1, NT) as i:
                pair(2 * i, 0, False)
                pair(2 * i + 1, 1, False)
            transposes(NPAIR - 1, 1)
            weighted_sum(NPAIR - 1, 0)
            weighted_sum(NPAIR - 1, 1)

        @block.scalar
        def _(eng):
            def split_hi(dst, src):
                return eng.activation(dst, src, ACT.Copy)

            eng.wait_ge(wq_in, 16)
            split_hi(wq_hi, raw[:, 0, :].rearrange("p (c n) -> p c n", c=CT)).then_inc(w_hi, 1)
            eng.wait_ge(wk_in, 16)
            split_hi(wk_hi[:, :, :], raw[:, 1, :].rearrange("p (c n) -> p c n", c=CT)).then_inc(w_hi, 1)

            def z_hi(t):
                eng.wait_ge(zT_done, t + 1)
                split_hi(c_hi[t // 4][:, :, t % 4 * P:(t % 4 + 1) * P],
                         tp[:, t % 2, :].rearrange("p (c n) -> p c n", c=CT)).then_inc(zT_hi, 1)

            def q_evac(k):
                eng.wait_ge(q_done, k + 1)
                if k == 0:
                    eng.wait_ge(bias_made, 1)
                eng.activation(Q_T[:, k % CT, k // CT * D:(k // CT + 1) * D], pj[k % 2][:, :], ACT.Identity,
                               bias=bq[:, k % CT:k % CT + 1], scale=SCALE).then_inc(q_out, 1)

            for t in range(4):
                z_hi(t)
            for k in range(CT):
                q_evac(k)
            for t in range(4, NT):
                z_hi(t)
            for k in range(CT, 2 * CT):
                q_evac(k)
            eng.wait_ge(wv_in, 16)
            split_hi(wv_hi[:, :, :], raw[:, 0, :].rearrange("p (c n) -> p c n", c=CT)).then_inc(w_hi, 1)
            eng.wait_ge(small_in, 7 * 16)
            split_hi(t_hi[:, :, :], tail[:, :, :]).then_inc(w_hi, 1)
            for i in range(2):
                eng.wait_ge(tail_done, i + 1)
                eng.activation(tail_nat[:, i, :], sc[i][0:B, :], ACT.Copy).then_inc(tail_out, 1)
            eng.wait_ge(tailT_out, 1)
            split_hi(kt_hi[:, :, :], kt32[:, :, :]).then_inc(tailT_out, 1)

            def ctx_split(n, p, i):
                eng.wait_ge(ctx_in[p], 16 * (i + 1))
                need(eng, kv_done, 8 * (n - 1))
                if isinstance(n, int) and n < 2:
                    eng.wait_ge(q_done, 4 * (n + 1))
                split_hi(c_hi[p][:, :, :], raw[:, p, :].rearrange("p (c n) -> p c n", c=CT)).then_inc(ctx_hi, 1)

            def k_evac(n, g):
                eng.wait_ge(kv_done, 8 * n + g + 1)
                if g == 0:
                    need(eng, s_done, 8 * n)
                eng.activation(K_hi[:, g, :, 0:SM], pj[g % 2][:, :].rearrange("p (j n) -> p j n", j=2),
                               ACT.Identity, bias=bk[:, g:g + 1]).then_inc(k_hi, 1)

            def v_evac(n, t):
                eng.wait_ge(kv_done, 8 * n + 5 + t)
                if t == 0:
                    need(eng, pv_done, 2 * n)
                eng.activation(V[:, t, :], pj[t % 2][:, :], ACT.Copy).then_inc(v_out, 1)

            def exps(n, j):
                b = 2 * n + j
                need(eng, tr_done, b - 1)
                need(eng, dt_made, b - 1)
                for g in range(CT):
                    eng.wait_ge(masked_made, 4 * b + g + 1)
                    eng.activation(probs[:, j, g, :], masked[:, j, g, :], ACT.Exp, bias=nmax[:, j, g:g + 1],
                                   scale=-1.0, accum_out=psum_[:, j, g:g + 1]).then_inc(exp_done, 1)

            def pt_evac(n, j):
                b = 2 * n + j
                eng.wait_ge(tr_done, b + 1)
                need(eng, pv_done, b - 1)
                eng.activation(P_T[:, j, 0, :], tp[:, 0, :], ACT.Copy).then_inc(pt_act, 1)

            def pair(n, p, i, first, last):
                k_evac(n, 0)
                if not first:
                    pt_evac(n - 1, 1)
                k_evac(n, 1)
                if not last:
                    ctx_split(n + 1, 1 - p, i + p)
                k_evac(n, 2)
                k_evac(n, 3)
                v_evac(n, 0)
                exps(n, 0)
                v_evac(n, 1)
                exps(n, 1)
                v_evac(n, 2)
                pt_evac(n, 0)
                v_evac(n, 3)

            ctx_split(0, 0, 0)
            pair(0, 0, 0, True, False)
            pair(1, 1, 0, False, False)
            with eng.Fori(1, NT - 1) as i:
                pair(2 * i, 0, i, False, False)
                pair(2 * i + 1, 1, i, False, False)
            pair(NPAIR - 2, 0, NT - 1, False, False)
            pair(NPAIR - 1, 1, NT - 1, False, True)
            pt_evac(NPAIR - 1, 1)

        @block.vector
        def _(eng):
            ch = Chain(eng, dve_step)

            def split_lo(dst, src, hi):
                return eng.tensor_tensor(dst, src, hi.bitcast(F32), ALU.subtract)

            eng.memset(same_head[:, :], 0.0).then_inc(heads_made, 1)
            eng.wait_ge(heads_made, 1)
            eng.wait_ge(ident_made, 1)
            for h in range(4):
                r = slice(h * S, (h + 1) * S)
                eng.memset(same_head[r, r], 1.0).then_inc(heads_made, 1)
                eng.tensor_copy(same_q[r, :], ident[r, r]).then_inc(heads_made, 1)
            eng.wait_ge(x_in, 16)
            for t in range(NT):
                eng.bn_stats(stats[:, t, :], x_nat[:, t, :]).then_inc(dve_step, 1)
                ch.k += 1
            for t in range(NT):
                eng.wait_ge(dve_step, t + 1)
                eng.bn_aggr(mv[:, t, :], stats[:, t, :]).then_inc(dve_step, 1)
                ch.k += 1
            eng.wait_ge(dve_step, ch.k)
            ch.link(eng.tensor_scalar(var[:, :], mv[:, :, 1], LN_EPS, None, ALU.add))
            rsqrt(eng, ch, rstd[:, :], var[:, :], tmp8[:, :])
            eng.wait_ge(small_in, 7 * 16)
            eng.tensor_scalar(bq[:, :], bq[:, :], SCALE, None, ALU.mult).then_inc(bias_made, 1)

            def z_make(t):
                need(eng, zT_done, t - 1)
                eng.tensor_scalar(z[:, t % 2, :], x_nat[:, t, :], mv[:, t, 0:1], rstd[:, t:t + 1],
                                  ALU.subtract, ALU.mult).then_inc(z_made, 1)

            def z_lo(t):
                eng.wait_ge(zT_hi, t + 1)
                cols = slice(t % 4 * P, (t % 4 + 1) * P)
                split_lo(c_lo[t // 4][:, :, cols], tp[:, t % 2, :].rearrange("p (c n) -> p c n", c=CT),
                         c_hi[t // 4][:, :, cols]).then_inc(zT_lo, 1)

            z_make(0)
            z_make(1)
            eng.wait_ge(w_hi, 1)
            split_lo(wq_lo, raw[:, 0, :].rearrange("p (c n) -> p c n", c=CT), wq_hi).then_inc(w_lo, 1)
            for t in range(NT):
                z_lo(t)
                if t + 2 < NT:
                    z_make(t + 2)
                if t == 3:
                    eng.wait_ge(w_hi, 2)
                    split_lo(wk_lo[:, :, :], raw[:, 1, :].rearrange("p (c n) -> p c n", c=CT), wk_hi[:, :, :]).then_inc(w_lo, 1)
            eng.wait_ge(w_hi, 3)
            split_lo(wv_lo[:, :, :], raw[:, 0, :].rearrange("p (c n) -> p c n", c=CT), wv_hi[:, :, :]).then_inc(w_lo, 1)
            eng.wait_ge(w_hi, 4)
            split_lo(t_lo[:, :, :], tail[:, :, :], t_hi[:, :, :]).then_inc(w_lo, 1)
            eng.wait_ge(tailT_done, 1)
            tails_T = pb[:, 0:2 * CT * B].rearrange("p (i g b) -> p i g b", i=2, g=CT)
            eng.tensor_tensor(kt32[:, :, :], tails_T[:, 0], bk[:, :].unsqueeze(2).broadcast_to([P, CT, B]),
                              ALU.add).then_inc(tailT_out, 1)
            eng.wait_ge(tailT_out, 2)
            split_lo(kt_lo[:, :, :], kt32[:, :, :], kt_hi[:, :, :]).then_inc(tailT_out, 2)
            eng.tensor_copy(vt[:, :, :], tails_T[:, 1]).then_inc(tailT_out, 1)

            def ctx_split(n, p):
                eng.wait_ge(ctx_hi, n + 1)
                split_lo(c_lo[p][:, :, :], raw[:, p, :].rearrange("p (c n) -> p c n", c=CT), c_hi[p][:, :, :]).then_inc(ctx_lo, 1)

            def k_evac(n, g):
                eng.wait_ge(k_hi, 4 * n + g + 1)
                eng.scalar_tensor_tensor(out=K_lo[:, g, :, 0:SM], in0=pj[g % 2][:, :].rearrange("p (j n) -> p j n", j=2),
                                         scalar=bk[:, g:g + 1], in1=K_hi[:, g, :, 0:SM].bitcast(F32),
                                         op0=ALU.add, op1=ALU.subtract).then_inc(k_lo, 1)

            def mask_max(n, j):
                b = 2 * n + j
                need(eng, exp_done, 4 * (b - 1))
                for g in range(CT):
                    eng.wait_ge(s_done, 4 * b + g + 1)
                    eng.sem_inc(s_seen, 1)
                    eng.tensor_tensor_reduce(masked[:, j, g, :], sc[g][:, 0:SK], mask[:, :], -1.0, BIG,
                                             ALU.add, ALU.min, nmax[:, j, g:g + 1]).then_inc(masked_made, 1)

            def normalise(n, j):
                b = 2 * n + j
                eng.wait_ge(exp_done, 4 * (b + 1))
                eng.reciprocal(rinv[:, j, :], psum_[:, j, :]).then_inc(rinv_made, 1)
                eng.wait_ge(rinv_made, b + 1)
                for g in range(CT):
                    eng.tensor_scalar(probs[:, j, g, :], probs[:, j, g, :], rinv[:, j, g:g + 1], None,
                                      ALU.mult).then_inc(probs_made, 1)
                eng.wait_ge(probs_made, 4 * (b + 1))
                need(eng, pb_done, b)
                eng.tensor_tensor(dtail[:, :, :], same_q[:, :].unsqueeze(1).broadcast_to([P, CT, S]),
                                  probs[:, j, :, SM:SK].broadcast_to([P, CT, S]), ALU.mult).then_inc(dt_made, 1)

            def pt_evac(n, j):
                b = 2 * n + j
                eng.wait_ge(tr_done, b + 1)
                need(eng, pv_done, b - 1)
                eng.tensor_copy(P_T[:, j, 1, :], tp[:, 1, :]).then_inc(pt_dve, 1)
                eng.wait_ge(pb_done, b + 1)
                need(eng, o_out, 4 * (b - 1))
                eng.tensor_tensor(otail[:, j, :, :], pb[:, 0:P].rearrange("p (g s) -> p g s", g=CT),
                                  vt[:, :, bass.ds(b, 1)].broadcast_to([P, CT, S]), ALU.mult).then_inc(ot_made, 1)

            def o_evac(n, j):
                b = 2 * n + j
                eng.wait_ge(pv_done, b + 1)
                eng.wait_ge(ot_made, b + 1)
                for h in range(4):
                    r = slice(h * S, (h + 1) * S)
                    eng.tensor_tensor(O_T[r, :, bass.ds(b * S, S)], po[r, :].rearrange("p (g n) -> p g n", g=CT)[:, :, r],
                                      otail[r, j, :, :], ALU.add).then_inc(o_out, 1)

            def pair(n, p, first, last):
                k_evac(n, 0)
                if not first:
                    pt_evac(n - 1, 1)
                k_evac(n, 1)
                if not first:
                    o_evac(n - 1, 0)
                if not last:
                    ctx_split(n + 1, 1 - p)
                k_evac(n, 2)
                if not first:
                    o_evac(n - 1, 1)
                k_evac(n, 3)
                mask_max(n, 0)
                mask_max(n, 1)
                normalise(n, 0)
                pt_evac(n, 0)
                normalise(n, 1)

            ctx_split(0, 0)
            pair(0, 0, True, False)
            pair(1, 1, False, False)
            with eng.Fori(1, NT - 1) as i:
                pair(2 * i, 0, False, False)
                pair(2 * i + 1, 1, False, False)
            pair(NPAIR - 2, 0, False, False)
            pair(NPAIR - 1, 1, False, True)
            pt_evac(NPAIR - 1, 1)
            o_evac(NPAIR - 1, 0)
            o_evac(NPAIR - 1, 1)


def layer_norm(eng, ch, stats, mv, rstd, tmp, x, z, seen):
    eng.sem_inc(seen, 1)
    ch.link(eng.bn_stats(stats[:, :], x))
    eng.sem_inc(seen, 1)
    ch.link(eng.bn_aggr(mv[:, :], stats[:, :]))
    ch.link(eng.tensor_scalar(mv[:, 1:2], mv[:, 1:2], LN_EPS, None, ALU.add))
    rsqrt(eng, ch, rstd[:, :], mv[:, 1:2], tmp[:, :])
    return eng.tensor_scalar(z, x, mv[:, 0:1], rstd[:, 0:1], ALU.subtract, ALU.mult)


def row_on_all(v):
    return v.unsqueeze(0).broadcast_to([P, v.shape[0]])


def self_attention(nc, io, x_nat, ident, O_T, raw, w_in, ln3):
    with ExitStack() as ctx:
        def sb(name, shape, dt=F32):
            return ctx.enter_context(nc.sbuf_tensor(name, shape, dt))

        def ps(name, shape):
            return ctx.enter_context(nc.psum_tensor(name, shape, F32))

        def sem(name):
            return ctx.enter_context(nc.semaphore(name))

        w_hi = [sb(f"w5_hi{i}", [P, CT, D], F32R) for i in range(5)]
        w_lo = [sb(f"w5_lo{i}", [P, CT, D], F32R) for i in range(5)]
        bv, bo, bqkv, bproj = sb("bv", [P, CT]), sb("bo", [P, D]), sb("bqkv", [P, 3, D]), sb("bproj", [P, D])
        qk_w = sb("qk_w", [P, 2, HD])
        o_b = sb("o_b", [P, CT, P])
        o_hi, o_lo = sb("o_hi", [P, CT, P], F32R), sb("o_lo", [P, CT, P], F32R)
        stats, mv, rstd, tmp = sb("stats2", [P, 6]), sb("mv2", [P, 2]), sb("rstd2", [P, 1]), sb("tmp2", [P, 1])
        z2, z3s = sb("z2", [P, D]), sb("z3s", [P, D])
        z2_hi, z2_lo = sb("z2_hi", [P, CT, P], F32R), sb("z2_lo", [P, CT, P], F32R)
        qk, v = sb("qk", [P, 2, D]), sb("v", [P, D])
        sq = sb("sq", [P, 2 * D])
        ms, rms, tmp32 = sb("ms", [P, 2 * H]), sb("rms", [P, 2 * H]), sb("tmp32", [P, 2 * H])
        q_T, k_T = sb("q_T", [P, CT, P]), sb("k_T", [P, CT, P])
        mx, sm, rs = sb("mx", [P, H]), sb("sm", [P, H]), sb("rs", [P, H])
        e = sb("e", [P, H * S])
        e_T = sb("e_T", [P, H * S])
        o2_hi, o2_lo = sb("o2_hi", [P, CT, P], F32R), sb("o2_lo", [P, CT, P], F32R)

        pw = [ps(f"pw{i}", [P, D]) for i in range(2)]
        pt = [ps(f"pt{i}", [P, D]) for i in range(2)]
        pa = ps("pa", [P, 4, D])

        small_in = sem("small_in2")
        whi, wlo, scaled = sem("whi"), sem("wlo"), sem("scaled")
        dve_seen, pe_seen = sem("dve_seen"), sem("pe_seen")
        ob_made, ohi_made, olo_made, pool_seen = sem("ob_made"), sem("ohi_made"), sem("olo_made"), sem("pool_seen")
        wo_done, x1_made, z2_made, x1b_made, z2T_done, z2hi_made, z2lo_made = (
            sem(n) for n in ("wo_done", "x1_made", "z2_made", "x1b_made", "z2T_done", "z2hi_made", "z2lo_made"))
        qkv_done, qk_out, v_out, sq_made, qkn_made, qkw_made, qkT_done, qT_out, kT_out = (
            sem(n) for n in ("qkv_done", "qk_out", "v_out2", "sq_made", "qkn_made", "qkw_made", "qkT_done", "qT_out", "kT_out"))
        s_done, shifted, e_made, eT_made, pv_done, o2hi_made, o2lo_made = (
            sem(n) for n in ("s_done2", "shifted", "e_made", "eT_made", "pv_done2", "o2hi_made", "o2lo_made"))
        proj_done, x2_made, z3_made, z3T_done, z3T_out, step = (
            sem(n) for n in ("proj_done", "x2_made", "z3_made", "z3T_done", "z3T_out", "step2"))

        def steps(eng, body):
            for it in range(3):
                body(it)
            with eng.Fori(3, NT) as i:
                body(i)
            for it in range(NT, NT + 3):
                body(it)

        def has(it, lag):
            return not isinstance(it, int) or 0 <= it - lag < NT

        block = ctx.enter_context(nc.Block())

        @block.sync
        def _(eng):
            for name, dst in (("bv", bv[:, :]), ("bo", bo[:, :]), ("bqkv", bqkv[:, :, :].rearrange("p a n -> p (a n)")),
                              ("bproj", bproj[:, :]), ("qn", qk_w[:, 0, :]), ("kn", qk_w[:, 1, :])):
                eng.dma_start(dst, io[name] if name == "bv" else row_on_all(io[name])).then_inc(small_in, 16)
            for i in range(2, 5):
                eng.wait_ge(wlo, i - 1)
                eng.dma_start(raw[:, i % 2, :], io["w5"][i]).then_inc(w_in[i % 2], 16)

        @block.gpsimd
        def _(eng):
            eng.wait_ge(small_in, 6 * 16)

            def body(it):
                if has(it, 0):
                    cols = bass.ds(it * P, P)
                    need(eng, olo_made, it)
                    eng.tensor_tensor(o_b[:, :, :], O_T[:, :, cols], bv[:, :].unsqueeze(2).broadcast_to([P, CT, P]),
                                      ALU.add).then_inc(ob_made, 1)
                    eng.wait_ge(ob_made, it + 1)
                    need(eng, wo_done, it)
                    eng.sem_inc(pool_seen, 1)
                    eng.tensor_copy(o_hi[:, :, :], o_b[:, :, :]).then_inc(ohi_made, 1)
                    eng.wait_ge(ohi_made, it + 1)
                    eng.tensor_tensor(o_lo[:, :, :], o_b[:, :, :], o_hi[:, :, :].bitcast(F32), ALU.subtract).then_inc(olo_made, 1)
                if has(it, 1):
                    u = it - 1
                    eng.wait_ge(qkn_made, u + 1)
                    eng.tensor_tensor(qk[:, :, :].rearrange("p i (h d) -> p i h d", h=H),
                                      qk[:, :, :].rearrange("p i (h d) -> p i h d", h=H),
                                      qk_w[:, :, :].unsqueeze(2).broadcast_to([P, 2, H, HD]), ALU.mult).then_inc(qkw_made, 1)
                if has(it, 0):
                    eng.wait_ge(z2_made, it + 1)
                    eng.sem_inc(pool_seen, 1)
                    eng.tensor_tensor(x_nat[:, bass.ds(it, 1), :], x_nat[:, bass.ds(it, 1), :], bproj[:, :].unsqueeze(1),
                                      ALU.add).then_inc(x1b_made, 1)

            steps(eng, body)

        @block.tensor
        def _(eng):
            def project(out, hi, lo, i):
                for c in range(CT):
                    mm = three(eng, out, hi[:, c, :], lo[:, c, :], w_hi[i][:, c, :], w_lo[i][:, c, :], c == 0, c == CT - 1)
                return mm

            def body(it):
                if has(it, 2):
                    u = it - 2
                    eng.wait_ge(qkw_made, u + 1)
                    need(eng, z2lo_made, u + 2 if has(it, 1) else u + 1)
                    for i in range(2):
                        if i == 1:
                            need(eng, z3T_out, u - 1)
                        for g in range(CT):
                            mm = eng.transpose(pt[i][:, g * P:(g + 1) * P], qk[:, i, g * P:(g + 1) * P], ident[:, :])
                        mm.then_inc(qkT_done, 1)
                if has(it, 3):
                    u = it - 3
                    eng.wait_ge(o2lo_made, u + 1)
                    if isinstance(it, int) and it == 3:
                        eng.wait_ge(wlo, 5)
                    if has(it, 2):
                        eng.wait_ge(qk_out, 2 * (u + 2))
                    else:
                        eng.wait_ge(x2_made, u)
                    project(pw[0][:, :], o2_hi, o2_lo, 4).then_inc(proj_done, 1)
                if has(it, 0):
                    if isinstance(it, int):
                        eng.wait_ge(wlo, 1 + 4 * (it == 2))
                    eng.wait_ge(olo_made, it + 1)
                    need(eng, x2_made, it - 2)
                    if has(it, 2):
                        eng.wait_ge(qk_out, 2 * (it - 1))
                    else:
                        need(eng, x1_made, it)
                    project(pw[0][:, :], o_hi, o_lo, 0).then_inc(wo_done, 1)
                if has(it, 2):
                    u = it - 2
                    eng.wait_ge(qT_out, u + 1)
                    eng.wait_ge(kT_out, u + 1)
                    need(eng, o2lo_made, u)
                    eng.sem_inc(pe_seen, 1)
                    for g in range(CT):
                        for b in range(4):
                            for r in range(4):
                                rows, cols = slice(r * HD, (r + 1) * HD), slice(b * S, (b + 1) * S)
                                mm = eng.matmul(pa[cols, r, g * S:(g + 1) * S], q_T[rows, g, cols], k_T[rows, g, cols],
                                                start=True, stop=True)
                    mm.then_inc(s_done, 1)
                if has(it, 1):
                    u = it - 1
                    eng.wait_ge(z2lo_made, u + 1)
                    for i in range(3):
                        if isinstance(it, int) and it == 1:
                            eng.wait_ge(wlo, i + 2)
                        if i == 0:
                            need(eng, v_out, u)
                        elif i == 1:
                            if has(it, 0):
                                eng.wait_ge(x1_made, it + 1)
                            else:
                                eng.wait_ge(x2_made, it - 2)
                        else:
                            eng.wait_ge(qk_out, 2 * u + 1)
                        project(pw[(i + 1) % 2][:, :], z2_hi, z2_lo, i + 1).then_inc(qkv_done, 1)
                if has(it, 2):
                    u = it - 2
                    eng.wait_ge(eT_made, u + 1)
                    eng.sem_inc(pe_seen, 1)
                    for g in range(CT):
                        for r in range(4):
                            for b in range(4):
                                keys, ds = slice(b * S, (b + 1) * S), slice(r * HD, (r + 1) * HD)
                                h = 4 * g + r
                                mm = eng.matmul(pa[ds, b, g * S:(g + 1) * S], v[keys, h * HD:(h + 1) * HD],
                                                e_T[keys, (r * CT + g) * S:(r * CT + g + 1) * S], start=True, stop=True)
                    mm.then_inc(pv_done, 1)
                if has(it, 0):
                    eng.wait_ge(z2_made, it + 1)
                    need(eng, qT_out, it - 1)
                    if not has(it, 2):
                        need(eng, z2lo_made, it)
                    for c in range(CT):
                        mm = eng.transpose(pt[0][:, c * P:(c + 1) * P], z2[:, c * P:(c + 1) * P], ident[:, :])
                    mm.then_inc(z2T_done, 1)
                if has(it, 3):
                    u = it - 3
                    eng.wait_ge(z3_made, u + 1)
                    if has(it, 2):
                        eng.wait_ge(kT_out, u + 2)
                    else:
                        eng.wait_ge(z3T_out, u)
                    for c in range(CT):
                        mm = eng.transpose(pt[1][:, c * P:(c + 1) * P], z3s[:, c * P:(c + 1) * P], ident[:, :])
                    mm.then_inc(z3T_done, 1)

            steps(eng, body)

        @block.scalar
        def _(eng):
            for i in range(5):
                eng.wait_ge(w_in[i % 2], 16 * (i // 2 + 1))
                eng.activation(w_hi[i][:, :, :], raw[:, i % 2, :].rearrange("p (c n) -> p c n", c=CT), ACT.Copy).then_inc(whi, 1)

            def body(it):
                if has(it, 2):
                    u = it - 2
                    eng.wait_ge(qkT_done, 2 * u + 1)
                    need(eng, s_done, u)
                    eng.activation(q_T[:, :, :].rearrange("p g t -> p (g t)"), pt[0][:, :], ACT.Copy).then_inc(qT_out, 1)
                    eng.wait_ge(qkT_done, 2 * u + 2)
                    eng.activation(k_T[:, :, :].rearrange("p g t -> p (g t)"), pt[1][:, :], ACT.Copy).then_inc(kT_out, 1)
                    eng.wait_ge(shifted, u + 1)
                    eng.activation(e[:, :], e[:, :], ACT.Exp).then_inc(e_made, 1)
                if has(it, 1):
                    u = it - 1
                    eng.wait_ge(qk_out, 2 * u + 2)
                    eng.activation(sq[:, :], qk[:, :, :].rearrange("p i n -> p (i n)"), ACT.Square).then_inc(sq_made, 1)
                if has(it, 2):
                    u = it - 2
                    eng.wait_ge(pv_done, u + 1)
                    need(eng, proj_done, u)
                    eng.activation(o2_hi[:, :, :].rearrange("p g (b s) -> p b g s", b=4),
                                   pa[:, :, 0:P].rearrange("p b (g s) -> p b g s", g=CT), ACT.Copy).then_inc(o2hi_made, 1)
                if has(it, 0):
                    eng.wait_ge(z2T_done, it + 1)
                    need(eng, qkv_done, 3 * it)
                    eng.activation(z2_hi[:, :, :].rearrange("p c t -> p (c t)"), pt[0][:, :], ACT.Copy).then_inc(z2hi_made, 1)
                if has(it, 3):
                    u = it - 3
                    eng.wait_ge(z3T_done, u + 1)
                    eng.activation(O_T[:, :, bass.ds(u * P, P)], pt[1][:, :].rearrange("p (c t) -> p c t", c=CT),
                                   ACT.Copy).then_inc(z3T_out, 1)

            steps(eng, body)

        @block.vector
        def _(eng):
            eng.wait_ge(small_in, 6 * 16)
            eng.tensor_scalar(qk_w[:, 0, :], qk_w[:, 0, :], SCALE, None, ALU.mult).then_inc(scaled, 1)
            for i in range(5):
                eng.wait_ge(whi, i + 1)
                eng.tensor_tensor(w_lo[i][:, :, :], raw[:, i % 2, :].rearrange("p (c n) -> p c n", c=CT),
                                  w_hi[i][:, :, :].bitcast(F32), ALU.subtract).then_inc(wlo, 1)
            count = {"at": 0}

            def body(it):
                whole = not isinstance(it, int)
                ch = Chain(eng, step, count["at"] if not whole else count["at"] + (it - 3) * PER_STEP)
                if has(it, 3):
                    u = it - 3
                    x_u = x_nat[:, bass.ds(u, 1), :]
                    eng.wait_ge(proj_done, u + 1)
                    eng.wait_ge(x1b_made, u + 1)
                    ins = eng.tensor_tensor(x_u, pw[0][:, :].unsqueeze(1), x_u, ALU.add)
                    ins.then_inc(x2_made, 1)
                    eng.wait_ge(x2_made, u + 1)
                    need(eng, z3T_done, u)
                    layer_norm(eng, ch, stats, mv, rstd, tmp, x_u, z3s[:, :].unsqueeze(1),
                               dve_seen).then_inc(z3_made, 1)
                    eng.wait_ge(z3_made, u + 1)
                    ch.link(eng.tensor_copy(ln3[:, bass.ds(u, 1), 0], mv[:, 0:1]))
                    ch.link(eng.tensor_copy(ln3[:, bass.ds(u, 1), 1], rstd[:, :]))
                if has(it, 0):
                    x_t = x_nat[:, bass.ds(it, 1), :]
                    ch.link(eng.tensor_tensor(x_t, x_t, bo[:, :].unsqueeze(1), ALU.add))
                    eng.wait_ge(wo_done, it + 1)
                    eng.tensor_tensor(x_t, pw[0][:, :].unsqueeze(1), x_t, ALU.add).then_inc(x1_made, 1)
                    eng.wait_ge(x1_made, it + 1)
                    need(eng, z2T_done, it)
                    layer_norm(eng, ch, stats, mv, rstd, tmp, x_t, z2[:, :].unsqueeze(1),
                               dve_seen).then_inc(z2_made, 1)
                if has(it, 2):
                    u = it - 2
                    s_p = pa[:, :, 0:P].rearrange("p r (g k) -> p r g k", g=CT)
                    e4 = e[:, :].rearrange("p (r g k) -> p r g k", r=4, g=CT)
                    eng.wait_ge(s_done, u + 1)
                    ch.link(eng.tensor_reduce(mx[:, :], s_p, AX.X, ALU.max))
                    m4 = mx[:, :].rearrange("p (r g) -> p r g", r=4).unsqueeze(3).broadcast_to([P, 4, CT, S])
                    eng.tensor_tensor(e4, s_p, m4, ALU.subtract).then_inc(shifted, 1)
                if has(it, 1):
                    eng.wait_ge(qkv_done, 3 * (it - 1) + 1)
                    need(eng, qkT_done, 2 * (it - 1))
                    eng.tensor_tensor(qk[:, 0, :], pw[1][:, :], bqkv[:, 0, :], ALU.add).then_inc(qk_out, 1)
                if has(it, 2):
                    u = it - 2
                    eng.wait_ge(e_made, u + 1)
                    e3 = e[:, :].rearrange("p (h k) -> p h k", k=S)
                    ch.link(eng.tensor_reduce(sm[:, :], e3, AX.X, ALU.add))
                    ch.link(eng.reciprocal(rs[:, :], sm[:, :]))
                    ch.link(eng.tensor_tensor(e3, e3, rs[:, :].unsqueeze(2).broadcast_to([P, H, S]), ALU.mult))
                    need(eng, pv_done, u)
                    eng.transpose(e_T[:, :], e[:, :]).then_inc(eT_made, 1)
                if has(it, 1):
                    u = it - 1
                    eng.wait_ge(qkv_done, 3 * u + 2)
                    eng.tensor_tensor(qk[:, 1, :], pw[0][:, :], bqkv[:, 1, :], ALU.add).then_inc(qk_out, 1)
                    eng.wait_ge(sq_made, u + 1)
                    ch.link(eng.tensor_reduce(ms[:, :], sq[:, :].rearrange("p (h d) -> p h d", d=HD), AX.X, ALU.add))
                    ch.link(eng.tensor_scalar(ms[:, :], ms[:, :], 1.0 / HD, RMS_EPS, ALU.mult, ALU.add))
                    rsqrt(eng, ch, rms[:, :], ms[:, :], tmp32[:, :])
                    qk3 = qk[:, :, :].rearrange("p i (h d) -> p (i h) d", d=HD)
                    eng.tensor_tensor(qk3, qk3, rms[:, :].unsqueeze(2).broadcast_to([P, 2 * H, HD]),
                                      ALU.mult).then_inc(qkn_made, 1)
                if has(it, 2):
                    u = it - 2
                    eng.wait_ge(o2hi_made, u + 1)
                    eng.tensor_tensor(o2_lo[:, :, :].rearrange("p g (b s) -> p b g s", b=4),
                                      pa[:, :, 0:P].rearrange("p b (g s) -> p b g s", g=CT),
                                      o2_hi[:, :, :].rearrange("p g (b s) -> p b g s", b=4).bitcast(F32),
                                      ALU.subtract).then_inc(o2lo_made, 1)
                if has(it, 1):
                    eng.wait_ge(qkv_done, 3 * (it - 1) + 3)
                    need(eng, pv_done, it - 1)
                    eng.tensor_tensor(v[:, :], pw[1][:, :], bqkv[:, 2, :], ALU.add).then_inc(v_out, 1)
                if has(it, 0):
                    eng.wait_ge(z2hi_made, it + 1)
                    eng.tensor_tensor(z2_lo[:, :, :].rearrange("p c t -> p (c t)"), pt[0][:, :],
                                      z2_hi[:, :, :].rearrange("p c t -> p (c t)").bitcast(F32), ALU.subtract).then_inc(z2lo_made, 1)
                if whole:
                    assert ch.k == PER_STEP
                    count["at"] += (NT - 3) * PER_STEP
                else:
                    count["at"] += ch.k

            RSQRT = 2 + 3 * 4
            PER_STEP = (3 + RSQRT + 2) + (1 + 3 + RSQRT) + 1 + 3 + (2 + RSQRT)
            steps(eng, body)


def experts(nc, io, out, x_nat, ident, ln3, z_T, raw):
    HT = T // 2
    NH = NT // 2
    EC = 3
    with ExitStack() as ctx:
        def sb(name, shape, dt=F32):
            return ctx.enter_context(nc.sbuf_tensor(name, shape, dt))

        def ps(name, shape):
            return ctx.enter_context(nc.psum_tensor(name, shape, F32))

        def sem(name):
            return ctx.enter_context(nc.semaphore(name))

        BF = mybir.dt.bfloat16
        y = raw[:, :, EC * D:EC * D + D]
        g_raw = y[:, 0, :].rearrange("p (c n) -> p c n", c=CT)
        b2 = y[0:E, 1, :]
        w1_hi, w1_lo = sb("w1_hi", [P, EC, CT, EC * DM], F32R), sb("w1_lo", [P, EC, CT, EC * DM], F32R)
        w2_hi, w2_lo = sb("w2_hi", [P, E, D], F32R), sb("w2_lo", [P, E, D], F32R)
        g_hi, g_lo = sb("g_hi", [P, CT, DM], F32R), sb("g_lo", [P, CT, DM], F32R)
        wo2 = sb("wo2", [P, E])
        b1, bo1, bo2 = sb("b1", [P, E]), sb("bo1", [P, 1]), sb("bo2", [P, E])
        b2_hi, b2_lo = sb("b2_hi", [E, D], F32R), sb("b2_lo", [E, D], F32R)
        gamma, beta = sb("gamma", [P, D]), sb("beta", [P, D])
        mixw = sb("mixw", [P, 3, CT])
        xm = sb("xm", [P, CT, HT])
        xm_hi, xm_lo = sb("xm_hi", [P, CT, HT], F32R), sb("xm_lo", [P, CT, HT], F32R)
        th = xm[:, 2, :]
        rank = sb("rank", [P, E])
        gs, key, top = sb("gs", [P, NH, E]), sb("key", [P, NH, E]), sb("top", [P, NH])
        choice = sb("choice", [P, NH, E])
        choice_T, choice_b = sb("choice_T", [E, HT], F32R), sb("choice_b", [E, HT], BF)
        sel = sb("sel", [E, E, P], BF)
        chosen = sb("chosen", [P, 2, HT], BF)
        h = xm[:, 0:2, :]
        z = sb("z3n", [P, 2, D])
        h_hi, h_lo = sb("h_hi", [P, E, HT], F32R), sb("h_lo", [P, E, HT], F32R)
        stats, mv, rstd, tmp = sb("stats3", [P, 6]), sb("mv3", [P, 2]), sb("rstd3", [P, 1]), sb("tmp3", [P, 1])

        ph = [ps(f"ph{i}", [P, D]) for i in range(2)]
        pc = [ps(f"pc{i}", [P, D]) for i in range(2)]
        pg = ps("pg", [P, D])
        py = [ps(f"py{i}", [P, D]) for i in range(2)]

        small_in, w1_in, w2_in = sem("small_in3"), sem("w1_in"), sem("w2_in")
        (whi, wlo, mix_made, xmhi, xmlo, g_done, th_made, gs_done, choice_made, cT_done, cT_out, cb_out, consts, pc_done,
         pc_out, h_done, h_made, hhi, hlo, y_done, y_made, xb_made, zn_made, fin, step) = (
            sem("s3_" + n) for n in (
                "whi wlo mix_made xmhi xmlo g_done th_made gs_done choice_made cT_done cT_out cb_out consts pc_done "
                "pc_out h_done h_made hhi hlo y_done y_made xb_made zn_made fin step").split())
        dve_seen = sem("dve_seen3")
        stored = [sem(f"stored{p}") for p in range(2)]
        block = ctx.enter_context(nc.Block())

        def landing(i):
            return raw[:, i % 2, 0:CT * EC * DM]

        @block.sync
        def _(eng):
            eng.dma_start(y[:, 0, :], io["wo1"]).then_inc(small_in, 16)
            for name, dst in (("mixw", mixw[:, :, :].rearrange("p a c -> p (a c)")), ("wo2", wo2[:, :]), ("b1", b1[:, :]),
                              ("bo1", bo1[:, :]), ("b2", b2)):
                eng.dma_start(dst, io[name]).then_inc(small_in, 16)
            for name, dst in (("bo2", bo2[:, :]), ("gamma", gamma[:, :]), ("beta", beta[:, :])):
                eng.dma_start(dst, row_on_all(io[name])).then_inc(small_in, 16)
            for i in range(3):
                need(eng, wlo, i - 1 + 1 if i >= 2 else 0)
                eng.dma_start(landing(i), io["w1"][i]).then_inc(w1_in, 16)
                eng.wait_ge(w1_in, 16 * (i + 1))
            for i in range(3):
                eng.wait_ge(wlo, i + 3)
                eng.dma_start(landing(i + 3), io["w2"][i]).then_inc(w2_in, 16)
                eng.wait_ge(w2_in, 16 * (i + 1))
            for t in range(NT):
                eng.wait_ge(fin, t + 1)
                eng.dma_start(out[t], y[:, t % 2, :]).then_inc(stored[t % 2], 16)
            for p in range(2):
                eng.wait_ge(stored[p], 16 * NH)

        @block.gpsimd
        def _(eng):
            eng.wait_ge(small_in, 9 * 16)
            for t in range(NT):
                need(eng, y_made, t - 1)
                eng.tensor_scalar(z[:, t % 2, :], x_nat[:, t, :], ln3[:, t, 0:1], ln3[:, t, 1:2],
                                  ALU.subtract, ALU.mult).then_inc(zn_made, 1)
                eng.wait_ge(zn_made, t + 1)
                eng.tensor_tensor(x_nat[:, t, :], x_nat[:, t, :], beta[:, :], ALU.add).then_inc(xb_made, 1)

        @block.tensor
        def _(eng):
            for hf in range(2):
                eng.wait_ge(wlo, 1)
                eng.wait_ge(xmlo, hf + 1)
                for c in range(CT):
                    mm = three(eng, pg[:, :], g_hi[:, c, :], g_lo[:, c, :], xm_hi[:, c, :], xm_lo[:, c, :], c == 0, c == CT - 1)
                mm.then_inc(g_done, 1)

                def hidden(e):
                    k = E * hf + e
                    if hf == 0 and e % EC == 0:
                        eng.wait_ge(wlo, 2 + e // EC)
                    need(eng, h_made, k - 1)
                    for c in range(CT):
                        cols = slice(e % EC * DM, (e % EC + 1) * DM)
                        mm = three(eng, ph[k % 2][:, :], w1_hi[:, e // EC, c, cols], w1_lo[:, e // EC, c, cols],
                                   xm_hi[:, c, :], xm_lo[:, c, :], c == 0, c == CT - 1)
                    mm.then_inc(h_done, 1)

                def spread(e):
                    k = E * hf + e
                    eng.wait_ge(cb_out, hf + 1)
                    need(eng, pc_out, k - 1)
                    eng.matmul(pc[k % 2][:, :], sel[:, e, :], choice_b[:, :], start=True, stop=True).then_inc(pc_done, 1)

                hidden(0)
                eng.wait_ge(th_made, hf + 1)
                for t in range(NH):
                    mm = eng.matmul(pg[:, t * E:(t + 1) * E], th[:, t * P:(t + 1) * P], wo2[:, :], start=True, stop=True)
                mm.then_inc(gs_done, 1)
                hidden(1)
                eng.wait_ge(choice_made, hf + 1)
                for t in range(NH):
                    mm = eng.transpose(pg[0:E, t * P:(t + 1) * P], choice[:, t, :], ident[:, :])
                mm.then_inc(cT_done, 1)
                spread(0)
                spread(1)
                for e in range(2, E):
                    hidden(e)
                    spread(e)
                for t in range(NH):
                    k = NH * hf + t
                    need(eng, y_made, k - 1)
                    cols = slice(t * P, (t + 1) * P)
                    eng.wait_ge(cT_out, hf + 1)
                    eng.matmul(py[k % 2][:, :], choice_T[:, cols], b2_hi[:, :], start=True, stop=False)
                    eng.matmul(py[k % 2][:, :], choice_T[:, cols], b2_lo[:, :], start=False, stop=False)
                    for e in range(E):
                        if t == 0:
                            eng.wait_ge(hlo, E * hf + e + 1)
                            if hf == 0 and e % EC == 0:
                                eng.wait_ge(wlo, 5 + e // EC)
                        mm = three(eng, py[k % 2][:, :], h_hi[:, e, cols], h_lo[:, e, cols], w2_hi[:, e, :], w2_lo[:, e, :],
                                   False, e == E - 1)
                    mm.then_inc(y_done, 1)

        def w_parts(i, w1, w2):
            if i <= 3:
                return w1[:, i - 1, :, :].rearrange("p c n -> p (c n)")
            return w2[:, (i - 4) * EC:(i - 3) * EC, :].rearrange("p e n -> p (e n)")

        def w_size(i):
            return CT * EC * DM if i <= 3 else EC * D

        @block.scalar
        def _(eng):
            def w_split(i):
                if i <= 3:
                    eng.wait_ge(w1_in, 16 * i)
                else:
                    eng.wait_ge(w2_in, 16 * (i - 3))
                eng.activation(w_parts(i, w1_hi, w2_hi), raw[:, (i - 1) % 2, 0:w_size(i)], ACT.Copy).then_inc(whi, 1)

            eng.wait_ge(small_in, 9 * 16)
            eng.activation(g_hi[:, :, :], g_raw, ACT.Copy).then_inc(whi, 1)
            for hf in range(2):
                eng.wait_ge(mix_made, 12 * (hf + 1))
                if hf:
                    eng.wait_ge(h_done, E * hf)
                eng.activation(xm_hi[:, :, :], xm[:, :, :], ACT.Copy).then_inc(xmhi, 1)
                if hf == 0:
                    w_split(1)
                    w_split(2)
                eng.wait_ge(g_done, hf + 1)
                eng.activation(th, pg[:, :], ACT.Tanh, bias=bo1[:, 0:1]).then_inc(th_made, 1)
                if hf == 0:
                    w_split(3)
                    eng.wait_ge(consts, 2)
                    eng.activation(b2_hi[:, :], b2, ACT.Copy).then_inc(consts, 1)
                eng.wait_ge(cT_done, hf + 1)
                if hf:
                    eng.wait_ge(y_done, NH)
                eng.activation(choice_T[:, :], pg[0:E, :], ACT.Copy).then_inc(cT_out, 1)
                for e in range(E):
                    k = E * hf + e
                    eng.wait_ge(pc_done, k + 1)
                    need(eng, h_made, k - 1)
                    eng.activation(chosen[:, k % 2, :], pc[k % 2][:, :], ACT.Copy).then_inc(pc_out, 1)
                    eng.wait_ge(h_made, k + 1)
                    if hf:
                        eng.wait_ge(y_done, NH)
                    eng.activation(h_hi[:, e, :], h[:, k % 2, :], ACT.Copy).then_inc(hhi, 1)
                    if hf == 0 and e in (1, 3, 5):
                        w_split(4 + e // 2)

        @block.vector
        def _(eng):
            ch = Chain(eng, step)

            def w_split(i):
                eng.wait_ge(whi, i + 1)
                eng.tensor_tensor(w_parts(i, w1_lo, w2_lo), raw[:, (i - 1) % 2, 0:w_size(i)],
                                  w_parts(i, w1_hi, w2_hi).bitcast(F32), ALU.subtract).then_inc(wlo, 1)

            def mix(hf):
                cols = slice(hf * HT, (hf + 1) * HT)
                for c in range(CT):
                    eng.tensor_scalar(xm[:, c, :], z_T[:, c, cols], mixw[:, 1, c:c + 1], None, ALU.mult).then_inc(mix_made, 1)
                for a, (dst, src) in ((0, (slice(1, S), slice(0, S - 1))), (2, (slice(0, S - 1), slice(1, S)))):
                    for c in range(CT):
                        xc = xm[:, c, :].rearrange("p (b s) -> p b s", s=S)
                        zc = z_T[:, c, cols].rearrange("p (b s) -> p b s", s=S)
                        eng.wait_ge(mix_made, 12 * hf + 4 * (a // 2) + c + 1)
                        eng.scalar_tensor_tensor(out=xc[:, :, dst], in0=zc[:, :, src], scalar=mixw[:, a, c:c + 1],
                                                 in1=xc[:, :, dst], op0=ALU.mult, op1=ALU.add).then_inc(mix_made, 1)

            def xm_split(hf):
                eng.wait_ge(xmhi, hf + 1)
                eng.tensor_tensor(xm_lo[:, :, :], xm[:, :, :], xm_hi[:, :, :].bitcast(F32), ALU.subtract).then_inc(xmlo, 1)

            eng.wait_ge(small_in, 9 * 16)
            mix(0)
            eng.wait_ge(whi, 1)
            eng.tensor_tensor(g_lo[:, :, :], g_raw, g_hi[:, :, :].bitcast(F32), ALU.subtract).then_inc(wlo, 1)
            xm_split(0)
            w_split(1)
            for e in range(E):
                eng.memset(rank[:, e:e + 1], float(E - e))
            eng.tensor_copy(sel[:, :, :], ident[0:E, 0:E].unsqueeze(2).broadcast_to([E, E, P])).then_inc(consts, 2)
            w_split(2)
            for hf in range(2):
                eng.wait_ge(gs_done, hf + 1)
                bc = [P, NH, E]
                ch.link(eng.tensor_tensor(gs[:, :, :], pg[:, 0:NH * E].rearrange("p (t e) -> p t e", t=NH),
                                          bo2[:, :].unsqueeze(1).broadcast_to(bc), ALU.add))
                ch.link(eng.tensor_reduce(top[:, :], gs[:, :, :], AX.X, ALU.max))
                ch.link(eng.tensor_tensor(key[:, :, :], gs[:, :, :], top[:, :].unsqueeze(2).broadcast_to(bc), ALU.is_equal))
                ch.link(eng.tensor_tensor(key[:, :, :], key[:, :, :], rank[:, :].unsqueeze(1).broadcast_to(bc), ALU.mult))
                ch.link(eng.tensor_reduce(top[:, :], key[:, :, :], AX.X, ALU.max))
                eng.tensor_tensor(choice[:, :, :], key[:, :, :], top[:, :].unsqueeze(2).broadcast_to(bc),
                                  ALU.is_equal).then_inc(choice_made, 1)
                eng.wait_ge(cT_out, hf + 1)
                eng.tensor_copy(choice_b[:, :], choice_T[:, :].bitcast(F32)).then_inc(cb_out, 1)
                if hf == 0:
                    w_split(3)
                    eng.wait_ge(consts, 3)
                    eng.tensor_tensor(b2_lo[:, :], b2, b2_hi[:, :].bitcast(F32), ALU.subtract).then_inc(consts, 1)
                for e in range(E):
                    k = E * hf + e
                    eng.wait_ge(pc_out, k + 1)
                    eng.wait_ge(h_done, k + 1)
                    need(eng, hlo, k - 1)
                    eng.scalar_tensor_tensor(out=h[:, k % 2, :], in0=ph[k % 2][:, :], scalar=b1[:, e:e + 1],
                                             in1=chosen[:, k % 2, :], op0=ALU.add, op1=ALU.mult).then_inc(h_made, 1)
                    eng.wait_ge(hhi, k + 1)
                    eng.tensor_tensor(h_lo[:, e, :], h[:, k % 2, :], h_hi[:, e, :].bitcast(F32), ALU.subtract).then_inc(hlo, 1)
                    if hf == 0 and e in (1, 3, 5):
                        w_split(4 + e // 2)
                if hf == 0:
                    eng.wait_ge(hlo, E)
                    mix(1)
                for t in range(NH):
                    if hf == 0 and t == 1:
                        xm_split(1)
                    k = NH * hf + t
                    eng.wait_ge(y_done, k + 1)
                    need(eng, stored[k % 2], 16 * (k // 2))
                    y_t = y[:, k % 2, :]
                    eng.wait_ge(zn_made, k + 1)
                    eng.tensor_tensor(y_t, py[k % 2][:, :], z[:, k % 2, :], ALU.add).then_inc(y_made, 1)
                    eng.wait_ge(y_made, k + 1)
                    ch.link(layer_norm(eng, ch, stats, mv, rstd, tmp, y_t, y_t, dve_seen))
                    ch.link(eng.tensor_tensor(y_t, y_t, gamma[:, :], ALU.mult))
                    eng.wait_ge(xb_made, k + 1)
                    eng.tensor_tensor(y_t, y_t, x_nat[:, k, :], ALU.add).then_inc(fin, 1)


def kernel(**inputs):
    import concourse.bacc as bacc
    from concourse.bass_utils import run_bass_kernel_spmd

    nc = bacc.Bacc("TRN2", target_bir_lowering=False, num_devices=1)
    a = {k: np.asarray(v) for k, v in inputs.items()}

    def rows(w):
        return w.reshape(-1, P, w.shape[1]).transpose(1, 0, 2).reshape(P, -1)

    def cols(b):
        return b.reshape(-1, P).T

    ctx = a["ctx_1024"]
    laid = {
        "x": a["x"].reshape(NT, P, D).transpose(1, 0, 2),
        "ctx": ctx[:, :SM].reshape(NPAIR, 2 * SM, CT, P).transpose(0, 3, 2, 1).reshape(NPAIR, P, CT * 2 * SM),
        "tail": ctx[:, SM].reshape(B, CT, P).transpose(2, 1, 0),
        "mask": a["mask_1x1xSxS2_ff0"].reshape(S, SK),
        "wq": rows(a["L0_xattn_Wq"].T), "wk": rows(a["L0_xattn_Wk"].T), "wv": rows(a["L0_xattn_Wv"].T),
        "w5": np.stack([rows(w) for w in [a["L0_xattn_Wo"].T, *np.split(a["L0_attn_Wqkv"].T, 3, axis=1), a["L0_attn_Wproj"].T]]),
        "bo": a["L0_xattn_bo"], "bqkv": a["L0_attn_bqkv"], "bproj": a["L0_attn_bproj"],
        "qn": a["L0_attn_qn_w"], "kn": a["L0_attn_kn_w"],
        "w1": np.stack([rows(w.transpose(1, 0, 2).reshape(D, -1)) for w in np.split(a["L0_ffn_W1"], 3)]),
        "w2": np.stack([w.transpose(1, 0, 2).reshape(DM, -1) for w in np.split(a["L0_ffn_W2"], 3)]),
        "wo1": rows(a["L0_ffn_Wo1"]), "wo2": a["L0_ffn_Wo2"],
        "b1": a["L0_ffn_b1"].T, "bo1": a["L0_ffn_bo1"].reshape(DM, 1), "b2": a["L0_ffn_b2"], "bo2": a["L0_ffn_bo2"],
        "mixw": a["L0_ffn_mix_kernel"].reshape(3, CT, P).transpose(2, 0, 1).reshape(P, 3 * CT),
        "gamma": a["L0_ffn_gamma"], "beta": a["L0_ffn_beta"],
        "bq": cols(a["L0_xattn_bq"]), "bk": cols(a["L0_xattn_bk"]), "bv": cols(a["L0_xattn_bv"]),
    }
    laid = {k: np.ascontiguousarray(v) for k, v in laid.items()}
    io = {k: nc.dram_tensor(k + "_dram", v.shape, mybir.dt.from_np(v.dtype), kind="ExternalInput").ap() for k, v in laid.items()}
    out = nc.dram_tensor("out_dram", (NT, P, D), F32, kind="ExternalOutput").ap()
    build(nc, io, out)
    r = run_bass_kernel_spmd(nc, [{k + "_dram": v for k, v in laid.items()}], core_ids=[0])
    return r.results[0]["out_dram"].reshape(B, S, D)
```

```python
import numpy as np
import concourse.bass as bass
from concourse import mybir
from contextlib import ExitStack

F32 = mybir.dt.float32
F32R = mybir.dt.float32r
I32 = mybir.dt.int32
ALU = mybir.AluOpType
ACT = mybir.ActivationFunctionType
AX = mybir.AxisListType

P = 128
D = 512
H, HD = 16, 32
B, S = 32, 32
T = B * S
NT = T // P
CT = D // P
SK = 257
SM = 256
NPAIR = B // 2
E = 9
DM = P
SCALE = 1.0 / float(np.sqrt(HD))
LN_EPS = 1e-5
RMS_EPS = 1e-6
BIG = 3.0e38


def need(eng, sem, value):
    if isinstance(value, (int, np.integer)) and value <= 0:
        return
    eng.wait_ge(sem, value)


class Chain:

    def __init__(self, eng, sem, start=0):
        self.eng, self.sem, self.start, self.k = eng, sem, start, 0

    def link(self, ins):
        self.k += 1
        ins.then_inc(self.sem, 1)
        self.eng.wait_ge(self.sem, self.start + self.k)


def rsqrt(eng, ch, y, v, t):
    ch.link(eng.tensor_scalar(t.bitcast(I32), v.bitcast(I32), 1, None, ALU.arith_shift_right))
    ch.link(eng.tensor_scalar(y.bitcast(I32), t.bitcast(I32), -1.0, 1597463007.0, ALU.mult, ALU.add))
    for _ in range(3):
        ch.link(eng.scalar_tensor_tensor(out=t, in0=y, scalar=-0.5, in1=y, op0=ALU.mult, op1=ALU.mult))
        ch.link(eng.tensor_tensor(t, t, v, ALU.mult))
        ch.link(eng.scalar_tensor_tensor(out=y, in0=t, scalar=1.5, in1=y, op0=ALU.add, op1=ALU.mult))


def build(nc, io, out):
    ctx = ExitStack()
    with ctx:
        def sb(name, shape, dt=F32, c=ctx):
            return c.enter_context(nc.sbuf_tensor(name, shape, dt))

        def sem(name, c=ctx):
            return c.enter_context(nc.semaphore(name))

        x_nat = sb("x_nat", [P, NT, D])
        ident = sb("ident", [P, P])
        ln3 = sb("ln3", [P, NT, 2])
        raw = sb("raw", [P, 2, CT * D])
        O_T = sb("O_T", [P, CT, T])
        w_in = [sem(f"w_in{i}") for i in range(2)]
        cross_attention(nc, io, x_nat, ident, O_T, raw, w_in)
        self_attention(nc, io, x_nat, ident, O_T, raw, w_in, ln3)
        experts(nc, io, out, x_nat, ident, ln3, O_T, raw)


def three(eng, out, a_hi, a_lo, b_hi, b_lo, first, last):
    eng.matmul(out, a_hi, b_hi, start=first, stop=False)
    eng.matmul(out, a_lo, b_hi, start=False, stop=False)
    return eng.matmul(out, a_hi, b_lo, start=False, stop=last)


def cross_attention(nc, io, x_nat, ident, O_T, raw, w_in):
    with ExitStack() as ctx:
        def sb(name, shape, dt=F32):
            return ctx.enter_context(nc.sbuf_tensor(name, shape, dt))

        def ps(name, shape):
            return ctx.enter_context(nc.psum_tensor(name, shape, F32))

        def sem(name):
            return ctx.enter_context(nc.semaphore(name))

        c_hi = [sb(f"c_hi{i}", [P, CT, D], F32R) for i in range(2)]
        c_lo = [sb(f"c_lo{i}", [P, CT, D], F32R) for i in range(2)]
        wk_hi, wk_lo = sb("wk_hi", [P, CT, D], F32R), sb("wk_lo", [P, CT, D], F32R)
        wv_hi, wv_lo = sb("wv_hi", [P, CT, D], F32R), sb("wv_lo", [P, CT, D], F32R)
        KW = SM + 2
        kf_hi, kf_lo = sb("kf_hi", [P, CT * 2 * KW], F32R), sb("kf_lo", [P, CT * 2 * KW], F32R)
        K_hi = kf_hi[:, :].rearrange("p (g j n) -> p g j n", g=CT, j=2)
        K_lo = kf_lo[:, :].rearrange("p (g j n) -> p g j n", g=CT, j=2)
        wq_hi = kf_hi[:, 0:CT * D].rearrange("p (c n) -> p c n", c=CT)
        wq_lo = kf_lo[:, 0:CT * D].rearrange("p (c n) -> p c n", c=CT)
        V = sb("V", [P, 4, D])
        m_flat, p_flat = sb("m_flat", [P, 2 * CT * SK]), sb("p_flat", [P, 2 * CT * SK])
        masked = m_flat[:, :].rearrange("p (j g n) -> p j g n", j=2, g=CT)
        probs = p_flat[:, :].rearrange("p (j g n) -> p j g n", j=2, g=CT)
        wv_raw = m_flat[:, 0:CT * D].rearrange("p (c n) -> p c n", c=CT)
        ctx0_raw = p_flat[:, 0:CT * D].rearrange("p (c n) -> p c n", c=CT)
        P_T = sb("P_T", [P, 2, 2, D])
        Qd_hi = [sb(f"Qd_hi{j}", [P, CT, P], F32R) for j in range(2)]
        Qd_lo = [sb(f"Qd_lo{j}", [P, CT, P], F32R) for j in range(2)]
        Q_T = sb("Q_T", [P, CT, T])
        mask = sb("mask", [P, SK])
        bq, bk = sb("bq", [P, CT]), sb("bk", [P, CT])
        tail = sb("tail", [P, CT, B])
        t_hi, t_lo = sb("t_hi", [P, CT, B], F32R), sb("t_lo", [P, CT, B], F32R)
        tail_nat = sb("tail_nat", [B, 2, D])
        kt32 = sb("kt32", [P, CT, B])
        kt_hi, kt_lo = sb("kt_hi", [P, CT, B], F32R), sb("kt_lo", [P, CT, B], F32R)
        vt = sb("vt", [P, CT, B])
        same_head = sb("same_head", [P, P])
        same_q = sb("same_q", [P, S])
        q_b_hi, q_b_lo = sb("q_b_hi", [P, CT, S], F32R), sb("q_b_lo", [P, CT, S])
        stats, mv = sb("stats", [P, NT, 6]), sb("mv", [P, NT, 2])
        var, rstd, tmp8 = sb("var", [P, NT]), sb("rstd", [P, NT]), sb("tmp8", [P, NT])
        z = sb("z", [P, 2, D])
        nmax, psum_, rinv = sb("nmax", [P, 2, CT]), sb("psum_", [P, 2, CT]), sb("rinv", [P, 2, CT])
        dtail = sb("dtail", [P, CT, S])
        otail = sb("otail", [P, 2, CT, S])

        pj = [ps(f"pj{i}", [P, D]) for i in range(2)]
        sc = [ps(f"sc{i}", [P, D]) for i in range(2)]
        tp = ps("tp", [P, 2, D])
        sc = sc + [tp[:, 0, :], tp[:, 1, :]]
        po = ps("po", [P, D])
        pb = ps("pb", [P, D])

        x_in = [sem(f"x_in{i}") for i in range(2)]
        wq_in, wv_in, wk_in, bias_in, small_in = (sem(n) for n in ("wq_in", "wv_in", "wk_in", "bias_in", "small_in"))
        ctx_in = [sem(f"ctx_in{i}") for i in range(2)]
        const_made, z_made, zT_done, zT_hi, zT_lo = (sem(n) for n in ("const_made", "z_made", "zT_done", "zT_hi", "zT_lo"))
        w_hi, w_lo, q_done, q_out = (sem(n) for n in ("w_hi", "w_lo", "q_done", "q_out"))
        tail_done, tail_out, tailT_done, tailT_out = (sem(n) for n in ("tail_done", "tail_out", "tailT_done", "tailT_out"))
        bias_made, dve_step = sem("bias_made"), sem("dve_step")
        ctx_hi, ctx_lo, kv_done, k_hi, k_lo, v_out = (sem(n) for n in ("ctx_hi", "ctx_lo", "kv_done", "k_hi", "k_lo", "v_out"))
        k_tail, q_hi, q_lo, qd_made = (sem(n) for n in ("k_tail", "q_hi", "q_lo", "qd_made"))
        ident_made, heads_made = sem("ident_made"), sem("heads_made")
        s_done, masked_made, exp_done, rinv_made, probs_made = (sem(n) for n in ("s_done", "masked_made", "exp_done", "rinv_made", "probs_made"))
        dt_made, pb_done, ot_made, tr_done, pt_act, pt_dve, pv_done, o_out = (
            sem(n) for n in ("dt_made", "pb_done", "ot_made", "tr_done", "pt_act", "pt_dve", "pv_done", "o_out"))

        s_seen, q_hi_seen = sem("s_seen"), sem("q_hi_seen")

        block = ctx.enter_context(nc.Block())

        @block.sync
        def _(eng):
            eng.dma_start(x_nat[:, 0:4, :], io["x"][:, 0:4, :]).then_inc(x_in[0], 16)
            eng.dma_start(raw[:, 0, :], io["wq"]).then_inc(wq_in, 16)
            eng.dma_start(x_nat[:, 4:NT, :], io["x"][:, 4:NT, :]).then_inc(x_in[1], 16)
            eng.dma_start(bq[:, :], io["bq"]).then_inc(bias_in, 16)
            eng.dma_start(bk[:, :], io["bk"]).then_inc(bias_in, 16)
            eng.dma_start(raw[:, 1, :], io["wk"]).then_inc(wk_in, 16)
            eng.dma_start(p_flat[:, 0:CT * D], io["ctx"][0]).then_inc(ctx_in[0], 16)
            eng.dma_start(m_flat[:, 0:CT * D], io["wv"]).then_inc(wv_in, 16)
            eng.dma_start(tail[:, :, :], io["tail"]).then_inc(small_in, 16)
            for h in range(4):
                eng.dma_start(mask[h * S:(h + 1) * S, :], io["mask"]).then_inc(small_in, 16)
            eng.wait_ge(w_lo, 2)
            eng.dma_start(raw[:, 1, :], io["ctx"][1]).then_inc(ctx_in[1], 16)
            with eng.Fori(1, NT) as i:
                for p in range(2):
                    n = 2 * i + p
                    eng.wait_ge(ctx_lo, n - 1)
                    eng.dma_start(raw[:, p, :], io["ctx"][n]).then_inc(ctx_in[p], 16)
            for p in range(2):
                eng.wait_ge(ctx_lo, NPAIR - 1 + p)
                eng.dma_start(raw[:, p, :], io["w5"][p]).then_inc(w_in[p], 16)

        @block.gpsimd
        def _(eng):
            eng.memset(ident[:, :], 0.0).then_inc(const_made, 1)
            eng.wait_ge(const_made, 1)
            eng.affine_select(out=ident[:, :], in_=ident[:, :], compare_op=ALU.not_equal, fill=1.0,
                              base=0, pattern=[[-1, P]], channel_multiplier=1).then_inc(ident_made, 1)
            eng.wait_ge(heads_made, 9)
            eng.wait_ge(q_out, 8)

            def q_blocks(n, j):
                b = 2 * n + j
                cols = bass.ds(b * S, S)
                need(eng, qd_made, 2 * b)
                eng.tensor_copy(q_b_hi[:, :, :], Q_T[:, :, cols]).then_inc(q_hi, 1)
                eng.wait_ge(q_hi, b + 1)
                eng.sem_inc(q_hi_seen, 1)
                eng.tensor_tensor(q_b_lo[:, :, :], Q_T[:, :, cols], q_b_hi[:, :, :].bitcast(F32), ALU.subtract).then_inc(q_lo, 1)
                need(eng, s_done, 4 * (b - 1))
                eng.wait_ge(q_lo, b + 1)
                for Qd, q in ((Qd_hi, q_b_hi[:, :, :].bitcast(F32)), (Qd_lo, q_b_lo)):
                    eng.tensor_tensor(Qd[j][:, :, :].rearrange("p g (h s) -> p g h s", h=4),
                                      q[:, :, :].unsqueeze(2).broadcast_to([P, CT, 4, S]),
                                      same_head[:, :].rearrange("p (h s) -> p h s", h=4).unsqueeze(1).broadcast_to([P, CT, 4, S]),
                                      ALU.mult).then_inc(qd_made, 1)

            def pair(n):
                need(eng, s_done, 8 * n)
                first = isinstance(n, int) and n == 0
                if first:
                    q_blocks(n, 0)
                    q_blocks(n, 1)
                    eng.wait_ge(tailT_out, 5)
                for j in range(2):
                    for K, kt in ((K_hi, kt_hi), (K_lo, kt_lo)):
                        eng.tensor_copy(K[:, :, j, SM:KW],
                                        kt[:, :, bass.ds(2 * n + j, 1)].broadcast_to([P, CT, 2])).then_inc(k_tail, 1)
                if not first:
                    q_blocks(n, 0)
                    q_blocks(n, 1)

            pair(0)
            pair(1)
            with eng.Fori(1, NT) as i:
                pair(2 * i)
                pair(2 * i + 1)

        @block.tensor
        def _(eng):
            def z_transposes(t):
                eng.wait_ge(z_made, t + 1)
                if t == 0:
                    eng.wait_ge(ident_made, 1)
                need(eng, zT_lo, t - 1)
                for c in range(CT):
                    mm = eng.transpose(tp[:, t % 2, c * P:(c + 1) * P], z[:, t % 2, c * P:(c + 1) * P], ident[:, :])
                mm.then_inc(zT_done, 1)

            def q_proj(hf, g):
                k = CT * hf + g
                if g == 0:
                    eng.wait_ge(zT_lo, 4 * (hf + 1))
                    eng.wait_ge(w_lo, 1)
                need(eng, q_out, k - 1)
                for c in range(CT):
                    mm = three(eng, pj[k % 2][:, :], wq_hi[:, c, g * P:(g + 1) * P], wq_lo[:, c, g * P:(g + 1) * P],
                               c_hi[hf][:, c, :], c_lo[hf][:, c, :], c == 0, c == CT - 1)
                mm.then_inc(q_done, 1)

            def tails():
                eng.wait_ge(w_lo, 4)
                for i, (hi, lo) in enumerate(((wk_hi, wk_lo), (wv_hi, wv_lo))):
                    for c in range(CT):
                        mm = three(eng, sc[i][0:B, :], t_hi[:, c, :], t_lo[:, c, :], hi[:, c, :], lo[:, c, :],
                                   c == 0, c == CT - 1)
                    mm.then_inc(tail_done, 1)

            def tail_transposes():
                for i in range(2):
                    eng.wait_ge(tail_out, i + 1)
                    for g in range(CT):
                        mm = eng.transpose(pb[:, (i * CT + g) * B:(i * CT + g + 1) * B],
                                           tail_nat[:, i, g * P:(g + 1) * P], ident[0:B, 0:B])
                mm.then_inc(tailT_done, 1)

            for t in range(4):
                z_transposes(t)
            q_proj(0, 0)
            q_proj(0, 1)
            z_transposes(4)
            z_transposes(5)
            q_proj(0, 2)
            z_transposes(6)
            z_transposes(7)
            q_proj(0, 3)
            for g in range(CT):
                q_proj(1, g)

            def k_tile(n, p, g):
                if g == 0:
                    eng.wait_ge(ctx_lo, n + 1)
                if g < 2:
                    need(eng, v_out, 4 * n - 1 + g)
                    if isinstance(n, int) and n == 0:
                        eng.wait_ge(q_out, 7 + g)
                        eng.wait_ge(w_lo, 2)
                else:
                    eng.wait_ge(k_lo, 4 * n + g - 1)
                for c in range(CT):
                    mm = three(eng, pj[g % 2][:, :], wk_hi[:, c, g * P:(g + 1) * P], wk_lo[:, c, g * P:(g + 1) * P],
                               c_hi[p][:, c, :], c_lo[p][:, c, :], c == 0, c == CT - 1)
                mm.then_inc(kv_done, 1)

            def v_tile(n, p, t):
                if isinstance(n, int) and n == 0 and t == 0:
                    eng.wait_ge(w_lo, 3)
                if t < 2:
                    eng.wait_ge(k_lo, 4 * n + 3 + t)
                else:
                    eng.wait_ge(v_out, 4 * n + t - 1)
                for c in range(CT):
                    mm = three(eng, pj[t % 2][:, :], c_hi[p][:, c, t * P:(t + 1) * P], c_lo[p][:, c, t * P:(t + 1) * P],
                               wv_hi[:, c, :], wv_lo[:, c, :], c == 0, c == CT - 1)
                mm.then_inc(kv_done, 1)

            def scores(n, j):
                eng.wait_ge(k_lo, 4 * n + 4)
                eng.wait_ge(k_tail, 4 * n + 2 * j + 2)
                eng.wait_ge(qd_made, 2 * (2 * n + j + 1))
                for g in range(CT):
                    need(eng, masked_made, 8 * n + 4 * (j - 1) + g + 1)
                    if g == 2 and j == 0:
                        need(eng, pt_act, 2 * n)
                        need(eng, pt_dve, 2 * n)
                    three(eng, sc[g][:, 0:KW], Qd_hi[j][:, g, :], Qd_lo[j][:, g, :],
                          K_hi[:, g, j, :], K_lo[:, g, j, :], True, True).then_inc(s_done, 1)

            def transposes(n, j):
                b = 2 * n + j
                eng.wait_ge(probs_made, 4 * (b + 1))
                eng.wait_ge(masked_made, 8 * (n + 1))
                need(eng, pt_act, b)
                need(eng, pt_dve, b)
                for k in range(2):
                    for g in range(CT):
                        mm = eng.transpose(tp[:, k, g * P:(g + 1) * P], probs[:, j, g, k * P:(k + 1) * P], ident[:, :])
                mm.then_inc(tr_done, 1)
                eng.wait_ge(dt_made, b + 1)
                need(eng, ot_made, b)
                eng.matmul(pb[:, 0:P], same_head[:, :], dtail[:, :, :].rearrange("p g s -> p (g s)"),
                           start=True, stop=True).then_inc(pb_done, 1)

            def weighted_sum(n, j):
                b = 2 * n + j
                eng.wait_ge(pt_act, b + 1)
                eng.wait_ge(pt_dve, b + 1)
                eng.wait_ge(v_out, 4 * (n + 1))
                need(eng, o_out, 4 * b)
                for g in range(CT):
                    for k in range(2):
                        mm = eng.matmul(po[:, g * P:(g + 1) * P], V[:, 2 * j + k, g * P:(g + 1) * P],
                                        P_T[:, j, k, g * P:(g + 1) * P], start=k == 0, stop=k == 1)
                mm.then_inc(pv_done, 1)

            def pair(n, p, first):
                k_tile(n, p, 0)
                if not first:
                    transposes(n - 1, 1)
                k_tile(n, p, 1)
                if not first:
                    weighted_sum(n - 1, 0)
                else:
                    tails()
                k_tile(n, p, 2)
                if not first:
                    weighted_sum(n - 1, 1)
                else:
                    tail_transposes()
                k_tile(n, p, 3)
                v_tile(n, p, 0)
                scores(n, 0)
                v_tile(n, p, 1)
                scores(n, 1)
                v_tile(n, p, 2)
                transposes(n, 0)
                v_tile(n, p, 3)

            pair(0, 0, True)
            pair(1, 1, False)
            with eng.Fori(1, NT) as i:
                pair(2 * i, 0, False)
                pair(2 * i + 1, 1, False)
            transposes(NPAIR - 1, 1)
            weighted_sum(NPAIR - 1, 0)
            weighted_sum(NPAIR - 1, 1)

        @block.scalar
        def _(eng):
            def split_hi(dst, src):
                return eng.activation(dst, src, ACT.Copy)

            eng.wait_ge(wq_in, 16)
            split_hi(wq_hi, raw[:, 0, :].rearrange("p (c n) -> p c n", c=CT)).then_inc(w_hi, 1)

            def z_hi(t):
                eng.wait_ge(zT_done, t + 1)
                split_hi(c_hi[t // 4][:, :, t % 4 * P:(t % 4 + 1) * P],
                         tp[:, t % 2, :].rearrange("p (c n) -> p c n", c=CT)).then_inc(zT_hi, 1)

            def q_evac(k):
                eng.wait_ge(q_done, k + 1)
                if k == 0:
                    eng.wait_ge(bias_made, 1)
                eng.activation(Q_T[:, k % CT, k // CT * D:(k // CT + 1) * D], pj[k % 2][:, :], ACT.Identity,
                               bias=bq[:, k % CT:k % CT + 1], scale=SCALE).then_inc(q_out, 1)

            def tail_evac():
                for i in range(2):
                    eng.wait_ge(tail_done, i + 1)
                    eng.activation(tail_nat[:, i, :], sc[i][0:B, :], ACT.Copy).then_inc(tail_out, 1)

            def tail_keys():
                eng.wait_ge(tailT_out, 1)
                split_hi(kt_hi[:, :, :], kt32[:, :, :]).then_inc(tailT_out, 1)

            def ctx_split(n, p, i):
                eng.wait_ge(ctx_in[p], 16 * (i + 1))
                need(eng, kv_done, 8 * (n - 1))
                if isinstance(n, int) and n < 2:
                    eng.wait_ge(q_done, 4 * (n + 1))
                src = ctx0_raw if isinstance(n, int) and n == 0 else raw[:, p, :].rearrange("p (c n) -> p c n", c=CT)
                split_hi(c_hi[p][:, :, :], src).then_inc(ctx_hi, 1)

            def k_evac(n, g):
                eng.wait_ge(kv_done, 8 * n + g + 1)
                if g == 0:
                    need(eng, s_done, 8 * n)
                eng.activation(K_hi[:, g, :, 0:SM], pj[g % 2][:, :].rearrange("p (j n) -> p j n", j=2),
                               ACT.Identity, bias=bk[:, g:g + 1]).then_inc(k_hi, 1)

            def v_evac(n, t):
                eng.wait_ge(kv_done, 8 * n + 5 + t)
                if t == 0:
                    need(eng, pv_done, 2 * n)
                eng.activation(V[:, t, :], pj[t % 2][:, :], ACT.Copy).then_inc(v_out, 1)

            def exps(n, j):
                b = 2 * n + j
                need(eng, tr_done, b - 1)
                need(eng, dt_made, b - 1)
                for g in range(CT):
                    eng.wait_ge(masked_made, 4 * b + g + 1)
                    eng.activation(probs[:, j, g, :], masked[:, j, g, :], ACT.Exp, bias=nmax[:, j, g:g + 1],
                                   scale=-1.0, accum_out=psum_[:, j, g:g + 1]).then_inc(exp_done, 1)

            def pt_evac(n, j):
                b = 2 * n + j
                eng.wait_ge(tr_done, b + 1)
                need(eng, pv_done, b - 1)
                eng.activation(P_T[:, j, 0, :], tp[:, 0, :], ACT.Copy).then_inc(pt_act, 1)

            def pair(n, p, i, first, last):
                k_evac(n, 0)
                if not first:
                    pt_evac(n - 1, 1)
                k_evac(n, 1)
                if first:
                    tail_evac()
                if not last:
                    ctx_split(n + 1, 1 - p, i + p)
                k_evac(n, 2)
                if first:
                    tail_keys()
                k_evac(n, 3)
                v_evac(n, 0)
                exps(n, 0)
                v_evac(n, 1)
                exps(n, 1)
                v_evac(n, 2)
                pt_evac(n, 0)
                v_evac(n, 3)

            for t in range(4):
                z_hi(t)
            eng.wait_ge(wk_in, 16)
            split_hi(wk_hi[:, :, :], raw[:, 1, :].rearrange("p (c n) -> p c n", c=CT)).then_inc(w_hi, 1)
            q_evac(0)
            q_evac(1)
            z_hi(4)
            z_hi(5)
            q_evac(2)
            z_hi(6)
            z_hi(7)
            q_evac(3)
            ctx_split(0, 0, 0)
            q_evac(4)
            eng.wait_ge(wv_in, 16)
            split_hi(wv_hi[:, :, :], wv_raw).then_inc(w_hi, 1)
            q_evac(5)
            eng.wait_ge(small_in, 5 * 16)
            split_hi(t_hi[:, :, :], tail[:, :, :]).then_inc(w_hi, 1)
            q_evac(6)
            q_evac(7)
            pair(0, 0, 0, True, False)
            pair(1, 1, 0, False, False)
            with eng.Fori(1, NT - 1) as i:
                pair(2 * i, 0, i, False, False)
                pair(2 * i + 1, 1, i, False, False)
            pair(NPAIR - 2, 0, NT - 1, False, False)
            pair(NPAIR - 1, 1, NT - 1, False, True)
            pt_evac(NPAIR - 1, 1)

        @block.vector
        def _(eng):
            ch = Chain(eng, dve_step)

            def split_lo(dst, src, hi):
                return eng.tensor_tensor(dst, src, hi.bitcast(F32), ALU.subtract)

            eng.memset(same_head[:, :], 0.0).then_inc(heads_made, 1)
            eng.wait_ge(heads_made, 1)
            eng.wait_ge(ident_made, 1)
            for h in range(4):
                r = slice(h * S, (h + 1) * S)
                eng.memset(same_head[r, r], 1.0).then_inc(heads_made, 1)
                eng.tensor_copy(same_q[r, :], ident[r, r]).then_inc(heads_made, 1)

            def layer_norm_stats(hf):
                eng.wait_ge(x_in[hf], 16)
                ts = slice(4 * hf, 4 * hf + 4)
                for t in range(4 * hf, 4 * hf + 4):
                    eng.bn_stats(stats[:, t, :], x_nat[:, t, :]).then_inc(dve_step, 1)
                    ch.k += 1
                first = ch.k - 4
                for t in range(4):
                    eng.wait_ge(dve_step, first + t + 1)
                    eng.bn_aggr(mv[:, 4 * hf + t, :], stats[:, 4 * hf + t, :]).then_inc(dve_step, 1)
                    ch.k += 1
                eng.wait_ge(dve_step, ch.k)
                ch.link(eng.tensor_scalar(var[:, ts], mv[:, ts, 1], LN_EPS, None, ALU.add))
                rsqrt(eng, ch, rstd[:, ts], var[:, ts], tmp8[:, ts])

            def z_make(t):
                need(eng, zT_done, t - 1)
                eng.tensor_scalar(z[:, t % 2, :], x_nat[:, t, :], mv[:, t, 0:1], rstd[:, t:t + 1],
                                  ALU.subtract, ALU.mult).then_inc(z_made, 1)

            def z_lo(t):
                eng.wait_ge(zT_hi, t + 1)
                cols = slice(t % 4 * P, (t % 4 + 1) * P)
                split_lo(c_lo[t // 4][:, :, cols], tp[:, t % 2, :].rearrange("p (c n) -> p c n", c=CT),
                         c_hi[t // 4][:, :, cols]).then_inc(zT_lo, 1)

            layer_norm_stats(0)
            z_make(0)
            z_make(1)
            eng.wait_ge(w_hi, 1)
            split_lo(wq_lo, raw[:, 0, :].rearrange("p (c n) -> p c n", c=CT), wq_hi).then_inc(w_lo, 1)
            for t in range(4):
                z_lo(t)
                if t < 2:
                    z_make(t + 2)
            eng.wait_ge(bias_in, 2 * 16)
            eng.tensor_scalar(bq[:, :], bq[:, :], SCALE, None, ALU.mult).then_inc(bias_made, 1)
            layer_norm_stats(1)
            z_make(4)
            z_make(5)
            for t in range(4, NT):
                z_lo(t)
                if t < 6:
                    z_make(t + 2)
            eng.wait_ge(w_hi, 2)
            split_lo(wk_lo[:, :, :], raw[:, 1, :].rearrange("p (c n) -> p c n", c=CT), wk_hi[:, :, :]).then_inc(w_lo, 1)

            def tail_keys():
                eng.wait_ge(tailT_done, 1)
                tails_T = pb[:, 0:2 * CT * B].rearrange("p (i g b) -> p i g b", i=2, g=CT)
                eng.tensor_tensor(kt32[:, :, :], tails_T[:, 0], bk[:, :].unsqueeze(2).broadcast_to([P, CT, B]),
                                  ALU.add).then_inc(tailT_out, 1)
                eng.wait_ge(tailT_out, 2)
                split_lo(kt_lo[:, :, :], kt32[:, :, :], kt_hi[:, :, :]).then_inc(tailT_out, 2)
                eng.tensor_copy(vt[:, :, :], tails_T[:, 1]).then_inc(tailT_out, 1)

            def ctx_split(n, p):
                eng.wait_ge(ctx_hi, n + 1)
                src = ctx0_raw if isinstance(n, int) and n == 0 else raw[:, p, :].rearrange("p (c n) -> p c n", c=CT)
                split_lo(c_lo[p][:, :, :], src, c_hi[p][:, :, :]).then_inc(ctx_lo, 1)

            def k_evac(n, g):
                eng.wait_ge(k_hi, 4 * n + g + 1)
                eng.scalar_tensor_tensor(out=K_lo[:, g, :, 0:SM], in0=pj[g % 2][:, :].rearrange("p (j n) -> p j n", j=2),
                                         scalar=bk[:, g:g + 1], in1=K_hi[:, g, :, 0:SM].bitcast(F32),
                                         op0=ALU.add, op1=ALU.subtract).then_inc(k_lo, 1)

            def mask_max(n, j):
                b = 2 * n + j
                need(eng, exp_done, 4 * (b - 1))
                for g in range(CT):
                    eng.wait_ge(s_done, 4 * b + g + 1)
                    eng.sem_inc(s_seen, 1)
                    eng.tensor_tensor_reduce(masked[:, j, g, :], sc[g][:, 0:SK], mask[:, :], -1.0, BIG,
                                             ALU.add, ALU.min, nmax[:, j, g:g + 1]).then_inc(masked_made, 1)

            def normalise(n, j):
                b = 2 * n + j
                eng.wait_ge(exp_done, 4 * (b + 1))
                eng.reciprocal(rinv[:, j, :], psum_[:, j, :]).then_inc(rinv_made, 1)
                eng.wait_ge(rinv_made, b + 1)
                for g in range(CT):
                    eng.tensor_scalar(probs[:, j, g, :], probs[:, j, g, :], rinv[:, j, g:g + 1], None,
                                      ALU.mult).then_inc(probs_made, 1)
                eng.wait_ge(probs_made, 4 * (b + 1))
                need(eng, pb_done, b)
                eng.tensor_tensor(dtail[:, :, :], same_q[:, :].unsqueeze(1).broadcast_to([P, CT, S]),
                                  probs[:, j, :, SM:SK].broadcast_to([P, CT, S]), ALU.mult).then_inc(dt_made, 1)

            def pt_evac(n, j):
                b = 2 * n + j
                eng.wait_ge(tr_done, b + 1)
                need(eng, pv_done, b - 1)
                eng.tensor_copy(P_T[:, j, 1, :], tp[:, 1, :]).then_inc(pt_dve, 1)
                eng.wait_ge(pb_done, b + 1)
                need(eng, o_out, 4 * (b - 1))
                eng.tensor_tensor(otail[:, j, :, :], pb[:, 0:P].rearrange("p (g s) -> p g s", g=CT),
                                  vt[:, :, bass.ds(b, 1)].broadcast_to([P, CT, S]), ALU.mult).then_inc(ot_made, 1)

            def o_evac(n, j):
                b = 2 * n + j
                eng.wait_ge(pv_done, b + 1)
                eng.wait_ge(ot_made, b + 1)
                for h in range(4):
                    r = slice(h * S, (h + 1) * S)
                    eng.tensor_tensor(O_T[r, :, bass.ds(b * S, S)], po[r, :].rearrange("p (g n) -> p g n", g=CT)[:, :, r],
                                      otail[r, j, :, :], ALU.add).then_inc(o_out, 1)

            def pair(n, p, first, last):
                k_evac(n, 0)
                if not first:
                    pt_evac(n - 1, 1)
                k_evac(n, 1)
                if not first:
                    o_evac(n - 1, 0)
                if not last:
                    ctx_split(n + 1, 1 - p)
                k_evac(n, 2)
                if not first:
                    o_evac(n - 1, 1)
                else:
                    tail_keys()
                k_evac(n, 3)
                mask_max(n, 0)
                mask_max(n, 1)
                normalise(n, 0)
                pt_evac(n, 0)
                normalise(n, 1)

            ctx_split(0, 0)
            eng.wait_ge(w_hi, 3)
            split_lo(wv_lo[:, :, :], wv_raw, wv_hi[:, :, :]).then_inc(w_lo, 1)
            eng.wait_ge(w_hi, 4)
            eng.wait_ge(small_in, 5 * 16)
            split_lo(t_lo[:, :, :], tail[:, :, :], t_hi[:, :, :]).then_inc(w_lo, 1)
            pair(0, 0, True, False)
            pair(1, 1, False, False)
            with eng.Fori(1, NT - 1) as i:
                pair(2 * i, 0, False, False)
                pair(2 * i + 1, 1, False, False)
            pair(NPAIR - 2, 0, False, False)
            pair(NPAIR - 1, 1, False, True)
            pt_evac(NPAIR - 1, 1)
            o_evac(NPAIR - 1, 0)
            o_evac(NPAIR - 1, 1)


def layer_norm(eng, ch, stats, mv, rstd, tmp, x, z, seen):
    eng.sem_inc(seen, 1)
    ch.link(eng.bn_stats(stats[:, :], x))
    eng.sem_inc(seen, 1)
    ch.link(eng.bn_aggr(mv[:, :], stats[:, :]))
    ch.link(eng.tensor_scalar(mv[:, 1:2], mv[:, 1:2], LN_EPS, None, ALU.add))
    rsqrt(eng, ch, rstd[:, :], mv[:, 1:2], tmp[:, :])
    return eng.tensor_scalar(z, x, mv[:, 0:1], rstd[:, 0:1], ALU.subtract, ALU.mult)


def row_on_all(v):
    return v.unsqueeze(0).broadcast_to([P, v.shape[0]])


def self_attention(nc, io, x_nat, ident, O_T, raw, w_in, ln3):
    with ExitStack() as ctx:
        def sb(name, shape, dt=F32):
            return ctx.enter_context(nc.sbuf_tensor(name, shape, dt))

        def ps(name, shape):
            return ctx.enter_context(nc.psum_tensor(name, shape, F32))

        def sem(name):
            return ctx.enter_context(nc.semaphore(name))

        w_hi = [sb(f"w5_hi{i}", [P, CT, D], F32R) for i in range(5)]
        w_lo = [sb(f"w5_lo{i}", [P, CT, D], F32R) for i in range(5)]
        bv, bo, bqkv, bproj = sb("bv", [P, CT]), sb("bo", [P, D]), sb("bqkv", [P, 3, D]), sb("bproj", [P, D])
        qk_w = sb("qk_w", [P, 2])
        o_b = sb("o_b", [P, CT, P])
        o_hi, o_lo = sb("o_hi", [P, CT, P], F32R), sb("o_lo", [P, CT, P], F32R)
        stats, mv = sb("stats2", [P, 2, 6]), sb("mv2", [P, 2, 2])
        rstd, tmp = sb("rstd2", [P, 2]), sb("tmp2", [P, 2])
        z2, z3s = sb("z2", [P, D]), sb("z3s", [P, D])
        z2_hi, z2_lo = sb("z2_hi", [P, CT, P], F32R), sb("z2_lo", [P, CT, P], F32R)
        qk, v = sb("qk", [P, 2, D]), sb("v", [P, D])
        sq = sb("sq", [P, 2 * D])
        ms, rms, tmp32 = sb("ms", [P, 2 * H]), sb("rms", [P, 2 * H]), sb("tmp32", [P, 2 * H])
        q_T, k_T = sb("q_T", [P, CT, P]), sb("k_T", [P, CT, P])
        mx, sm, rs = sb("mx", [P, H]), sb("sm", [P, H]), sb("rs", [P, H])
        e = sb("e", [P, H * S])
        e_T = sb("e_T", [P, H * S])
        o2_hi, o2_lo = sb("o2_hi", [P, CT, P], F32R), sb("o2_lo", [P, CT, P], F32R)

        pw = [ps(f"pw{i}", [P, D]) for i in range(2)]
        pt = [ps(f"pt{i}", [P, D]) for i in range(2)]
        pa = ps("pa", [P, 4, D])

        bv_in, small_in = sem("bv_in"), sem("small_in2")
        whi, wlo, scaled = sem("whi"), sem("wlo"), sem("scaled")
        dve_seen, pe_seen = sem("dve_seen"), sem("pe_seen")
        ob_made, ohi_made, olo_made, pool_seen = sem("ob_made"), sem("ohi_made"), sem("olo_made"), sem("pool_seen")
        wo_done, x1_made, z2_made, x1b_made, z2T_done, z2hi_made, z2lo_made = (
            sem(n) for n in ("wo_done", "x1_made", "z2_made", "x1b_made", "z2T_done", "z2hi_made", "z2lo_made"))
        qkv_done, qk_out, v_out, sq_made, qkn_made, x0_made, qkT_done, qT_out, kT_out = (
            sem(n) for n in ("qkv_done", "qk_out", "v_out2", "sq_made", "qkn_made", "x0_made", "qkT_done", "qT_out", "kT_out"))
        s_done, shifted, e_made, eT_made, pv_done, o2hi_made, o2lo_made = (
            sem(n) for n in ("s_done2", "shifted", "e_made", "eT_made", "pv_done2", "o2hi_made", "o2lo_made"))
        proj_done, x2_made, z3_made, z3T_done, z3T_out, step = (
            sem(n) for n in ("proj_done", "x2_made", "z3_made", "z3T_done", "z3T_out", "step2"))

        def steps(eng, body):
            for it in range(3):
                body(it)
            with eng.Fori(3, NT) as i:
                body(i)
            for it in range(NT, NT + 3):
                body(it)

        def has(it, lag):
            return not isinstance(it, int) or 0 <= it - lag < NT

        block = ctx.enter_context(nc.Block())

        @block.sync
        def _(eng):
            eng.dma_start(bv[:, :], io["bv"]).then_inc(bv_in, 16)
            eng.dma_start(qk_w[:, :], io["qk_w"]).then_inc(small_in, 16)
            for name, dst in (("bo", bo[:, :]), ("bqkv", bqkv[:, :, :].rearrange("p a n -> p (a n)")), ("bproj", bproj[:, :])):
                eng.dma_start(dst, row_on_all(io[name])).then_inc(small_in, 16)
            for i in range(2, 5):
                eng.wait_ge(wlo, i - 1)
                eng.dma_start(raw[:, i % 2, :], io["w5"][i]).then_inc(w_in[i % 2], 16)

        @block.gpsimd
        def _(eng):
            def body(it):
                if has(it, 0):
                    cols = bass.ds(it * P, P)
                    if isinstance(it, int) and it == 0:
                        eng.wait_ge(bv_in, 16)
                    need(eng, olo_made, it)
                    eng.tensor_tensor(o_b[:, :, :], O_T[:, :, cols], bv[:, :].unsqueeze(2).broadcast_to([P, CT, P]),
                                      ALU.add).then_inc(ob_made, 1)
                    eng.wait_ge(ob_made, it + 1)
                    need(eng, wo_done, it)
                    eng.sem_inc(pool_seen, 1)
                    eng.tensor_copy(o_hi[:, :, :], o_b[:, :, :]).then_inc(ohi_made, 1)
                    eng.wait_ge(ohi_made, it + 1)
                    eng.tensor_tensor(o_lo[:, :, :], o_b[:, :, :], o_hi[:, :, :].bitcast(F32), ALU.subtract).then_inc(olo_made, 1)
                    if isinstance(it, int) and it == 0:
                        eng.wait_ge(small_in, 4 * 16)
                    x_t = x_nat[:, bass.ds(it, 1), :]
                    eng.tensor_tensor(x_t, x_t, bo[:, :].unsqueeze(1), ALU.add).then_inc(x0_made, 1)
                    eng.wait_ge(z2_made, it + 1)
                    eng.sem_inc(pool_seen, 1)
                    eng.tensor_tensor(x_t, x_t, bproj[:, :].unsqueeze(1), ALU.add).then_inc(x1b_made, 1)

            steps(eng, body)

        @block.tensor
        def _(eng):
            def project(out, hi, lo, i):
                for c in range(CT):
                    mm = three(eng, out, hi[:, c, :], lo[:, c, :], w_hi[i][:, c, :], w_lo[i][:, c, :], c == 0, c == CT - 1)
                return mm

            eng.sem_inc(z3T_done, 1)

            def body(it):
                if has(it, 0):
                    if isinstance(it, int) and it == 0:
                        eng.wait_ge(wlo, 1)
                    eng.wait_ge(olo_made, it + 1)
                    if has(it, 2):
                        eng.wait_ge(qk_out, 2 * (it - 1))
                    else:
                        need(eng, x1_made, it)
                    project(pw[0][:, :], o_hi, o_lo, 0).then_inc(wo_done, 1)
                if has(it, 3):
                    u = it - 3
                    eng.wait_ge(o2lo_made, u + 1)
                    if has(it, 2):
                        eng.wait_ge(v_out, u + 2)
                    else:
                        eng.wait_ge(x2_made, u)
                    project(pw[1][:, :], o2_hi, o2_lo, 4).then_inc(proj_done, 1)
                if has(it, 2):
                    u = it - 2
                    eng.wait_ge(qkn_made, u + 1)
                    need(eng, z2lo_made, u + 2 if has(it, 1) else u + 1)
                    for i in range(2):
                        if i == 1:
                            need(eng, z3T_out, u)
                        for g in range(CT):
                            mm = eng.transpose(pt[i][:, g * P:(g + 1) * P], qk[:, i, g * P:(g + 1) * P], ident[:, :])
                        mm.then_inc(qkT_done, 1)

                def qkv(i):
                    u = it - 1
                    if isinstance(it, int) and it == 1:
                        eng.wait_ge(wlo, i + 2)
                    if isinstance(it, int) and it == 2:
                        eng.wait_ge(wlo, 5)
                    if i == 0:
                        eng.wait_ge(z2lo_made, u + 1)
                        if has(it, 0):
                            eng.wait_ge(x1_made, it + 1)
                        else:
                            eng.wait_ge(qk_out, 2 * u)
                    elif i == 1:
                        eng.wait_ge(qk_out, 2 * u + 1)
                    elif has(it, 3):
                        eng.wait_ge(x2_made, it - 2)
                    else:
                        need(eng, v_out, u)
                    project(pw[i // 2][:, :], z2_hi, z2_lo, i + 1).then_inc(qkv_done, 1)

                if has(it, 1):
                    qkv(0)
                if has(it, 2):
                    u = it - 2
                    eng.wait_ge(qT_out, u + 1)
                    eng.wait_ge(kT_out, u + 1)
                    need(eng, o2lo_made, u)
                    eng.sem_inc(pe_seen, 1)
                    for g in range(CT):
                        for b in range(4):
                            for r in range(4):
                                rows, cols = slice(r * HD, (r + 1) * HD), slice(b * S, (b + 1) * S)
                                mm = eng.matmul(pa[cols, r, g * S:(g + 1) * S], q_T[rows, g, cols], k_T[rows, g, cols],
                                                start=True, stop=True)
                    mm.then_inc(s_done, 1)
                if has(it, 1):
                    qkv(1)
                    qkv(2)
                if has(it, 2):
                    u = it - 2
                    eng.wait_ge(eT_made, u + 1)
                    eng.sem_inc(pe_seen, 1)
                    for g in range(CT):
                        for r in range(4):
                            for b in range(4):
                                keys, ds = slice(b * S, (b + 1) * S), slice(r * HD, (r + 1) * HD)
                                h = 4 * g + r
                                mm = eng.matmul(pa[ds, b, g * S:(g + 1) * S], v[keys, h * HD:(h + 1) * HD],
                                                e_T[keys, (r * CT + g) * S:(r * CT + g + 1) * S], start=True, stop=True)
                    mm.then_inc(pv_done, 1)
                if has(it, 0):
                    eng.wait_ge(z2_made, it + 1)
                    need(eng, qT_out, it - 1)
                    if not has(it, 2):
                        need(eng, z2lo_made, it)
                    for c in range(CT):
                        mm = eng.transpose(pt[0][:, c * P:(c + 1) * P], z2[:, c * P:(c + 1) * P], ident[:, :])
                    mm.then_inc(z2T_done, 1)
                if has(it, 3):
                    u = it - 3
                    eng.wait_ge(z3_made, u + 1)
                    if has(it, 2):
                        eng.wait_ge(kT_out, u + 2)
                    else:
                        eng.wait_ge(z3T_out, u + 1)
                    for c in range(CT):
                        mm = eng.transpose(pt[1][:, c * P:(c + 1) * P], z3s[:, c * P:(c + 1) * P], ident[:, :])
                    mm.then_inc(z3T_done, 1)

            steps(eng, body)

        splits = {0: (0, 1), 1: (2, 3), 2: (4,)}

        def splits_before(it):
            return splits.get(it, ()) if isinstance(it, int) else ()

        @block.scalar
        def _(eng):
            eng.sem_inc(z3T_out, 1)

            def body(it):
                for i in splits_before(it):
                    eng.wait_ge(w_in[i % 2], 16 * (i // 2 + 1))
                    eng.activation(w_hi[i][:, :, :], raw[:, i % 2, :].rearrange("p (c n) -> p c n", c=CT),
                                   ACT.Copy).then_inc(whi, 1)
                if has(it, 2):
                    u = it - 2
                    eng.wait_ge(qkT_done, 2 * u + 1)
                    if isinstance(it, int) and it == 2:
                        eng.wait_ge(scaled, 1)
                    need(eng, s_done, u)
                    eng.activation(q_T[:, :, :].rearrange("p g t -> p (g t)"), pt[0][:, :], ACT.Copy,
                                   scale=qk_w[:, 0:1]).then_inc(qT_out, 1)
                    eng.wait_ge(qkT_done, 2 * u + 2)
                    eng.activation(k_T[:, :, :].rearrange("p g t -> p (g t)"), pt[1][:, :], ACT.Copy,
                                   scale=qk_w[:, 1:2]).then_inc(kT_out, 1)
                if has(it, 1):
                    u = it - 1
                    eng.wait_ge(qk_out, 2 * u + 1)
                    eng.activation(sq[:, 0:D], qk[:, 0, :], ACT.Square).then_inc(sq_made, 1)
                if has(it, 2):
                    eng.wait_ge(shifted, it - 1)
                    eng.activation(e[:, :], e[:, :], ACT.Exp).then_inc(e_made, 1)
                if has(it, 1):
                    u = it - 1
                    eng.wait_ge(qk_out, 2 * u + 2)
                    eng.activation(sq[:, D:2 * D], qk[:, 1, :], ACT.Square).then_inc(sq_made, 1)
                if has(it, 2):
                    u = it - 2
                    eng.wait_ge(pv_done, u + 1)
                    need(eng, proj_done, u)
                    eng.activation(o2_hi[:, :, :].rearrange("p g (b s) -> p b g s", b=4),
                                   pa[:, :, 0:P].rearrange("p b (g s) -> p b g s", g=CT), ACT.Copy).then_inc(o2hi_made, 1)
                if has(it, 0):
                    eng.wait_ge(z2T_done, it + 1)
                    need(eng, qkv_done, 3 * it)
                    eng.activation(z2_hi[:, :, :].rearrange("p c t -> p (c t)"), pt[0][:, :], ACT.Copy).then_inc(z2hi_made, 1)
                if has(it, 3):
                    u = it - 3
                    eng.wait_ge(z3T_done, u + 2)
                    eng.activation(O_T[:, :, bass.ds(u * P, P)], pt[1][:, :].rearrange("p (c t) -> p c t", c=CT),
                                   ACT.Copy).then_inc(z3T_out, 1)

            steps(eng, body)

        @block.vector
        def _(eng):
            count = {"at": 0}

            def body(it):
                whole = not isinstance(it, int)
                ch = Chain(eng, step, count["at"] if not whole else count["at"] + (it - 3) * PER_STEP)
                for i in splits_before(it):
                    eng.wait_ge(whi, i + 1)
                    eng.tensor_tensor(w_lo[i][:, :, :], raw[:, i % 2, :].rearrange("p (c n) -> p c n", c=CT),
                                      w_hi[i][:, :, :].bitcast(F32), ALU.subtract).then_inc(wlo, 1)
                    if i == 1:
                        eng.wait_ge(small_in, 4 * 16)
                        eng.tensor_scalar(qk_w[:, 0:1], qk_w[:, 0:1], SCALE, None, ALU.mult).then_inc(scaled, 1)

                def stats_of(k, x):
                    eng.sem_inc(dve_seen, 1)
                    ch.link(eng.bn_stats(stats[:, k, :], x))
                    eng.sem_inc(dve_seen, 1)
                    ch.link(eng.bn_aggr(mv[:, k, :], stats[:, k, :]))

                if has(it, 0):
                    x_t = x_nat[:, bass.ds(it, 1), :]
                    eng.wait_ge(x0_made, it + 1)
                    eng.wait_ge(wo_done, it + 1)
                    eng.sem_inc(dve_seen, 1)
                    eng.tensor_tensor(x_t, pw[0][:, :].unsqueeze(1), x_t, ALU.add).then_inc(x1_made, 1)
                    eng.wait_ge(x1_made, it + 1)
                    stats_of(0, x_t)
                if has(it, 3):
                    u = it - 3
                    x_u = x_nat[:, bass.ds(u, 1), :]
                    eng.wait_ge(x1b_made, u + 1)
                    eng.wait_ge(proj_done, u + 1)
                    eng.sem_inc(dve_seen, 1)
                    eng.tensor_tensor(x_u, pw[1][:, :].unsqueeze(1), x_u, ALU.add).then_inc(x2_made, 1)
                    eng.wait_ge(x2_made, u + 1)
                    stats_of(1, x_u)
                if has(it, 0) or has(it, 3):
                    k = slice(0 if has(it, 0) else 1, 2 if has(it, 3) else 1)
                    ch.link(eng.tensor_scalar(mv[:, k, 1], mv[:, k, 1], LN_EPS, None, ALU.add))
                    rsqrt(eng, ch, rstd[:, k], mv[:, k, 1], tmp[:, k])
                if has(it, 0):
                    need(eng, z2T_done, it)
                    eng.tensor_scalar(z2[:, :].unsqueeze(1), x_t, mv[:, 0, 0:1], rstd[:, 0:1],
                                      ALU.subtract, ALU.mult).then_inc(z2_made, 1)
                if has(it, 1):
                    eng.wait_ge(qkv_done, 3 * (it - 1) + 1)
                    need(eng, qkT_done, 2 * (it - 1))
                    eng.tensor_tensor(qk[:, 0, :], pw[0][:, :], bqkv[:, 0, :], ALU.add).then_inc(qk_out, 1)
                if has(it, 3):
                    need(eng, z3T_done, u + 1)
                    eng.tensor_scalar(z3s[:, :].unsqueeze(1), x_u, mv[:, 1, 0:1], rstd[:, 1:2],
                                      ALU.subtract, ALU.mult).then_inc(z3_made, 1)
                    ch.link(eng.tensor_copy(ln3[:, bass.ds(u, 1), 0], mv[:, 1, 0:1]))
                    ch.link(eng.tensor_copy(ln3[:, bass.ds(u, 1), 1], rstd[:, 1:2]))
                if has(it, 2):
                    u = it - 2
                    s_p = pa[:, :, 0:P].rearrange("p r (g k) -> p r g k", g=CT)
                    e4 = e[:, :].rearrange("p (r g k) -> p r g k", r=4, g=CT)
                    eng.wait_ge(s_done, u + 1)
                    ch.link(eng.tensor_reduce(mx[:, :], s_p, AX.X, ALU.max))
                    m4 = mx[:, :].rearrange("p (r g) -> p r g", r=4).unsqueeze(3).broadcast_to([P, 4, CT, S])
                    eng.tensor_tensor(e4, s_p, m4, ALU.subtract).then_inc(shifted, 1)
                    eng.wait_ge(e_made, u + 1)
                    e3 = e[:, :].rearrange("p (h k) -> p h k", k=S)
                    ch.link(eng.tensor_reduce(sm[:, :], e3, AX.X, ALU.add))
                    ch.link(eng.reciprocal(rs[:, :], sm[:, :]))
                    ch.link(eng.tensor_tensor(e3, e3, rs[:, :].unsqueeze(2).broadcast_to([P, H, S]), ALU.mult))
                    need(eng, pv_done, u)
                    eng.transpose(e_T[:, :], e[:, :]).then_inc(eT_made, 1)
                if has(it, 1):
                    u = it - 1
                    eng.wait_ge(qkv_done, 3 * u + 2)
                    eng.tensor_tensor(qk[:, 1, :], pw[0][:, :], bqkv[:, 1, :], ALU.add).then_inc(qk_out, 1)
                    eng.wait_ge(sq_made, 2 * u + 2)
                    ch.link(eng.tensor_reduce(ms[:, :], sq[:, :].rearrange("p (h d) -> p h d", d=HD), AX.X, ALU.add))
                    ch.link(eng.tensor_scalar(ms[:, :], ms[:, :], 1.0 / HD, RMS_EPS, ALU.mult, ALU.add))
                    rsqrt(eng, ch, rms[:, :], ms[:, :], tmp32[:, :])
                    eng.wait_ge(qkv_done, 3 * u + 3)
                    need(eng, pv_done, u)
                    eng.tensor_tensor(v[:, :], pw[1][:, :], bqkv[:, 2, :], ALU.add).then_inc(v_out, 1)
                if has(it, 2):
                    u = it - 2
                    eng.wait_ge(o2hi_made, u + 1)
                    eng.tensor_tensor(o2_lo[:, :, :].rearrange("p g (b s) -> p b g s", b=4),
                                      pa[:, :, 0:P].rearrange("p b (g s) -> p b g s", g=CT),
                                      o2_hi[:, :, :].rearrange("p g (b s) -> p b g s", b=4).bitcast(F32),
                                      ALU.subtract).then_inc(o2lo_made, 1)
                if has(it, 1):
                    qk3 = qk[:, :, :].rearrange("p i (h d) -> p (i h) d", d=HD)
                    eng.tensor_tensor(qk3, qk3, rms[:, :].unsqueeze(2).broadcast_to([P, 2 * H, HD]),
                                      ALU.mult).then_inc(qkn_made, 1)
                if has(it, 0):
                    eng.wait_ge(z2hi_made, it + 1)
                    eng.tensor_tensor(z2_lo[:, :, :].rearrange("p c t -> p (c t)"), pt[0][:, :],
                                      z2_hi[:, :, :].rearrange("p c t -> p (c t)").bitcast(F32), ALU.subtract).then_inc(z2lo_made, 1)
                if whole:
                    assert ch.k == PER_STEP
                    count["at"] += (NT - 3) * PER_STEP
                else:
                    count["at"] += ch.k

            RSQRT = 2 + 3 * 3
            PER_STEP = 2 + 2 + (1 + RSQRT) + 2 + 1 + 3 + (2 + RSQRT)
            steps(eng, body)


def experts(nc, io, out, x_nat, ident, ln3, z_T, raw):
    HT = T // 2
    NH = NT // 2
    EC = 3
    with ExitStack() as ctx:
        def sb(name, shape, dt=F32):
            return ctx.enter_context(nc.sbuf_tensor(name, shape, dt))

        def ps(name, shape):
            return ctx.enter_context(nc.psum_tensor(name, shape, F32))

        def sem(name):
            return ctx.enter_context(nc.semaphore(name))

        BF = mybir.dt.bfloat16
        y = raw[:, :, EC * D:EC * D + D]
        g_raw = y[:, 0, :].rearrange("p (c n) -> p c n", c=CT)
        b2 = y[0:E, 1, :]
        w1_hi, w1_lo = sb("w1_hi", [P, EC, CT, EC * DM], F32R), sb("w1_lo", [P, EC, CT, EC * DM], F32R)
        w2_hi, w2_lo = sb("w2_hi", [P, E, D], F32R), sb("w2_lo", [P, E, D], F32R)
        g_hi, g_lo = sb("g_hi", [P, CT, DM], F32R), sb("g_lo", [P, CT, DM], F32R)
        wo2 = sb("wo2", [P, E])
        b1, bo1, bo2 = sb("b1", [P, E]), sb("bo1", [P, 1]), sb("bo2", [P, E])
        b2_hi, b2_lo = sb("b2_hi", [E, D], F32R), sb("b2_lo", [E, D], F32R)
        gamma, beta = sb("gamma", [P, D]), sb("beta", [P, D])
        mixw = sb("mixw", [P, 3, CT])
        xm = sb("xm", [P, CT, HT])
        xm_hi, xm_lo = sb("xm_hi", [P, CT, HT], F32R), sb("xm_lo", [P, CT, HT], F32R)
        th = xm[:, 2, :]
        rank = sb("rank", [P, E])
        gs, key, top = sb("gs", [P, NH, E]), sb("key", [P, NH, E]), sb("top", [P, NH])
        choice = sb("choice", [P, NH, E])
        choice_T, choice_b = sb("choice_T", [E, HT], F32R), sb("choice_b", [E, HT], BF)
        sel = sb("sel", [E, E, P], BF)
        chosen = sb("chosen", [P, 2, HT], BF)
        h = xm[:, 0:2, :]
        z = sb("z3n", [P, 2, D])
        h_hi, h_lo = sb("h_hi", [P, E, HT], F32R), sb("h_lo", [P, E, HT], F32R)
        stats, mv, rstd, tmp = sb("stats3", [P, 6]), sb("mv3", [P, 2]), sb("rstd3", [P, 1]), sb("tmp3", [P, 1])

        ph = [ps(f"ph{i}", [P, D]) for i in range(2)]
        pc = [ps(f"pc{i}", [P, D]) for i in range(2)]
        pg = ps("pg", [P, D])
        py = [ps(f"py{i}", [P, D]) for i in range(2)]

        small_in, w1_in, w2_in = sem("small_in3"), sem("w1_in"), sem("w2_in")
        (whi, wlo, mix_made, xmhi, xmlo, g_done, th_made, gs_done, choice_made, cT_done, cT_out, cb_out, consts, pc_done,
         pc_out, h_done, h_made, hhi, hlo, y_done, y_made, xb_made, zn_made, fin, step) = (
            sem("s3_" + n) for n in (
                "whi wlo mix_made xmhi xmlo g_done th_made gs_done choice_made cT_done cT_out cb_out consts pc_done "
                "pc_out h_done h_made hhi hlo y_done y_made xb_made zn_made fin step").split())
        dve_seen = sem("dve_seen3")
        stored = [sem(f"stored{p}") for p in range(2)]
        block = ctx.enter_context(nc.Block())

        def landing(i):
            return raw[:, i % 2, 0:CT * EC * DM]

        @block.sync
        def _(eng):
            eng.dma_start(y[:, 0, :], io["wo1"]).then_inc(small_in, 16)
            for name, dst in (("mixw", mixw[:, :, :].rearrange("p a c -> p (a c)")), ("wo2", wo2[:, :]), ("b1", b1[:, :]),
                              ("bo1", bo1[:, :]), ("b2", b2)):
                eng.dma_start(dst, io[name]).then_inc(small_in, 16)
            for name, dst in (("bo2", bo2[:, :]), ("gamma", gamma[:, :]), ("beta", beta[:, :])):
                eng.dma_start(dst, row_on_all(io[name])).then_inc(small_in, 16)
            for i in range(3):
                need(eng, wlo, i - 1 + 1 if i >= 2 else 0)
                eng.dma_start(landing(i), io["w1"][i]).then_inc(w1_in, 16)
                eng.wait_ge(w1_in, 16 * (i + 1))
            for i in range(3):
                eng.wait_ge(wlo, i + 3)
                eng.dma_start(landing(i + 3), io["w2"][i]).then_inc(w2_in, 16)
                eng.wait_ge(w2_in, 16 * (i + 1))
            for t in range(NT):
                eng.wait_ge(fin, t + 1)
                eng.dma_start(out[t], y[:, t % 2, :]).then_inc(stored[t % 2], 16)
            for p in range(2):
                eng.wait_ge(stored[p], 16 * NH)

        @block.gpsimd
        def _(eng):
            eng.wait_ge(small_in, 9 * 16)
            for t in range(NT):
                need(eng, y_made, t - 1)
                eng.tensor_scalar(z[:, t % 2, :], x_nat[:, t, :], ln3[:, t, 0:1], ln3[:, t, 1:2],
                                  ALU.subtract, ALU.mult).then_inc(zn_made, 1)
                eng.wait_ge(zn_made, t + 1)
                eng.tensor_tensor(x_nat[:, t, :], x_nat[:, t, :], beta[:, :], ALU.add).then_inc(xb_made, 1)

        @block.tensor
        def _(eng):
            for hf in range(2):
                eng.wait_ge(wlo, 1)
                eng.wait_ge(xmlo, hf + 1)
                for c in range(CT):
                    mm = three(eng, pg[:, :], g_hi[:, c, :], g_lo[:, c, :], xm_hi[:, c, :], xm_lo[:, c, :], c == 0, c == CT - 1)
                mm.then_inc(g_done, 1)

                def hidden(e):
                    k = E * hf + e
                    if hf == 0 and e % EC == 0:
                        eng.wait_ge(wlo, 2 + e // EC)
                    need(eng, h_made, k - 1)
                    for c in range(CT):
                        cols = slice(e % EC * DM, (e % EC + 1) * DM)
                        mm = three(eng, ph[k % 2][:, :], w1_hi[:, e // EC, c, cols], w1_lo[:, e // EC, c, cols],
                                   xm_hi[:, c, :], xm_lo[:, c, :], c == 0, c == CT - 1)
                    mm.then_inc(h_done, 1)

                def spread(e):
                    k = E * hf + e
                    eng.wait_ge(cb_out, hf + 1)
                    need(eng, pc_out, k - 1)
                    eng.matmul(pc[k % 2][:, :], sel[:, e, :], choice_b[:, :], start=True, stop=True).then_inc(pc_done, 1)

                hidden(0)
                eng.wait_ge(th_made, hf + 1)
                for t in range(NH):
                    mm = eng.matmul(pg[:, t * E:(t + 1) * E], th[:, t * P:(t + 1) * P], wo2[:, :], start=True, stop=True)
                mm.then_inc(gs_done, 1)
                hidden(1)
                eng.wait_ge(choice_made, hf + 1)
                for t in range(NH):
                    mm = eng.transpose(pg[0:E, t * P:(t + 1) * P], choice[:, t, :], ident[:, :])
                mm.then_inc(cT_done, 1)
                spread(0)
                spread(1)
                for e in range(2, E):
                    hidden(e)
                    spread(e)
                for t in range(NH):
                    k = NH * hf + t
                    need(eng, y_made, k - 1)
                    cols = slice(t * P, (t + 1) * P)
                    eng.wait_ge(cT_out, hf + 1)
                    eng.matmul(py[k % 2][:, :], choice_T[:, cols], b2_hi[:, :], start=True, stop=False)
                    eng.matmul(py[k % 2][:, :], choice_T[:, cols], b2_lo[:, :], start=False, stop=False)
                    for e in range(E):
                        if t == 0:
                            eng.wait_ge(hlo, E * hf + e + 1)
                            if hf == 0 and e % EC == 0:
                                eng.wait_ge(wlo, 5 + e // EC)
                        mm = three(eng, py[k % 2][:, :], h_hi[:, e, cols], h_lo[:, e, cols], w2_hi[:, e, :], w2_lo[:, e, :],
                                   False, e == E - 1)
                    mm.then_inc(y_done, 1)

        def w_parts(i, w1, w2):
            if i <= 3:
                return w1[:, i - 1, :, :].rearrange("p c n -> p (c n)")
            return w2[:, (i - 4) * EC:(i - 3) * EC, :].rearrange("p e n -> p (e n)")

        def w_size(i):
            return CT * EC * DM if i <= 3 else EC * D

        @block.scalar
        def _(eng):
            def w_split(i):
                if i <= 3:
                    eng.wait_ge(w1_in, 16 * i)
                else:
                    eng.wait_ge(w2_in, 16 * (i - 3))
                eng.activation(w_parts(i, w1_hi, w2_hi), raw[:, (i - 1) % 2, 0:w_size(i)], ACT.Copy).then_inc(whi, 1)

            eng.wait_ge(small_in, 9 * 16)
            eng.activation(g_hi[:, :, :], g_raw, ACT.Copy).then_inc(whi, 1)
            for hf in range(2):
                eng.wait_ge(mix_made, 12 * (hf + 1))
                if hf:
                    eng.wait_ge(h_done, E * hf)
                eng.activation(xm_hi[:, :, :], xm[:, :, :], ACT.Copy).then_inc(xmhi, 1)
                if hf == 0:
                    w_split(1)
                    w_split(2)
                eng.wait_ge(g_done, hf + 1)
                eng.activation(th, pg[:, :], ACT.Tanh, bias=bo1[:, 0:1]).then_inc(th_made, 1)
                if hf == 0:
                    w_split(3)
                    eng.wait_ge(consts, 2)
                    eng.activation(b2_hi[:, :], b2, ACT.Copy).then_inc(consts, 1)
                eng.wait_ge(cT_done, hf + 1)
                if hf:
                    eng.wait_ge(y_done, NH)
                eng.activation(choice_T[:, :], pg[0:E, :], ACT.Copy).then_inc(cT_out, 1)
                for e in range(E):
                    k = E * hf + e
                    eng.wait_ge(pc_done, k + 1)
                    need(eng, h_made, k - 1)
                    eng.activation(chosen[:, k % 2, :], pc[k % 2][:, :], ACT.Copy).then_inc(pc_out, 1)
                    eng.wait_ge(h_made, k + 1)
                    if hf:
                        eng.wait_ge(y_done, NH)
                    eng.activation(h_hi[:, e, :], h[:, k % 2, :], ACT.Copy).then_inc(hhi, 1)
                    if hf == 0 and e in (1, 3, 5):
                        w_split(4 + e // 2)

        @block.vector
        def _(eng):
            ch = Chain(eng, step)

            def w_split(i):
                eng.wait_ge(whi, i + 1)
                eng.tensor_tensor(w_parts(i, w1_lo, w2_lo), raw[:, (i - 1) % 2, 0:w_size(i)],
                                  w_parts(i, w1_hi, w2_hi).bitcast(F32), ALU.subtract).then_inc(wlo, 1)

            def mix(hf):
                cols = slice(hf * HT, (hf + 1) * HT)
                for c in range(CT):
                    eng.tensor_scalar(xm[:, c, :], z_T[:, c, cols], mixw[:, 1, c:c + 1], None, ALU.mult).then_inc(mix_made, 1)
                for a, (dst, src) in ((0, (slice(1, S), slice(0, S - 1))), (2, (slice(0, S - 1), slice(1, S)))):
                    for c in range(CT):
                        xc = xm[:, c, :].rearrange("p (b s) -> p b s", s=S)
                        zc = z_T[:, c, cols].rearrange("p (b s) -> p b s", s=S)
                        eng.wait_ge(mix_made, 12 * hf + 4 * (a // 2) + c + 1)
                        eng.scalar_tensor_tensor(out=xc[:, :, dst], in0=zc[:, :, src], scalar=mixw[:, a, c:c + 1],
                                                 in1=xc[:, :, dst], op0=ALU.mult, op1=ALU.add).then_inc(mix_made, 1)

            def xm_split(hf):
                eng.wait_ge(xmhi, hf + 1)
                eng.tensor_tensor(xm_lo[:, :, :], xm[:, :, :], xm_hi[:, :, :].bitcast(F32), ALU.subtract).then_inc(xmlo, 1)

            eng.wait_ge(small_in, 9 * 16)
            mix(0)
            eng.wait_ge(whi, 1)
            eng.tensor_tensor(g_lo[:, :, :], g_raw, g_hi[:, :, :].bitcast(F32), ALU.subtract).then_inc(wlo, 1)
            xm_split(0)
            w_split(1)
            for e in range(E):
                eng.memset(rank[:, e:e + 1], float(E - e))
            eng.tensor_copy(sel[:, :, :], ident[0:E, 0:E].unsqueeze(2).broadcast_to([E, E, P])).then_inc(consts, 2)
            w_split(2)
            for hf in range(2):
                eng.wait_ge(gs_done, hf + 1)
                bc = [P, NH, E]
                ch.link(eng.tensor_tensor(gs[:, :, :], pg[:, 0:NH * E].rearrange("p (t e) -> p t e", t=NH),
                                          bo2[:, :].unsqueeze(1).broadcast_to(bc), ALU.add))
                ch.link(eng.tensor_reduce(top[:, :], gs[:, :, :], AX.X, ALU.max))
                ch.link(eng.tensor_tensor(key[:, :, :], gs[:, :, :], top[:, :].unsqueeze(2).broadcast_to(bc), ALU.is_equal))
                ch.link(eng.tensor_tensor(key[:, :, :], key[:, :, :], rank[:, :].unsqueeze(1).broadcast_to(bc), ALU.mult))
                ch.link(eng.tensor_reduce(top[:, :], key[:, :, :], AX.X, ALU.max))
                eng.tensor_tensor(choice[:, :, :], key[:, :, :], top[:, :].unsqueeze(2).broadcast_to(bc),
                                  ALU.is_equal).then_inc(choice_made, 1)
                eng.wait_ge(cT_out, hf + 1)
                eng.tensor_copy(choice_b[:, :], choice_T[:, :].bitcast(F32)).then_inc(cb_out, 1)
                if hf == 0:
                    w_split(3)
                    eng.wait_ge(consts, 3)
                    eng.tensor_tensor(b2_lo[:, :], b2, b2_hi[:, :].bitcast(F32), ALU.subtract).then_inc(consts, 1)
                for e in range(E):
                    k = E * hf + e
                    eng.wait_ge(pc_out, k + 1)
                    eng.wait_ge(h_done, k + 1)
                    need(eng, hlo, k - 1)
                    eng.scalar_tensor_tensor(out=h[:, k % 2, :], in0=ph[k % 2][:, :], scalar=b1[:, e:e + 1],
                                             in1=chosen[:, k % 2, :], op0=ALU.add, op1=ALU.mult).then_inc(h_made, 1)
                    eng.wait_ge(hhi, k + 1)
                    eng.tensor_tensor(h_lo[:, e, :], h[:, k % 2, :], h_hi[:, e, :].bitcast(F32), ALU.subtract).then_inc(hlo, 1)
                    if hf == 0 and e in (1, 3, 5):
                        w_split(4 + e // 2)
                if hf == 0:
                    eng.wait_ge(hlo, E)
                    mix(1)
                for t in range(NH):
                    if hf == 0 and t == 1:
                        xm_split(1)
                    k = NH * hf + t
                    eng.wait_ge(y_done, k + 1)
                    need(eng, stored[k % 2], 16 * (k // 2))
                    y_t = y[:, k % 2, :]
                    eng.wait_ge(zn_made, k + 1)
                    eng.tensor_tensor(y_t, py[k % 2][:, :], z[:, k % 2, :], ALU.add).then_inc(y_made, 1)
                    eng.wait_ge(y_made, k + 1)
                    ch.link(layer_norm(eng, ch, stats, mv, rstd, tmp, y_t, y_t, dve_seen))
                    ch.link(eng.tensor_tensor(y_t, y_t, gamma[:, :], ALU.mult))
                    eng.wait_ge(xb_made, k + 1)
                    eng.tensor_tensor(y_t, y_t, x_nat[:, k, :], ALU.add).then_inc(fin, 1)


def kernel(**inputs):
    import concourse.bacc as bacc
    from concourse.bass_utils import run_bass_kernel_spmd

    nc = bacc.Bacc("TRN2", target_bir_lowering=False, num_devices=1)
    a = {k: np.asarray(v) for k, v in inputs.items()}

    def rows(w):
        return w.reshape(-1, P, w.shape[1]).transpose(1, 0, 2).reshape(P, -1)

    def cols(b):
        return b.reshape(-1, P).T

    ctx = a["ctx_1024"]
    laid = {
        "x": a["x"].reshape(NT, P, D).transpose(1, 0, 2),
        "ctx": ctx[:, :SM].reshape(NPAIR, 2 * SM, CT, P).transpose(0, 3, 2, 1).reshape(NPAIR, P, CT * 2 * SM),
        "tail": ctx[:, SM].reshape(B, CT, P).transpose(2, 1, 0),
        "mask": a["mask_1x1xSxS2_ff0"].reshape(S, SK),
        "wq": rows(a["L0_xattn_Wq"].T), "wk": rows(a["L0_xattn_Wk"].T), "wv": rows(a["L0_xattn_Wv"].T),
        "w5": np.stack([rows(w) for w in [a["L0_xattn_Wo"].T, *np.split(a["L0_attn_Wqkv"].T, 3, axis=1), a["L0_attn_Wproj"].T]]),
        "bo": a["L0_xattn_bo"], "bqkv": a["L0_attn_bqkv"], "bproj": a["L0_attn_bproj"],
        "qk_w": np.stack([np.tile(a["L0_attn_qn_w"], P // HD), np.tile(a["L0_attn_kn_w"], P // HD)], axis=1),
        "w1": np.stack([rows(w.transpose(1, 0, 2).reshape(D, -1)) for w in np.split(a["L0_ffn_W1"], 3)]),
        "w2": np.stack([w.transpose(1, 0, 2).reshape(DM, -1) for w in np.split(a["L0_ffn_W2"], 3)]),
        "wo1": rows(a["L0_ffn_Wo1"]), "wo2": a["L0_ffn_Wo2"],
        "b1": a["L0_ffn_b1"].T, "bo1": a["L0_ffn_bo1"].reshape(DM, 1), "b2": a["L0_ffn_b2"], "bo2": a["L0_ffn_bo2"],
        "mixw": a["L0_ffn_mix_kernel"].reshape(3, CT, P).transpose(2, 0, 1).reshape(P, 3 * CT),
        "gamma": a["L0_ffn_gamma"], "beta": a["L0_ffn_beta"],
        "bq": cols(a["L0_xattn_bq"]), "bk": cols(a["L0_xattn_bk"]), "bv": cols(a["L0_xattn_bv"]),
    }
    laid = {k: np.ascontiguousarray(v) for k, v in laid.items()}
    io = {k: nc.dram_tensor(k + "_dram", v.shape, mybir.dt.from_np(v.dtype), kind="ExternalInput").ap() for k, v in laid.items()}
    out = nc.dram_tensor("out_dram", (NT, P, D), F32, kind="ExternalOutput").ap()
    build(nc, io, out)
    r = run_bass_kernel_spmd(nc, [{k + "_dram": v for k, v in laid.items()}], core_ids=[0])
    return r.results[0]["out_dram"].reshape(B, S, D)
```

```python
import numpy as np
import concourse.bass as bass
from concourse import mybir
from contextlib import ExitStack

F32 = mybir.dt.float32
F32R = mybir.dt.float32r
I32 = mybir.dt.int32
ALU = mybir.AluOpType
ACT = mybir.ActivationFunctionType
AX = mybir.AxisListType

P = 128
D = 512
H, HD = 16, 32
B, S = 32, 32
T = B * S
NT = T // P
CT = D // P
SK = 257
SM = 256
NPAIR = B // 2
E = 9
DM = P
SCALE = 1.0 / float(np.sqrt(HD))
LN_EPS = 1e-5
RMS_EPS = 1e-6
BIG = 3.0e38


def need(eng, sem, value):
    if isinstance(value, (int, np.integer)) and value <= 0:
        return
    eng.wait_ge(sem, value)


class Chain:

    def __init__(self, eng, sem, start=0):
        self.eng, self.sem, self.start, self.k = eng, sem, start, 0

    def link(self, ins):
        self.k += 1
        ins.then_inc(self.sem, 1)
        self.eng.wait_ge(self.sem, self.start + self.k)


def rsqrt(eng, ch, y, v, t):
    ch.link(eng.tensor_scalar(t.bitcast(I32), v.bitcast(I32), 1, None, ALU.arith_shift_right))
    ch.link(eng.tensor_scalar(y.bitcast(I32), t.bitcast(I32), -1.0, 1597463007.0, ALU.mult, ALU.add))
    for _ in range(3):
        ch.link(eng.scalar_tensor_tensor(out=t, in0=y, scalar=-0.5, in1=y, op0=ALU.mult, op1=ALU.mult))
        ch.link(eng.tensor_tensor(t, t, v, ALU.mult))
        ch.link(eng.scalar_tensor_tensor(out=y, in0=t, scalar=1.5, in1=y, op0=ALU.add, op1=ALU.mult))


def build(nc, io, out):
    ctx = ExitStack()
    with ctx:
        def sb(name, shape, dt=F32, c=ctx):
            return c.enter_context(nc.sbuf_tensor(name, shape, dt))

        def sem(name, c=ctx):
            return c.enter_context(nc.semaphore(name))

        x_nat = sb("x_nat", [P, NT, D])
        ident = sb("ident", [P, P])
        ln3 = sb("ln3", [P, NT, 2])
        raw = sb("raw", [P, 2, CT * D])
        O_T = sb("O_T", [P, CT, T])
        W_hi, W_lo = sb("W_hi", [P, 4, CT * D], F32R), sb("W_lo", [P, 4, CT * D], F32R)
        bv, bo = sb("bv", [P, CT]), sb("bo", [P, D])
        o_b = sb("o_b", [P, CT, P])
        o_first = [sb("o_first_hi", [P, CT, P], F32R), sb("o_first_lo", [P, CT, P], F32R)]
        w_in = [sem(f"w_in{i}") for i in range(2)]
        whi, wlo = sem("whi"), sem("wlo")
        cross_attention(nc, io, x_nat, ident, O_T, raw, W_hi, W_lo, bv, bo, o_b, o_first, w_in, whi, wlo)
        Wp_hi, Wp_lo = sb("Wp_hi", [P, CT * D], F32R), sb("Wp_lo", [P, CT * D], F32R)
        self_attention_and_experts(nc, io, out, x_nat, ident, O_T, raw, W_hi, W_lo, Wp_hi, Wp_lo, bv, bo, o_b, o_first,
                                   w_in, whi, wlo, ln3)


def three(eng, out, a_hi, a_lo, b_hi, b_lo, first, last):
    eng.matmul(out, a_hi, b_hi, start=first, stop=False)
    eng.matmul(out, a_lo, b_hi, start=False, stop=False)
    return eng.matmul(out, a_hi, b_lo, start=False, stop=last)


def cross_attention(nc, io, x_nat, ident, O_T, raw, W_hi, W_lo, bv, bo, o_b, o_first, w_in, whi, wlo):
    with ExitStack() as ctx:
        def sb(name, shape, dt=F32):
            return ctx.enter_context(nc.sbuf_tensor(name, shape, dt))

        def ps(name, shape):
            return ctx.enter_context(nc.psum_tensor(name, shape, F32))

        def sem(name):
            return ctx.enter_context(nc.semaphore(name))

        def halves(i):
            return [w[:, i, :].rearrange("p (c n) -> p c n", c=CT) for w in (W_hi, W_lo)]

        (c_hi0, c_lo0), (wk_hi, wk_lo), (c_hi1, c_lo1), (wv_hi, wv_lo) = (halves(i) for i in range(4))
        c_hi, c_lo = [c_hi0, c_hi1], [c_lo0, c_lo1]
        KW = SM + 2
        kf_hi, kf_lo = sb("kf_hi", [P, CT * 2 * KW], F32R), sb("kf_lo", [P, CT * 2 * KW], F32R)
        K_hi = kf_hi[:, :].rearrange("p (g j n) -> p g j n", g=CT, j=2)
        K_lo = kf_lo[:, :].rearrange("p (g j n) -> p g j n", g=CT, j=2)
        wq_hi = kf_hi[:, 0:CT * D].rearrange("p (c n) -> p c n", c=CT)
        wq_lo = kf_lo[:, 0:CT * D].rearrange("p (c n) -> p c n", c=CT)
        V = sb("V", [P, 4, D])
        m_flat, p_flat = sb("m_flat", [P, 2 * CT * SK]), sb("p_flat", [P, 2 * CT * SK])
        masked = m_flat[:, :].rearrange("p (j g n) -> p j g n", j=2, g=CT)
        probs = p_flat[:, :].rearrange("p (j g n) -> p j g n", j=2, g=CT)
        wv_raw = m_flat[:, 0:CT * D].rearrange("p (c n) -> p c n", c=CT)
        ctx0_raw = p_flat[:, 0:CT * D].rearrange("p (c n) -> p c n", c=CT)
        P_T = sb("P_T", [P, 2, 2, D])
        tail_nat = P_T[0:B, 0, :, :]
        Qd_hi = [sb(f"Qd_hi{j}", [P, CT, P], F32R) for j in range(2)]
        Qd_lo = [sb(f"Qd_lo{j}", [P, CT, P], F32R) for j in range(2)]
        Q_T = sb("Q_T", [P, CT, T])
        mask = sb("mask", [P, SK])
        bq, bk = sb("bq", [P, CT]), sb("bk", [P, CT])
        tail = sb("tail", [P, CT, B])
        t_hi, t_lo = sb("t_hi", [P, CT, B], F32R), sb("t_lo", [P, CT, B], F32R)
        kt32 = sb("kt32", [P, CT, B])
        kt_hi, kt_lo = sb("kt_hi", [P, CT, B], F32R), sb("kt_lo", [P, CT, B], F32R)
        vt = sb("vt", [P, CT, B])
        same_head = sb("same_head", [P, P])
        same_q = sb("same_q", [P, S])
        q_b_hi, q_b_lo = sb("q_b_hi", [P, CT, S], F32R), sb("q_b_lo", [P, CT, S])
        stats, mv = sb("stats", [P, NT, 6]), sb("mv", [P, NT, 2])
        var, rstd, tmp8 = sb("var", [P, NT]), sb("rstd", [P, NT]), sb("tmp8", [P, NT])
        z = sb("z", [P, 2, D])
        nmax, psum_, rinv = sb("nmax", [P, 2, CT]), sb("psum_", [P, 2, CT]), sb("rinv", [P, 2, CT])
        dtail = sb("dtail", [P, CT, S])
        otail = sb("otail", [P, 2, CT, S])

        pj = [ps(f"pj{i}", [P, D]) for i in range(2)]
        sc = [ps(f"sc{i}", [P, D]) for i in range(2)]
        tp = ps("tp", [P, 2, D])
        sc = sc + [tp[:, 0, :], tp[:, 1, :]]
        po = ps("po", [P, D])
        pb = ps("pb", [P, D])

        x_first, wq_lo_made = sem("x_first"), sem("wq_lo_made")
        x_in = [sem(f"x_in{i}") for i in range(2)]
        wq_in, wv_in, wk_in, bias_in, small_in = (sem(n) for n in ("wq_in", "wv_in", "wk_in", "bias_in", "small_in"))
        ctx_in = [sem(f"ctx_in{i}") for i in range(2)]
        const_made, z_made, zT_done, zT_hi, zT_lo = (sem(n) for n in ("const_made", "z_made", "zT_done", "zT_hi", "zT_lo"))
        w_hi, w_lo, q_done, q_out = (sem(n) for n in ("w_hi", "w_lo", "q_done", "q_out"))
        tail_done, tail_out, tailT_done, tailT_out = (sem(n) for n in ("tail_done", "tail_out", "tailT_done", "tailT_out"))
        bias_made, dve_step = sem("bias_made"), sem("dve_step")
        ctx_hi, ctx_lo, kv_done, k_hi, k_lo, v_out = (sem(n) for n in ("ctx_hi", "ctx_lo", "kv_done", "k_hi", "k_lo", "v_out"))
        k_tail, q_hi, q_lo, qd_made = (sem(n) for n in ("k_tail", "q_hi", "q_lo", "qd_made"))
        ident_made, heads_made = sem("ident_made"), sem("heads_made")
        s_done, masked_made, exp_done, rinv_made, probs_made = (sem(n) for n in ("s_done", "masked_made", "exp_done", "rinv_made", "probs_made"))
        dt_made, pb_done, ot_made, tr_done, pt_act, pt_dve, pv_done, o_out = (
            sem(n) for n in ("dt_made", "pb_done", "ot_made", "tr_done", "pt_act", "pt_dve", "pv_done", "o_out"))

        s_seen, q_hi_seen = sem("s_seen"), sem("q_hi_seen")
        first_made = sem("first_made")

        block = ctx.enter_context(nc.Block())

        @block.sync
        def _(eng):
            eng.dma_start(x_nat[:, 0:2, :], io["x"][:, 0:2, :]).then_inc(x_first, 16)
            eng.dma_start(x_nat[:, 2:4, :], io["x"][:, 2:4, :]).then_inc(x_in[0], 16)
            eng.dma_start(raw[:, 0, :], io["wq"]).then_inc(wq_in, 16)
            eng.dma_start(x_nat[:, 4:NT, :], io["x"][:, 4:NT, :]).then_inc(x_in[1], 16)
            eng.dma_start(bq[:, :], io["bq"]).then_inc(bias_in, 16)
            eng.dma_start(bk[:, :], io["bk"]).then_inc(bias_in, 16)
            eng.dma_start(raw[:, 1, :], io["wk"]).then_inc(wk_in, 16)
            eng.dma_start(p_flat[:, 0:CT * D], io["ctx"][0]).then_inc(ctx_in[0], 16)
            eng.dma_start(m_flat[:, 0:CT * D], io["wv"]).then_inc(wv_in, 16)
            eng.dma_start(tail[:, :, :], io["tail"]).then_inc(small_in, 16)
            eng.dma_start(bv[:, :], io["bv"]).then_inc(small_in, 16)
            eng.dma_start(bo[:, :], row_on_all(io["bo"])).then_inc(small_in, 16)
            for h in range(4):
                eng.dma_start(mask[h * S:(h + 1) * S, :], io["mask"]).then_inc(small_in, 16)
            eng.wait_ge(w_lo, 1)
            eng.dma_start(raw[:, 1, :], io["ctx"][1]).then_inc(ctx_in[1], 16)
            with eng.Fori(1, NT) as i:
                for p in range(2):
                    n = 2 * i + p
                    eng.wait_ge(ctx_lo, n - 1)
                    eng.dma_start(raw[:, p, :], io["ctx"][n]).then_inc(ctx_in[p], 16)
            for p in range(2):
                eng.wait_ge(ctx_lo, NPAIR - 1 + p)
                eng.dma_start(raw[:, p, :], io["w5"][p]).then_inc(w_in[p], 16)
            for p in range(2):
                eng.wait_ge(wlo, p + 1)
                eng.dma_start(raw[:, p, :], io["w5"][2 + p]).then_inc(w_in[p], 16)

        @block.gpsimd
        def _(eng):
            eng.memset(ident[:, :], 0.0).then_inc(const_made, 1)
            eng.wait_ge(const_made, 1)
            eng.affine_select(out=ident[:, :], in_=ident[:, :], compare_op=ALU.not_equal, fill=1.0,
                              base=0, pattern=[[-1, P]], channel_multiplier=1).then_inc(ident_made, 1)
            eng.wait_ge(w_hi, 1)
            eng.tensor_tensor(wq_lo, raw[:, 0, :].rearrange("p (c n) -> p c n", c=CT), wq_hi.bitcast(F32),
                              ALU.subtract).then_inc(wq_lo_made, 1)
            eng.wait_ge(heads_made, 9)
            eng.wait_ge(q_out, 8)

            def q_blocks(n, j):
                b = 2 * n + j
                cols = bass.ds(b * S, S)
                need(eng, qd_made, 2 * b)
                eng.tensor_copy(q_b_hi[:, :, :], Q_T[:, :, cols]).then_inc(q_hi, 1)
                eng.wait_ge(q_hi, b + 1)
                eng.sem_inc(q_hi_seen, 1)
                eng.tensor_tensor(q_b_lo[:, :, :], Q_T[:, :, cols], q_b_hi[:, :, :].bitcast(F32), ALU.subtract).then_inc(q_lo, 1)
                need(eng, s_done, 4 * (b - 1))
                eng.wait_ge(q_lo, b + 1)
                for Qd, q in ((Qd_hi, q_b_hi[:, :, :].bitcast(F32)), (Qd_lo, q_b_lo)):
                    eng.tensor_tensor(Qd[j][:, :, :].rearrange("p g (h s) -> p g h s", h=4),
                                      q[:, :, :].unsqueeze(2).broadcast_to([P, CT, 4, S]),
                                      same_head[:, :].rearrange("p (h s) -> p h s", h=4).unsqueeze(1).broadcast_to([P, CT, 4, S]),
                                      ALU.mult).then_inc(qd_made, 1)

            def pair(n):
                need(eng, s_done, 8 * n)
                first = isinstance(n, int) and n == 0
                if first:
                    q_blocks(n, 0)
                    q_blocks(n, 1)
                    eng.wait_ge(tailT_out, 5)
                for j in range(2):
                    for K, kt in ((K_hi, kt_hi), (K_lo, kt_lo)):
                        eng.tensor_copy(K[:, :, j, SM:KW],
                                        kt[:, :, bass.ds(2 * n + j, 1)].broadcast_to([P, CT, 2])).then_inc(k_tail, 1)
                if not first:
                    q_blocks(n, 0)
                    q_blocks(n, 1)

            pair(0)
            pair(1)
            with eng.Fori(1, NT) as i:
                pair(2 * i)
                pair(2 * i + 1)
            eng.wait_ge(small_in, 7 * 16)
            eng.wait_ge(o_out, 4 * 4)
            eng.tensor_tensor(o_b[:, :, :], O_T[:, :, 0:P], bv[:, :].unsqueeze(2).broadcast_to([P, CT, P]),
                              ALU.add).then_inc(first_made, 1)
            eng.wait_ge(first_made, 1)
            eng.tensor_copy(o_first[0][:, :, :], o_b[:, :, :]).then_inc(first_made, 1)
            eng.wait_ge(first_made, 2)
            eng.tensor_tensor(o_first[1][:, :, :], o_b[:, :, :], o_first[0][:, :, :].bitcast(F32),
                              ALU.subtract).then_inc(first_made, 1)
            eng.wait_ge(z_made, 1)
            eng.tensor_tensor(x_nat[:, 0, :], x_nat[:, 0, :], bo[:, :], ALU.add).then_inc(first_made, 1)

        @block.tensor
        def _(eng):
            def z_transposes(t):
                eng.wait_ge(z_made, t + 1)
                if t == 0:
                    eng.wait_ge(ident_made, 1)
                need(eng, zT_lo, t - 1)
                for c in range(CT):
                    mm = eng.transpose(tp[:, t % 2, c * P:(c + 1) * P], z[:, t % 2, c * P:(c + 1) * P], ident[:, :])
                mm.then_inc(zT_done, 1)

            def q_proj(hf, g):
                k = CT * hf + g
                if g == 0:
                    eng.wait_ge(zT_lo, 4 * (hf + 1))
                    eng.wait_ge(wq_lo_made, 1)
                need(eng, q_out, k - 1)
                for c in range(CT):
                    mm = three(eng, pj[k % 2][:, :], wq_hi[:, c, g * P:(g + 1) * P], wq_lo[:, c, g * P:(g + 1) * P],
                               c_hi[hf][:, c, :], c_lo[hf][:, c, :], c == 0, c == CT - 1)
                mm.then_inc(q_done, 1)

            def tails():
                eng.wait_ge(w_lo, 3)
                for i, (hi, lo) in enumerate(((wk_hi, wk_lo), (wv_hi, wv_lo))):
                    for c in range(CT):
                        mm = three(eng, sc[i][0:B, :], t_hi[:, c, :], t_lo[:, c, :], hi[:, c, :], lo[:, c, :],
                                   c == 0, c == CT - 1)
                    mm.then_inc(tail_done, 1)

            def tail_transposes():
                for i in range(2):
                    eng.wait_ge(tail_out, i + 1)
                    for g in range(CT):
                        mm = eng.transpose(pb[:, (i * CT + g) * B:(i * CT + g + 1) * B],
                                           tail_nat[:, i, g * P:(g + 1) * P], ident[0:B, 0:B])
                mm.then_inc(tailT_done, 1)

            for t in range(4):
                z_transposes(t)
            q_proj(0, 0)
            q_proj(0, 1)
            z_transposes(4)
            z_transposes(5)
            q_proj(0, 2)
            z_transposes(6)
            z_transposes(7)
            q_proj(0, 3)
            for g in range(CT):
                q_proj(1, g)

            def k_tile(n, p, g):
                if g == 0:
                    eng.wait_ge(ctx_lo, n + 1)
                if g < 2:
                    need(eng, v_out, 4 * n - 1 + g)
                    if isinstance(n, int) and n == 0:
                        eng.wait_ge(q_out, 7 + g)
                        eng.wait_ge(w_lo, 1)
                else:
                    eng.wait_ge(k_lo, 4 * n + g - 1)
                for c in range(CT):
                    mm = three(eng, pj[g % 2][:, :], wk_hi[:, c, g * P:(g + 1) * P], wk_lo[:, c, g * P:(g + 1) * P],
                               c_hi[p][:, c, :], c_lo[p][:, c, :], c == 0, c == CT - 1)
                mm.then_inc(kv_done, 1)

            def v_tile(n, p, t):
                if isinstance(n, int) and n == 0 and t == 0:
                    eng.wait_ge(w_lo, 2)
                if t < 2:
                    eng.wait_ge(k_lo, 4 * n + 3 + t)
                else:
                    eng.wait_ge(v_out, 4 * n + t - 1)
                for c in range(CT):
                    mm = three(eng, pj[t % 2][:, :], c_hi[p][:, c, t * P:(t + 1) * P], c_lo[p][:, c, t * P:(t + 1) * P],
                               wv_hi[:, c, :], wv_lo[:, c, :], c == 0, c == CT - 1)
                mm.then_inc(kv_done, 1)

            def scores(n, j):
                eng.wait_ge(k_lo, 4 * n + 4)
                eng.wait_ge(k_tail, 4 * n + 2 * j + 2)
                eng.wait_ge(qd_made, 2 * (2 * n + j + 1))
                for g in range(CT):
                    need(eng, masked_made, 8 * n + 4 * (j - 1) + g + 1)
                    if g == 2 and j == 0:
                        need(eng, pt_act, 2 * n)
                        need(eng, pt_dve, 2 * n)
                    three(eng, sc[g][:, 0:KW], Qd_hi[j][:, g, :], Qd_lo[j][:, g, :],
                          K_hi[:, g, j, :], K_lo[:, g, j, :], True, True).then_inc(s_done, 1)

            def transposes(n, j):
                b = 2 * n + j
                eng.wait_ge(probs_made, 4 * (b + 1))
                eng.wait_ge(masked_made, 8 * (n + 1))
                need(eng, pt_act, b)
                need(eng, pt_dve, b)
                for k in range(2):
                    for g in range(CT):
                        mm = eng.transpose(tp[:, k, g * P:(g + 1) * P], probs[:, j, g, k * P:(k + 1) * P], ident[:, :])
                mm.then_inc(tr_done, 1)
                eng.wait_ge(dt_made, b + 1)
                need(eng, ot_made, b)
                eng.matmul(pb[:, 0:P], same_head[:, :], dtail[:, :, :].rearrange("p g s -> p (g s)"),
                           start=True, stop=True).then_inc(pb_done, 1)

            def weighted_sum(n, j):
                b = 2 * n + j
                eng.wait_ge(pt_act, b + 1)
                eng.wait_ge(pt_dve, b + 1)
                eng.wait_ge(v_out, 4 * (n + 1))
                need(eng, o_out, 4 * b)
                for g in range(CT):
                    for k in range(2):
                        mm = eng.matmul(po[:, g * P:(g + 1) * P], V[:, 2 * j + k, g * P:(g + 1) * P],
                                        P_T[:, j, k, g * P:(g + 1) * P], start=k == 0, stop=k == 1)
                mm.then_inc(pv_done, 1)

            def pair(n, p, first):
                k_tile(n, p, 0)
                if not first:
                    transposes(n - 1, 1)
                k_tile(n, p, 1)
                if not first:
                    weighted_sum(n - 1, 0)
                else:
                    tails()
                k_tile(n, p, 2)
                if not first:
                    weighted_sum(n - 1, 1)
                else:
                    tail_transposes()
                k_tile(n, p, 3)
                v_tile(n, p, 0)
                scores(n, 0)
                v_tile(n, p, 1)
                scores(n, 1)
                v_tile(n, p, 2)
                transposes(n, 0)
                v_tile(n, p, 3)

            pair(0, 0, True)
            pair(1, 1, False)
            with eng.Fori(1, NT) as i:
                pair(2 * i, 0, False)
                pair(2 * i + 1, 1, False)
            transposes(NPAIR - 1, 1)
            weighted_sum(NPAIR - 1, 0)
            weighted_sum(NPAIR - 1, 1)

        @block.scalar
        def _(eng):
            def split_hi(dst, src):
                return eng.activation(dst, src, ACT.Copy)

            eng.wait_ge(wq_in, 16)
            split_hi(wq_hi, raw[:, 0, :].rearrange("p (c n) -> p c n", c=CT)).then_inc(w_hi, 1)

            def z_hi(t):
                eng.wait_ge(zT_done, t + 1)
                split_hi(c_hi[t // 4][:, :, t % 4 * P:(t % 4 + 1) * P],
                         tp[:, t % 2, :].rearrange("p (c n) -> p c n", c=CT)).then_inc(zT_hi, 1)

            def q_evac(k):
                eng.wait_ge(q_done, k + 1)
                if k == 0:
                    eng.wait_ge(bias_made, 1)
                eng.activation(Q_T[:, k % CT, k // CT * D:(k // CT + 1) * D], pj[k % 2][:, :], ACT.Identity,
                               bias=bq[:, k % CT:k % CT + 1], scale=SCALE).then_inc(q_out, 1)

            def tail_evac():
                for i in range(2):
                    eng.wait_ge(tail_done, i + 1)
                    eng.activation(tail_nat[:, i, :], sc[i][0:B, :], ACT.Copy).then_inc(tail_out, 1)

            def tail_keys():
                eng.wait_ge(tailT_out, 1)
                split_hi(kt_hi[:, :, :], kt32[:, :, :]).then_inc(tailT_out, 1)

            def ctx_split(n, p, i):
                eng.wait_ge(ctx_in[p], 16 * (i + 1))
                need(eng, kv_done, 8 * (n - 1))
                if isinstance(n, int) and n < 2:
                    eng.wait_ge(q_done, 4 * (n + 1))
                src = ctx0_raw if isinstance(n, int) and n == 0 else raw[:, p, :].rearrange("p (c n) -> p c n", c=CT)
                split_hi(c_hi[p][:, :, :], src).then_inc(ctx_hi, 1)

            def weight_split(i, used):
                eng.wait_ge(w_in[i], 16)
                eng.wait_ge(kv_done, used)
                split_hi(W_hi[:, i, :], raw[:, i, :]).then_inc(whi, 1)

            def k_evac(n, g):
                eng.wait_ge(kv_done, 8 * n + g + 1)
                if g == 0:
                    need(eng, s_done, 8 * n)
                eng.activation(K_hi[:, g, :, 0:SM], pj[g % 2][:, :].rearrange("p (j n) -> p j n", j=2),
                               ACT.Identity, bias=bk[:, g:g + 1]).then_inc(k_hi, 1)

            def v_evac(n, t):
                eng.wait_ge(kv_done, 8 * n + 5 + t)
                if t == 0:
                    need(eng, pv_done, 2 * n)
                eng.activation(V[:, t, :], pj[t % 2][:, :], ACT.Copy).then_inc(v_out, 1)

            def exps(n, j):
                b = 2 * n + j
                need(eng, tr_done, b - 1)
                need(eng, dt_made, b - 1)
                for g in range(CT):
                    eng.wait_ge(masked_made, 4 * b + g + 1)
                    eng.activation(probs[:, j, g, :], masked[:, j, g, :], ACT.Exp, bias=nmax[:, j, g:g + 1],
                                   scale=-1.0, accum_out=psum_[:, j, g:g + 1]).then_inc(exp_done, 1)

            def pt_evac(n, j):
                b = 2 * n + j
                eng.wait_ge(tr_done, b + 1)
                need(eng, pv_done, b - 1)
                eng.activation(P_T[:, j, 0, :], tp[:, 0, :], ACT.Copy).then_inc(pt_act, 1)

            def pair(n, p, i, first, last):
                k_evac(n, 0)
                if not first:
                    pt_evac(n - 1, 1)
                k_evac(n, 1)
                if first:
                    tail_evac()
                if not last:
                    ctx_split(n + 1, 1 - p, i + p)
                else:
                    weight_split(0, 8 * (NPAIR - 1))
                k_evac(n, 2)
                if first:
                    tail_keys()
                k_evac(n, 3)
                v_evac(n, 0)
                exps(n, 0)
                v_evac(n, 1)
                exps(n, 1)
                v_evac(n, 2)
                if last:
                    weight_split(1, 8 * (NPAIR - 1) + 4)
                pt_evac(n, 0)
                v_evac(n, 3)

            for t in range(4):
                z_hi(t)
            eng.wait_ge(wk_in, 16)
            split_hi(wk_hi[:, :, :], raw[:, 1, :].rearrange("p (c n) -> p c n", c=CT)).then_inc(w_hi, 1)
            q_evac(0)
            q_evac(1)
            z_hi(4)
            z_hi(5)
            q_evac(2)
            z_hi(6)
            z_hi(7)
            q_evac(3)
            ctx_split(0, 0, 0)
            q_evac(4)
            eng.wait_ge(wv_in, 16)
            split_hi(wv_hi[:, :, :], wv_raw).then_inc(w_hi, 1)
            q_evac(5)
            eng.wait_ge(small_in, 7 * 16)
            split_hi(t_hi[:, :, :], tail[:, :, :]).then_inc(w_hi, 1)
            q_evac(6)
            q_evac(7)
            pair(0, 0, 0, True, False)
            pair(1, 1, 0, False, False)
            with eng.Fori(1, NT - 1) as i:
                pair(2 * i, 0, i, False, False)
                pair(2 * i + 1, 1, i, False, False)
            pair(NPAIR - 2, 0, NT - 1, False, False)
            pair(NPAIR - 1, 1, NT - 1, False, True)
            pt_evac(NPAIR - 1, 1)

        @block.vector
        def _(eng):
            ch = Chain(eng, dve_step)

            def split_lo(dst, src, hi):
                return eng.tensor_tensor(dst, src, hi.bitcast(F32), ALU.subtract)

            eng.memset(same_head[:, :], 0.0).then_inc(heads_made, 1)
            eng.wait_ge(heads_made, 1)
            eng.wait_ge(ident_made, 1)
            for h in range(4):
                r = slice(h * S, (h + 1) * S)
                eng.memset(same_head[r, r], 1.0).then_inc(heads_made, 1)
                eng.tensor_copy(same_q[r, :], ident[r, r]).then_inc(heads_made, 1)

            def layer_norm_stats(hf):
                eng.wait_ge(x_first if hf == 0 else x_in[1], 16)
                ts = slice(4 * hf, 4 * hf + 4)
                for t in range(4 * hf, 4 * hf + 4):
                    if t == 2:
                        eng.wait_ge(x_in[0], 16)
                    eng.bn_stats(stats[:, t, :], x_nat[:, t, :]).then_inc(dve_step, 1)
                    ch.k += 1
                first = ch.k - 4
                for t in range(4):
                    eng.wait_ge(dve_step, first + t + 1)
                    eng.bn_aggr(mv[:, 4 * hf + t, :], stats[:, 4 * hf + t, :]).then_inc(dve_step, 1)
                    ch.k += 1
                eng.wait_ge(dve_step, ch.k)
                ch.link(eng.tensor_scalar(var[:, ts], mv[:, ts, 1], LN_EPS, None, ALU.add))
                rsqrt(eng, ch, rstd[:, ts], var[:, ts], tmp8[:, ts])

            def z_make(t):
                need(eng, zT_done, t - 1)
                eng.tensor_scalar(z[:, t % 2, :], x_nat[:, t, :], mv[:, t, 0:1], rstd[:, t:t + 1],
                                  ALU.subtract, ALU.mult).then_inc(z_made, 1)

            def z_lo(t):
                eng.wait_ge(zT_hi, t + 1)
                cols = slice(t % 4 * P, (t % 4 + 1) * P)
                split_lo(c_lo[t // 4][:, :, cols], tp[:, t % 2, :].rearrange("p (c n) -> p c n", c=CT),
                         c_hi[t // 4][:, :, cols]).then_inc(zT_lo, 1)

            layer_norm_stats(0)
            z_make(0)
            z_make(1)
            for t in range(4):
                z_lo(t)
                if t < 2:
                    z_make(t + 2)
            eng.wait_ge(bias_in, 2 * 16)
            eng.tensor_scalar(bq[:, :], bq[:, :], SCALE, None, ALU.mult).then_inc(bias_made, 1)
            layer_norm_stats(1)
            z_make(4)
            z_make(5)
            for t in range(4, NT):
                z_lo(t)
                if t < 6:
                    z_make(t + 2)
            eng.wait_ge(w_hi, 2)
            split_lo(wk_lo[:, :, :], raw[:, 1, :].rearrange("p (c n) -> p c n", c=CT), wk_hi[:, :, :]).then_inc(w_lo, 1)

            def tail_keys():
                eng.wait_ge(tailT_done, 1)
                tails_T = pb[:, 0:2 * CT * B].rearrange("p (i g b) -> p i g b", i=2, g=CT)
                eng.tensor_tensor(kt32[:, :, :], tails_T[:, 0], bk[:, :].unsqueeze(2).broadcast_to([P, CT, B]),
                                  ALU.add).then_inc(tailT_out, 1)
                eng.wait_ge(tailT_out, 2)
                split_lo(kt_lo[:, :, :], kt32[:, :, :], kt_hi[:, :, :]).then_inc(tailT_out, 2)
                eng.tensor_copy(vt[:, :, :], tails_T[:, 1]).then_inc(tailT_out, 1)

            def ctx_split(n, p):
                eng.wait_ge(ctx_hi, n + 1)
                src = ctx0_raw if isinstance(n, int) and n == 0 else raw[:, p, :].rearrange("p (c n) -> p c n", c=CT)
                split_lo(c_lo[p][:, :, :], src, c_hi[p][:, :, :]).then_inc(ctx_lo, 1)

            def weight_split(i):
                eng.wait_ge(whi, i + 1)
                split_lo(W_lo[:, i, :], raw[:, i, :], W_hi[:, i, :]).then_inc(wlo, 1)

            def k_evac(n, g):
                eng.wait_ge(k_hi, 4 * n + g + 1)
                eng.scalar_tensor_tensor(out=K_lo[:, g, :, 0:SM], in0=pj[g % 2][:, :].rearrange("p (j n) -> p j n", j=2),
                                         scalar=bk[:, g:g + 1], in1=K_hi[:, g, :, 0:SM].bitcast(F32),
                                         op0=ALU.add, op1=ALU.subtract).then_inc(k_lo, 1)

            def mask_max(n, j):
                b = 2 * n + j
                need(eng, exp_done, 4 * (b - 1))
                for g in range(CT):
                    eng.wait_ge(s_done, 4 * b + g + 1)
                    eng.sem_inc(s_seen, 1)
                    eng.tensor_tensor_reduce(masked[:, j, g, :], sc[g][:, 0:SK], mask[:, :], -1.0, BIG,
                                             ALU.add, ALU.min, nmax[:, j, g:g + 1]).then_inc(masked_made, 1)

            def normalise(n, j):
                b = 2 * n + j
                eng.wait_ge(exp_done, 4 * (b + 1))
                eng.reciprocal(rinv[:, j, :], psum_[:, j, :]).then_inc(rinv_made, 1)
                eng.wait_ge(rinv_made, b + 1)
                for g in range(CT):
                    eng.tensor_scalar(probs[:, j, g, :], probs[:, j, g, :], rinv[:, j, g:g + 1], None,
                                      ALU.mult).then_inc(probs_made, 1)
                eng.wait_ge(probs_made, 4 * (b + 1))
                need(eng, pb_done, b)
                eng.tensor_tensor(dtail[:, :, :], same_q[:, :].unsqueeze(1).broadcast_to([P, CT, S]),
                                  probs[:, j, :, SM:SK].broadcast_to([P, CT, S]), ALU.mult).then_inc(dt_made, 1)

            def pt_evac(n, j):
                b = 2 * n + j
                eng.wait_ge(tr_done, b + 1)
                need(eng, pv_done, b - 1)
                eng.tensor_copy(P_T[:, j, 1, :], tp[:, 1, :]).then_inc(pt_dve, 1)
                eng.wait_ge(pb_done, b + 1)
                need(eng, o_out, 4 * (b - 1))
                eng.tensor_tensor(otail[:, j, :, :], pb[:, 0:P].rearrange("p (g s) -> p g s", g=CT),
                                  vt[:, :, bass.ds(b, 1)].broadcast_to([P, CT, S]), ALU.mult).then_inc(ot_made, 1)

            def o_evac(n, j):
                b = 2 * n + j
                eng.wait_ge(pv_done, b + 1)
                eng.wait_ge(ot_made, b + 1)
                for h in range(4):
                    r = slice(h * S, (h + 1) * S)
                    eng.tensor_tensor(O_T[r, :, bass.ds(b * S, S)], po[r, :].rearrange("p (g n) -> p g n", g=CT)[:, :, r],
                                      otail[r, j, :, :], ALU.add).then_inc(o_out, 1)

            def pair(n, p, first, last):
                k_evac(n, 0)
                if not first:
                    pt_evac(n - 1, 1)
                k_evac(n, 1)
                if not first:
                    o_evac(n - 1, 0)
                if not last:
                    ctx_split(n + 1, 1 - p)
                else:
                    weight_split(0)
                k_evac(n, 2)
                if not first:
                    o_evac(n - 1, 1)
                else:
                    tail_keys()
                k_evac(n, 3)
                mask_max(n, 0)
                mask_max(n, 1)
                normalise(n, 0)
                pt_evac(n, 0)
                normalise(n, 1)
                if last:
                    weight_split(1)

            ctx_split(0, 0)
            eng.wait_ge(w_hi, 3)
            split_lo(wv_lo[:, :, :], wv_raw, wv_hi[:, :, :]).then_inc(w_lo, 1)
            eng.wait_ge(w_hi, 4)
            eng.wait_ge(small_in, 7 * 16)
            split_lo(t_lo[:, :, :], tail[:, :, :], t_hi[:, :, :]).then_inc(w_lo, 1)
            pair(0, 0, True, False)
            pair(1, 1, False, False)
            with eng.Fori(1, NT - 1) as i:
                pair(2 * i, 0, False, False)
                pair(2 * i + 1, 1, False, False)
            pair(NPAIR - 2, 0, False, False)
            pair(NPAIR - 1, 1, False, True)
            pt_evac(NPAIR - 1, 1)
            o_evac(NPAIR - 1, 0)
            o_evac(NPAIR - 1, 1)


def row_on_all(v):
    return v.unsqueeze(0).broadcast_to([P, v.shape[0]])


HT, NH = T // 2, NT // 2
EC = 3


def self_attention_and_experts(nc, io, out, x_nat, ident, O_T, raw, W_hi, W_lo, Wp_hi, Wp_lo, bv, bo, o_b, o_first, w_in, whi, wlo, ln3):
    with ExitStack() as ctx:
        def sb(name, shape, dt=F32):
            return ctx.enter_context(nc.sbuf_tensor(name, shape, dt))

        def ps(name, shape):
            return ctx.enter_context(nc.psum_tensor(name, shape, F32))

        def sem(name):
            return ctx.enter_context(nc.semaphore(name))

        w_hi, w_lo = ([w.rearrange("p (c n) -> p c n", c=CT) for w in (*(W[:, i, :] for i in range(4)), Wp[:, :])]
                      for W, Wp in ((W_hi, Wp_hi), (W_lo, Wp_lo)))
        bqkv, bproj = sb("bqkv", [P, 3, D]), sb("bproj", [P, D])
        qk_w = sb("qk_w", [P, 2])
        o_hi, o_lo = sb("o_hi", [P, CT, P], F32R), sb("o_lo", [P, CT, P], F32R)
        stats, mv = sb("stats2", [P, 2, 6]), sb("mv2", [P, 2, 2])
        rstd, tmp = sb("rstd2", [P, 2]), sb("tmp2", [P, 2])
        mixed = sb("mixed", [P, CT, P])
        z2, z3s = sb("z2", [P, D]), sb("z3s", [P, D])
        z2_hi, z2_lo = sb("z2_hi", [P, CT, P], F32R), sb("z2_lo", [P, CT, P], F32R)
        qk, v, v_raw = sb("qk", [P, 2, D]), sb("v", [P, D]), sb("v_raw", [P, D])
        sq = sb("sq", [P, 2 * D])
        ms, rms, tmp32 = (sb(n, [P, 2 * H + 1]) for n in ("ms", "rms", "tmp32"))
        q_T, k_T = sb("q_T", [P, CT, P]), sb("k_T", [P, CT, P])
        mx, sm, rs = sb("mx", [P, H]), sb("sm", [P, H]), sb("rs", [P, H])
        e = sb("e", [P, H * S])
        e_T = sb("e_T", [P, H * S])
        o2_hi, o2_lo = sb("o2_hi", [P, CT, P], F32R), sb("o2_lo", [P, CT, P], F32R)

        pw = [ps(f"pw{i}", [P, D]) for i in range(2)]
        pt = [ps(f"pt{i}", [P, D]) for i in range(2)]
        pa = ps("pa", [P, 4, D])

        small_in, scaled, wp_lo, vr_out = sem("small_in2"), sem("scaled"), sem("wp_lo"), sem("vr_out")
        dve_seen, pe_seen = sem("dve_seen"), sem("pe_seen")
        ob_made, ohi_made, olo_made, pool_seen = sem("ob_made"), sem("ohi_made"), sem("olo_made"), sem("pool_seen")
        wo_done, x1_made, z2_made, x1b_made, z2T_done, z2hi_made, z2lo_made = (
            sem(n) for n in ("wo_done", "x1_made", "z2_made", "x1b_made", "z2T_done", "z2hi_made", "z2lo_made"))
        qkv_done, qk_out, v_out, sq_made, qkn_made, x0_made, qkT_done, qT_out, kT_out = (
            sem(n) for n in ("qkv_done", "qk_out", "v_out2", "sq_made", "qkn_made", "x0_made", "qkT_done", "qT_out", "kT_out"))
        s_done, shifted, e_made, eT_made, pv_done, o2hi_made, o2lo_made = (
            sem(n) for n in ("s_done2", "shifted", "e_made", "eT_made", "pv_done2", "o2hi_made", "o2lo_made"))
        proj_done, x2_made, z3_made, z3T_done, z3T_out, step = (
            sem(n) for n in ("proj_done", "x2_made", "z3_made", "z3T_done", "z3T_out", "step2"))


        BF = mybir.dt.bfloat16
        RING = 3
        g_hi, g_lo = sb("g_hi", [P, CT, DM], F32R), sb("g_lo", [P, CT, DM], F32R)
        wo2, b1, bo1, bo2 = sb("wo2", [P, E]), sb("b1", [P, E]), sb("bo1", [P, 1]), sb("bo2", [P, E])
        mixw = sb("mixw", [P, 3, CT])
        xm_hi, xm_lo = sb("xm_hi", [P, CT, HT], F32R), sb("xm_lo", [P, CT, HT], F32R)
        rank = sb("rank", [P, E])
        gs, key, top = sb("gs", [P, NH, E]), sb("key", [P, NH, E]), sb("top", [P, NH])
        choice = sb("choice", [P, NH, E])
        choice_b = sb("choice_b", [E, HT], BF)
        sel = sb("sel", [E, E, P], BF)
        stats4, mv4 = sb("stats4", [P, NH, 6]), sb("mv4", [P, NH, 2])
        rstd4, tmp4 = sb("rstd4", [P, NH]), sb("tmp4", [P, NH])
        h_hi, h_lo = ([t[:, :, :].rearrange("p c n -> p (c n)") for t in ts]
                      for ts in ((o_hi, o_first[0], z2_hi), (o_lo, o_first[1], z2_lo)))
        h = [z2[:, :], bqkv[:, 0, :]]
        th = bqkv[:, 1, :]
        chosen = [sq[:, 0:D], sq[:, D:2 * D]]
        b2_hi, b2_lo = (W[0:E, EC * D:EC * D + D] for W in (Wp_hi, Wp_lo))
        choice_T = W_hi[0:E, 3, EC * D:EC * D + D]
        gamma, beta = bproj[:, :], bo[:, :]
        g_raw = raw[:, 0, EC * D:].rearrange("p (c n) -> p c n", c=CT)
        b2 = raw[0:E, 1, EC * D:]

        def y(t):
            return raw[:, t // NH, t % NH * D:(t % NH + 1) * D]

        def y_pair(hf):
            return raw[:, hf, :].rearrange("p (t n) -> p t n", t=NH)

        def split_parts(i):
            src, n = raw[:, i % 2, 0:EC * D], EC * D
            if i % 2 == 0:
                return (src, *(W[:, i // 2, 0:n] for W in (W_hi, W_lo)))
            if i == 1:
                return (src, *(W[:, 3, 0:n] for W in (W_hi, W_lo)))
            if i == 3:
                return (src, *(W[:, 0:n] for W in (Wp_hi, Wp_lo)))
            return (src.rearrange("p (a n) -> p a n", a=EC), *(W[:, 0:EC, n:n + D] for W in (W_hi, W_lo)))

        def w1(half, e, c):
            at = c * EC * DM + e % EC * DM
            return (W_hi, W_lo)[half][:, e // EC, at:at + DM]

        def w2(half, e):
            if e < EC:
                return (W_hi, W_lo)[half][:, 3, e * D:(e + 1) * D]
            if e < 2 * EC:
                return (Wp_hi, Wp_lo)[half][:, (e - EC) * D:(e - EC + 1) * D]
            return (W_hi, W_lo)[half][:, e - 2 * EC, EC * D:EC * D + D]

        def ph(k):
            return pt[k % 2]

        def z3_bank(it):
            return pw[1] if isinstance(it, int) and it > NT else pt[1]

        pc = pw[0]
        pg = [pw[0], pw[1]]

        stats_made, centred = sem("stats_made"), sem("centred")
        ex_in, exw_in, ln_in, stored = sem("ex_in"), sem("exw_in"), sem("ln_in"), sem("stored")
        (w_hi_made, w_lo_made, g_split, mixes, mix_made, xmhi, xmlo, g_done, th_made, gs_done, choice_made, cT_done, cT_out,
         cb_out, consts, b2_split, pc_done, pc_out, h_done, h_made, hhi, hlo, h_used, y_done, y_made, xb_made, zn_made, fin,
         step3) = (
            sem("x_" + n) for n in (
                "w_hi_made w_lo_made g_split mixes mix_made xmhi xmlo g_done th_made gs_done choice_made cT_done cT_out "
                "cb_out consts b2_split pc_done pc_out h_done h_made hhi hlo h_used y_done y_made xb_made zn_made fin "
                "step3").split())

        def steps(eng, body):
            for it in range(3):
                body(it)
            with eng.Fori(3, NT) as i:
                body(i)

        def wo_bank(it):
            return pw[1] if isinstance(it, int) and it == 1 else pw[0]

        def k_bank(it):
            return pt[1] if isinstance(it, int) and it == 1 else pw[0]

        def has(it, lag):
            return not isinstance(it, int) or 0 <= it - lag < NT

        block = ctx.enter_context(nc.Block())

        @block.sync
        def _(eng):
            eng.dma_start(qk_w[:, :], io["qk_w"]).then_inc(small_in, 16)
            eng.dma_start(mixw[:, :, :].rearrange("p a c -> p (a c)"), io["mixw"]).then_inc(small_in, 16)
            for name, dst in (("bqkv", bqkv[:, :, :].rearrange("p a n -> p (a n)")), ("bproj", bproj[:, :])):
                eng.dma_start(dst, row_on_all(io[name])).then_inc(small_in, 16)
            eng.wait_ge(wlo, 3)
            eng.dma_start(raw[:, 0, :], io["w5"][4]).then_inc(w_in[0], 16)
            eng.wait_ge(wlo, 4)
            eng.wait_ge(wp_lo, 1)
            eng.dma_start(g_raw, io["wo1"].rearrange("p (c n) -> p c n", c=CT)).then_inc(ex_in, 16)
            for name, dst in (("wo2", wo2[:, :]), ("b1", b1[:, :]), ("bo1", bo1[:, :]), ("b2", b2)):
                eng.dma_start(dst, io[name]).then_inc(ex_in, 16)
            eng.dma_start(bo2[:, :], row_on_all(io["bo2"])).then_inc(ex_in, 16)
            for i in range(6):
                need(eng, w_lo_made, i - 1)
                eng.dma_start(raw[:, i % 2, 0:EC * D], io["w1" if i % 2 == 0 else "w2"][i // 2]).then_inc(exw_in, 16)
                eng.wait_ge(exw_in, 16 * (i + 1))
                if i == 1:
                    eng.wait_ge(x1b_made, NT)
                    eng.dma_start(gamma, row_on_all(io["gamma"])).then_inc(ln_in, 16)
                    eng.dma_start(beta, row_on_all(io["beta"])).then_inc(ln_in, 16)
            for i, t in enumerate((0, 1, 2, 3, 6, 7, 4, 5)):
                eng.wait_ge(fin, i + 1)
                eng.dma_start(out[t], y(t)).then_inc(stored, 16)
            eng.wait_ge(stored, 16 * NT)

        @block.gpsimd
        def _(eng):
            def o_split(t):
                need(eng, olo_made, t - 1)
                eng.tensor_tensor(o_b[:, :, :], O_T[:, :, bass.ds(t * P, P)], bv[:, :].unsqueeze(2).broadcast_to([P, CT, P]),
                                  ALU.add).then_inc(ob_made, 1)
                eng.wait_ge(ob_made, t)
                if not (isinstance(t, int) and t == 1):
                    eng.wait_ge(wo_done, t)
                eng.sem_inc(pool_seen, 1)
                eng.tensor_copy(o_hi[:, :, :], o_b[:, :, :]).then_inc(ohi_made, 1)
                eng.wait_ge(ohi_made, t)
                eng.tensor_tensor(o_lo[:, :, :], o_b[:, :, :], o_hi[:, :, :].bitcast(F32), ALU.subtract).then_inc(olo_made, 1)

            def with_bo(t):
                x_t = x_nat[:, bass.ds(t, 1), :]
                eng.tensor_tensor(x_t, x_t, bo[:, :].unsqueeze(1), ALU.add).then_inc(x0_made, 1)

            def with_bproj(t):
                x_t = x_nat[:, bass.ds(t, 1), :]
                eng.wait_ge(z2_made, t + 1)
                eng.sem_inc(pool_seen, 1)
                eng.tensor_tensor(x_t, x_t, bproj[:, :].unsqueeze(1), ALU.add).then_inc(x1b_made, 1)

            def v_bias(u):
                eng.wait_ge(vr_out, u + 1)
                need(eng, pv_done, u)
                eng.sem_inc(pool_seen, 1)
                eng.tensor_tensor(v[:, :], v_raw[:, :], bqkv[:, 2, :], ALU.add).then_inc(v_out, 1)

            def mix(u):
                z = O_T[:, :, bass.ds(u * P, P)].rearrange("p c (b s) -> p c b s", s=S)
                part, xm = (t[:, :, :].rearrange("p c (b s) -> p c b s", s=S) for t in (o_b, mixed))
                left, right = slice(0, S - 1), slice(1, S)

                def k(a, n):
                    return mixw[:, a, :].unsqueeze(2).unsqueeze(3).broadcast_to([P, CT, 4, n])

                def linked(i, *args):
                    eng.tensor_tensor(*args).then_inc(mixes, 1)
                    eng.wait_ge(mixes, 5 * u + i)
                    eng.sem_inc(pool_seen, 1)

                eng.wait_ge(z3T_out, u + 2)
                eng.sem_inc(pool_seen, 1)
                linked(1, xm, z, k(1, S), ALU.mult)
                linked(2, part[:, :, :, right], z[:, :, :, left], k(0, S - 1), ALU.mult)
                linked(3, xm[:, :, :, right], xm[:, :, :, right], part[:, :, :, right], ALU.add)
                linked(4, part[:, :, :, left], z[:, :, :, right], k(2, S - 1), ALU.mult)
                linked(5, z[:, :, :, left], xm[:, :, :, left], part[:, :, :, left], ALU.add)
                eng.tensor_copy(z[:, :, :, S - 1:S], xm[:, :, :, S - 1:S]).then_inc(mix_made, 1)
                eng.wait_ge(mix_made, u + 1)
                eng.sem_inc(pool_seen, 1)

            o_split(1)
            eng.wait_ge(small_in, 4 * 16)
            with_bproj(0)
            with_bo(1)
            o_split(2)
            with_bproj(1)
            v_bias(0)
            with_bo(2)
            eng.wait_ge(whi, 5)
            eng.tensor_tensor(w_lo[4], raw[:, 0, :].rearrange("p (c n) -> p c n", c=CT), w_hi[4].bitcast(F32),
                              ALU.subtract).then_inc(wp_lo, 1)
            with_bproj(2)
            o_split(3)
            v_bias(1)
            with_bo(3)
            with_bproj(3)
            with eng.Fori(4, NT) as t:
                o_split(t)
                v_bias(t - 2)
                with_bo(t)
                mix(t - 4)
                with_bproj(t)

            v_bias(NT - 2)
            eng.wait_ge(xmhi, 1)
            eng.tensor_tensor(xm_lo[:, :, :], O_T[:, :, 0:HT], xm_hi[:, :, :].bitcast(F32), ALU.subtract).then_inc(xmlo, 1)
            eng.wait_ge(g_split, 1)
            eng.tensor_tensor(g_lo[:, :, :], g_raw, g_hi[:, :, :].bitcast(F32), ALU.subtract).then_inc(g_split, 1)
            v_bias(NT - 1)
            for u in range(4, NT):
                mix(u)
            eng.wait_ge(ln_in, 2 * 16)
            eng.wait_ge(b2_split, 2)
            for t in range(NT):
                eng.wait_ge(w_lo_made, 5 if t < NH else 6)
                eng.tensor_scalar(y(t), x_nat[:, t, :], ln3[:, t, 0:1], ln3[:, t, 1:2],
                                  ALU.subtract, ALU.mult).then_inc(zn_made, 1)
                eng.wait_ge(zn_made, t + 1)
                eng.tensor_tensor(x_nat[:, t, :], x_nat[:, t, :], beta, ALU.add).then_inc(xb_made, 1)
            for t in range(2):
                y_t = y(NH + t)
                eng.wait_ge(stats_made, NH + t + 1)
                eng.tensor_scalar(y_t, y_t, mv4[:, t, 0:1], None, ALU.subtract).then_inc(centred, 1)
                eng.wait_ge(centred, 2 * t + 1)
                eng.tensor_tensor(y_t, y_t, gamma, ALU.mult).then_inc(centred, 1)

        @block.tensor
        def _(eng):
            def project(out, hi, lo, i):
                for c in range(CT):
                    mm = three(eng, out, hi[:, c, :], lo[:, c, :], w_hi[i][:, c, :], w_lo[i][:, c, :], c == 0, c == CT - 1)
                return mm

            def z2_transposes(t):
                eng.wait_ge(z2_made, t + 1)
                need(eng, qT_out, t - 1)
                if not has(t, 2):
                    need(eng, z2lo_made, t)
                for c in range(CT):
                    mm = eng.transpose(pt[0][:, c * P:(c + 1) * P], z2[:, c * P:(c + 1) * P], ident[:, :])
                mm.then_inc(z2T_done, 1)

            eng.sem_inc(z3T_done, 1)

            def wo_proj(it):
                if isinstance(it, int) and it == 0:
                    eng.wait_ge(wlo, 1)
                need(eng, olo_made, it)
                if has(it, 2):
                    eng.wait_ge(qk_out, 2 * (it - 1))
                halves = o_first if isinstance(it, int) and it == 0 else (o_hi, o_lo)
                project(wo_bank(it)[:, :], *halves, 0).then_inc(wo_done, 1)

            def out_proj(it):
                u = it - 3
                eng.wait_ge(o2lo_made, u + 1)
                if has(it, 2):
                    eng.wait_ge(vr_out, u + 2)
                else:
                    eng.wait_ge(x2_made, u)
                project(pw[1][:, :], o2_hi, o2_lo, 4).then_inc(proj_done, 1)

            def qk_transposes(it):
                u = it - 2
                eng.wait_ge(qkn_made, u + 1)
                need(eng, z2lo_made, u + 2 if has(it, 1) else u + 1)
                for i in range(2):
                    if i == 1:
                        need(eng, z3T_out, u)
                    for g in range(CT):
                        mm = eng.transpose(pt[i][:, g * P:(g + 1) * P], qk[:, i, g * P:(g + 1) * P], ident[:, :])
                    mm.then_inc(qkT_done, 1)

            def qkv(it, i):
                u = it - 1
                if isinstance(it, int) and it == 1:
                    eng.wait_ge(wlo, i + 2)
                if isinstance(it, int) and it == 2 and i == 2:
                    eng.wait_ge(wp_lo, 1)
                if i == 0:
                    eng.wait_ge(z2lo_made, u + 1)
                    if isinstance(it, int) and it == 1:
                        eng.wait_ge(x1_made, 1)
                    elif has(it, 0):
                        eng.wait_ge(x1_made, it + 1)
                    else:
                        eng.wait_ge(qk_out, 2 * u)
                elif i == 1:
                    if not (isinstance(it, int) and it == 1):
                        eng.wait_ge(qk_out, 2 * u + 1)
                elif has(it, 3):
                    eng.wait_ge(x2_made, it - 2)
                else:
                    need(eng, vr_out, u)
                    if isinstance(it, int) and it == 1:
                        eng.wait_ge(x1_made, 2)
                bank = (pw[0], k_bank(it), pw[1])[i]
                project(bank[:, :], z2_hi, z2_lo, i + 1).then_inc(qkv_done, 1)

            def scores(it):
                u = it - 2
                eng.wait_ge(qT_out, u + 1)
                eng.wait_ge(kT_out, u + 1)
                need(eng, o2lo_made, u)
                eng.sem_inc(pe_seen, 1)
                for g in range(CT):
                    for b in range(4):
                        for r in range(4):
                            rows, cols = slice(r * HD, (r + 1) * HD), slice(b * S, (b + 1) * S)
                            mm = eng.matmul(pa[cols, r, g * S:(g + 1) * S], q_T[rows, g, cols], k_T[rows, g, cols],
                                            start=True, stop=True)
                mm.then_inc(s_done, 1)

            def weighted_sum(it):
                eng.wait_ge(eT_made, it - 1)
                eng.wait_ge(v_out, it - 1)
                eng.sem_inc(pe_seen, 1)
                for g in range(CT):
                    for r in range(4):
                        for b in range(4):
                            keys, ds = slice(b * S, (b + 1) * S), slice(r * HD, (r + 1) * HD)
                            h = 4 * g + r
                            mm = eng.matmul(pa[ds, b, g * S:(g + 1) * S], v[keys, h * HD:(h + 1) * HD],
                                            e_T[keys, (r * CT + g) * S:(r * CT + g + 1) * S], start=True, stop=True)
                mm.then_inc(pv_done, 1)

            def z3_transposes(it):
                u = it - 3
                eng.wait_ge(z3_made, u + 1)
                if isinstance(it, int) and it > NT:
                    eng.wait_ge(x2_made, NT)
                    eng.wait_ge(z3T_out, u + 1)
                else:
                    eng.wait_ge(kT_out, u + 2)
                for c in range(CT):
                    mm = eng.transpose(z3_bank(it)[:, c * P:(c + 1) * P], z3s[:, c * P:(c + 1) * P], ident[:, :])
                mm.then_inc(z3T_done, 1)

            def body(it):
                if has(it, 0):
                    wo_proj(it)
                if isinstance(it, int) and it in (1, 2):
                    z2_transposes(it - 1)
                if has(it, 3):
                    out_proj(it)
                if has(it, 2):
                    qk_transposes(it)
                if has(it, 1):
                    qkv(it, 0)
                if has(it, 2):
                    scores(it)
                if has(it, 1):
                    qkv(it, 1)
                    qkv(it, 2)
                if has(it, 2):
                    weighted_sum(it)
                if not isinstance(it, int) or it == 2:
                    z2_transposes(it)
                if has(it, 3):
                    z3_transposes(it)

            def gate(hf):
                eng.wait_ge(g_split, 2)
                eng.wait_ge(xmlo, hf + 1)
                if hf == 0:
                    eng.wait_ge(qk_out, 2 * NT)
                else:
                    eng.wait_ge(z3T_out, NT + 1)
                for c in range(CT):
                    mm = three(eng, pg[hf][:, :], g_hi[:, c, :], g_lo[:, c, :], xm_hi[:, c, :], xm_lo[:, c, :],
                               c == 0, c == CT - 1)
                mm.then_inc(g_done, 1)

            def gate_scores(hf):
                eng.wait_ge(th_made, hf + 1)
                for t in range(NH):
                    mm = eng.matmul(pg[hf][:, t * E:(t + 1) * E], th[:, t * P:(t + 1) * P], wo2[:, :], start=True, stop=True)
                mm.then_inc(gs_done, 1)

            def choice_transposes(hf):
                eng.wait_ge(choice_made, hf + 1)
                for t in range(NH):
                    mm = eng.transpose(pg[hf][0:E, t * P:(t + 1) * P], choice[:, t, :], ident[:, :])
                mm.then_inc(cT_done, 1)

            def hidden(k):
                e = k % E
                if k in (0, EC, 2 * EC):
                    eng.wait_ge(w_lo_made, 1 + 2 * (k // EC))
                need(eng, h_made, k - 1)
                if k < 2:
                    eng.wait_ge((qT_out, kT_out)[k], NT)
                for c in range(CT):
                    mm = three(eng, ph(k)[:, :], w1(0, e, c), w1(1, e, c), xm_hi[:, c, :], xm_lo[:, c, :],
                               c == 0, c == CT - 1)
                mm.then_inc(h_done, 1)

            def spread(k):
                eng.wait_ge(cb_out, k // E + 1)
                need(eng, pc_out, k)
                eng.matmul(pc[:, :], sel[:, k % E, :], choice_b[:, :], start=True, stop=True).then_inc(pc_done, 1)

            def outputs(k, t):
                hf, e = divmod(k, E)
                cols, slot = slice(t * P, (t + 1) * P), k % RING
                if e == 0:
                    if t == 0:
                        eng.wait_ge(cT_out, hf + 1)
                        if hf == 0:
                            eng.wait_ge(b2_split, 2)
                            eng.wait_ge(o2lo_made, NT)
                    need(eng, y_made, NH * hf - NH + t + 1)
                    eng.matmul(pa[:, t, :], choice_T[:, cols], b2_hi, start=True, stop=False)
                    eng.matmul(pa[:, t, :], choice_T[:, cols], b2_lo, start=False, stop=False)
                if t == 0:
                    eng.wait_ge(hlo, k + 1)
                    if k in (0, EC, 2 * EC):
                        eng.wait_ge(w_lo_made, 2 + 2 * (k // EC))
                mm = three(eng, pa[:, t, :], h_hi[slot][:, cols], h_lo[slot][:, cols], w2(0, e), w2(1, e), False, e == E - 1)
                if e == E - 1 and t < NH - 1:
                    mm.then_inc(y_done, 1)
                return mm

            def expert(k):
                hidden(k)
                spread(k)
                for t in range(NH):
                    mm = outputs(k - RING, t)
                mm.then_inc(h_used, 1)

            def last_outputs(hf, tiles):
                for t in tiles:
                    for k in range(E * hf + E - RING, E * hf + E):
                        mm = outputs(k, t)
                    if t == NH - 1:
                        mm.then_inc(h_used, RING)

            steps(eng, body)
            out_proj(NT)
            qk_transposes(NT)
            qkv(NT, 0)
            scores(NT)
            qkv(NT, 1)
            qkv(NT, 2)
            weighted_sum(NT)
            z3_transposes(NT)
            gate(0)
            out_proj(NT + 1)
            qk_transposes(NT + 1)
            gate_scores(0)
            scores(NT + 1)
            hidden(0)
            choice_transposes(0)
            hidden(1)
            weighted_sum(NT + 1)
            spread(0)
            spread(1)
            out_proj(NT + 2)
            hidden(2)
            spread(2)
            z3_transposes(NT + 1)
            expert(RING)
            z3_transposes(NT + 2)
            for e in range(RING + 1, E):
                expert(e)
            last_outputs(0, range(2))
            gate(1)
            last_outputs(0, range(2, 3))
            gate_scores(1)
            last_outputs(0, range(3, NH))
            hidden(E)
            choice_transposes(1)
            hidden(E + 1)
            spread(E)
            spread(E + 1)
            hidden(E + 2)
            spread(E + 2)
            for e in range(RING, E):
                expert(E + e)
            last_outputs(1, range(NH))


        @block.scalar
        def _(eng):
            eng.sem_inc(z3T_out, 1)

            def weight_split(i):
                eng.wait_ge(w_in[i % 2], 16 * (i // 2 + 1))
                eng.activation(w_hi[i][:, :, :], raw[:, i % 2, :].rearrange("p (c n) -> p c n", c=CT),
                               ACT.Copy).then_inc(whi, 1)

            def qk_evac(it):
                u = it - 2
                eng.wait_ge(qkT_done, 2 * u + 1)
                if isinstance(it, int) and it == 2:
                    eng.wait_ge(scaled, 1)
                need(eng, s_done, u)
                eng.activation(q_T[:, :, :].rearrange("p g t -> p (g t)"), pt[0][:, :], ACT.Copy,
                               scale=qk_w[:, 0:1]).then_inc(qT_out, 1)
                eng.wait_ge(qkT_done, 2 * u + 2)
                eng.activation(k_T[:, :, :].rearrange("p g t -> p (g t)"), pt[1][:, :], ACT.Copy,
                               scale=qk_w[:, 1:2]).then_inc(kT_out, 1)

            def square(it, i):
                eng.wait_ge(qk_out, 2 * (it - 1) + 1 + i)
                eng.activation(sq[:, i * D:(i + 1) * D], qk[:, i, :], ACT.Square).then_inc(sq_made, 1)

            def exps(it):
                eng.wait_ge(shifted, it - 1)
                eng.activation(e[:, :], e[:, :], ACT.Exp).then_inc(e_made, 1)

            def v_evac(it):
                eng.wait_ge(qkv_done, 3 * it)
                need(eng, v_out, it - 1)
                eng.activation(v_raw[:, :], pw[1][:, :], ACT.Copy).then_inc(vr_out, 1)

            def o2_split(it):
                u = it - 2
                eng.wait_ge(pv_done, u + 1)
                need(eng, proj_done, u)
                eng.activation(o2_hi[:, :, :].rearrange("p g (b s) -> p b g s", b=4),
                               pa[:, :, 0:P].rearrange("p b (g s) -> p b g s", g=CT), ACT.Copy).then_inc(o2hi_made, 1)

            def z3_evac(it):
                u = it - 3
                eng.wait_ge(z3T_done, u + 2)
                eng.activation(O_T[:, :, bass.ds(u * P, P)], z3_bank(it)[:, :].rearrange("p (c t) -> p c t", c=CT),
                               ACT.Copy).then_inc(z3T_out, 1)

            def body(it):
                if isinstance(it, int) and it == 0:
                    weight_split(2)
                    weight_split(3)
                if has(it, 2):
                    qk_evac(it)
                if has(it, 1):
                    square(it, 0)
                if has(it, 2):
                    exps(it)
                if has(it, 1):
                    square(it, 1)
                    v_evac(it)
                if has(it, 2):
                    o2_split(it)
                if isinstance(it, int) and it == 1:
                    weight_split(4)
                eng.wait_ge(z2T_done, it + 1)
                need(eng, qkv_done, 3 * it)
                eng.activation(z2_hi[:, :, :].rearrange("p c t -> p (c t)"), pt[0][:, :], ACT.Copy).then_inc(z2hi_made, 1)
                if has(it, 3):
                    z3_evac(it)

            def w_split(i):
                eng.wait_ge(exw_in, 16 * (i + 1))
                src, hi, _ = split_parts(i)
                eng.activation(hi, src, ACT.Copy).then_inc(w_hi_made, 1)

            def xm_split(hf):
                eng.wait_ge(mix_made, NH * (hf + 1))
                if hf:
                    eng.wait_ge(h_done, E)
                eng.activation(xm_hi[:, :, :], O_T[:, :, hf * HT:(hf + 1) * HT], ACT.Copy).then_inc(xmhi, 1)

            def tanh(hf):
                eng.wait_ge(g_done, hf + 1)
                eng.activation(th, pg[hf][:, :], ACT.Tanh, bias=bo1[:, 0:1]).then_inc(th_made, 1)

            def choice_evac(hf):
                eng.wait_ge(cT_done, hf + 1)
                if hf:
                    eng.wait_ge(h_used, 1)
                eng.activation(choice_T, pg[hf][0:E, :], ACT.Copy).then_inc(cT_out, 1)

            def spread_evac(k):
                eng.wait_ge(pc_done, k + 1)
                need(eng, h_made, k - 1)
                eng.activation(chosen[k % 2], pc[:, :], ACT.Copy).then_inc(pc_out, 1)

            def hidden_split(k):
                eng.wait_ge(h_made, k + 1)
                need(eng, h_used, k - RING + 1)
                eng.activation(h_hi[k % RING], h[k % 2], ACT.Copy).then_inc(hhi, 1)

            steps(eng, body)
            xm_split(0)
            eng.wait_ge(ex_in, 6 * 16)
            eng.activation(g_hi[:, :, :], g_raw, ACT.Copy).then_inc(g_split, 1)
            qk_evac(NT)
            square(NT, 0)
            exps(NT)
            square(NT, 1)
            v_evac(NT)
            o2_split(NT)
            z3_evac(NT)
            eng.wait_ge(wo_done, NT)
            w_split(0)
            tanh(0)
            qk_evac(NT + 1)
            exps(NT + 1)
            eng.wait_ge(qkv_done, 3 * NT)
            choice_evac(0)
            w_split(1)
            w_split(2)
            o2_split(NT + 1)
            spread_evac(0)
            hidden_split(0)
            spread_evac(1)
            hidden_split(1)
            eng.wait_ge(proj_done, NT)
            eng.activation(b2_hi, b2, ACT.Copy).then_inc(b2_split, 1)
            spread_evac(2)
            z3_evac(NT + 1)
            hidden_split(2)
            w_split(3)
            spread_evac(RING)
            hidden_split(RING)
            z3_evac(NT + 2)
            w_split(4)
            spread_evac(RING + 1)
            hidden_split(RING + 1)
            w_split(5)
            for k in range(RING + 2, E):
                spread_evac(k)
                hidden_split(k)
            xm_split(1)
            tanh(1)
            choice_evac(1)
            for k in range(E, 2 * E):
                spread_evac(k)
                hidden_split(k)

        @block.vector
        def _(eng):
            count = {"at": 0}

            def weight_split(i):
                eng.wait_ge(whi, i + 1)
                eng.tensor_tensor(w_lo[i][:, :, :], raw[:, i % 2, :].rearrange("p (c n) -> p c n", c=CT),
                                  w_hi[i][:, :, :].bitcast(F32), ALU.subtract).then_inc(wlo, 1)

            def q_evac(it):
                eng.wait_ge(qkv_done, 3 * (it - 1) + 1)
                need(eng, qkT_done, 2 * (it - 1))
                eng.tensor_tensor(qk[:, 0, :], pw[0][:, :], bqkv[:, 0, :], ALU.add).then_inc(qk_out, 1)

            def take_x2(it):
                u = it - 3
                x_u = x_nat[:, bass.ds(u, 1), :]
                eng.wait_ge(x1b_made, u + 1)
                eng.wait_ge(proj_done, u + 1)
                eng.sem_inc(dve_seen, 1)
                eng.tensor_tensor(x_u, pw[1][:, :].unsqueeze(1), x_u, ALU.add).then_inc(x2_made, 1)

            def norms(it, ch, taken=False, ms_too=False):
                def stats_of(k, x):
                    eng.sem_inc(dve_seen, 1)
                    ch.link(eng.bn_stats(stats[:, k, :], x))
                    eng.sem_inc(dve_seen, 1)
                    ch.link(eng.bn_aggr(mv[:, k, :], stats[:, k, :]))

                if has(it, 0):
                    x_t = x_nat[:, bass.ds(it, 1), :]
                    need(eng, x0_made, it)
                    eng.wait_ge(wo_done, it + 1)
                    eng.sem_inc(dve_seen, 1)
                    eng.tensor_tensor(x_t, wo_bank(it)[:, :].unsqueeze(1), x_t, ALU.add).then_inc(x1_made, 1)
                    eng.wait_ge(x1_made, it + 1)
                    stats_of(0, x_t)
                if has(it, 3):
                    u = it - 3
                    x_u = x_nat[:, bass.ds(u, 1), :]
                    if not taken:
                        take_x2(it)
                    eng.wait_ge(x2_made, u + 1)
                    stats_of(1, x_u)
                if ms_too:
                    k_squares(it, ch)
                    ch.link(eng.tensor_scalar(ms[:, 2 * H:2 * H + 1], mv[:, 0, 1:2], LN_EPS, None, ALU.add))
                    rsqrt(eng, ch, rms[:, :], ms[:, :], tmp32[:, :])
                else:
                    k = slice(0 if has(it, 0) else 1, 2 if has(it, 3) else 1)
                    ch.link(eng.tensor_scalar(mv[:, k, 1], mv[:, k, 1], LN_EPS, None, ALU.add))
                    rsqrt(eng, ch, rstd[:, k], mv[:, k, 1], tmp[:, k])
                scale = rms[:, 2 * H:2 * H + 1] if ms_too else rstd[:, 0:1]
                if has(it, 1) and not (isinstance(it, int) and it == 1):
                    q_evac(it)
                if has(it, 0):
                    need(eng, z2T_done, it)
                    eng.tensor_scalar(z2[:, :].unsqueeze(1), x_t, mv[:, 0, 0:1], scale,
                                      ALU.subtract, ALU.mult).then_inc(z2_made, 1)
                if has(it, 3):
                    need(eng, z3T_done, u + 1)
                    eng.tensor_scalar(z3s[:, :].unsqueeze(1), x_u, mv[:, 1, 0:1], rstd[:, 1:2],
                                      ALU.subtract, ALU.mult).then_inc(z3_made, 1)
                    for i, one in enumerate((mv[:, 1, 0:1], rstd[:, 1:2])):
                        eng.tensor_copy(ln3[:, bass.ds(u, 1), i], one).then_inc(step, 1)
                        ch.k += 1

            def softmax(it, ch):
                u = it - 2
                s_p = pa[:, :, 0:P].rearrange("p r (g k) -> p r g k", g=CT)
                e4 = e[:, :].rearrange("p (r g k) -> p r g k", r=4, g=CT)
                eng.wait_ge(s_done, u + 1)
                ch.link(eng.tensor_reduce(mx[:, :], s_p, AX.X, ALU.max))
                m4 = mx[:, :].rearrange("p (r g) -> p r g", r=4).unsqueeze(3).broadcast_to([P, 4, CT, S])
                eng.tensor_tensor(e4, s_p, m4, ALU.subtract).then_inc(shifted, 1)
                eng.wait_ge(e_made, u + 1)
                e3 = e[:, :].rearrange("p (h k) -> p h k", k=S)
                ch.link(eng.tensor_reduce(sm[:, :], e3, AX.X, ALU.add))
                ch.link(eng.reciprocal(rs[:, :], sm[:, :]))
                ch.link(eng.tensor_tensor(e3, e3, rs[:, :].unsqueeze(2).broadcast_to([P, H, S]), ALU.mult))
                need(eng, pv_done, u)
                eng.transpose(e_T[:, :], e[:, :]).then_inc(eT_made, 1)

            def k_squares(it, ch):
                u = it - 1
                eng.wait_ge(qkv_done, 3 * u + 2)
                eng.tensor_tensor(qk[:, 1, :], k_bank(it)[:, :], bqkv[:, 1, :], ALU.add).then_inc(qk_out, 1)
                eng.wait_ge(sq_made, 2 * u + 2)
                ch.link(eng.tensor_reduce(ms[:, 0:2 * H], sq[:, :].rearrange("p (h d) -> p h d", d=HD), AX.X, ALU.add))
                ch.link(eng.tensor_scalar(ms[:, 0:2 * H], ms[:, 0:2 * H], 1.0 / HD, RMS_EPS, ALU.mult, ALU.add))

            def o2_split(it):
                eng.wait_ge(o2hi_made, it - 1)
                eng.tensor_tensor(o2_lo[:, :, :].rearrange("p g (b s) -> p b g s", b=4),
                                  pa[:, :, 0:P].rearrange("p b (g s) -> p b g s", g=CT),
                                  o2_hi[:, :, :].rearrange("p g (b s) -> p b g s", b=4).bitcast(F32),
                                  ALU.subtract).then_inc(o2lo_made, 1)

            def qk_norm():
                qk3 = qk[:, :, :].rearrange("p i (h d) -> p (i h) d", d=HD)
                eng.tensor_tensor(qk3, qk3, rms[:, 0:2 * H].unsqueeze(2).broadcast_to([P, 2 * H, HD]),
                                  ALU.mult).then_inc(qkn_made, 1)

            ch3 = Chain(eng, step3)

            def body(it):
                whole = not isinstance(it, int)
                ch = Chain(eng, step, count["at"] if not whole else count["at"] + (it - 3) * PER_STEP)
                second = isinstance(it, int) and it == 1
                if second:
                    q_evac(it)
                norms(it, ch, ms_too=second)
                if isinstance(it, int) and it == 0:
                    weight_split(2)
                if has(it, 2):
                    softmax(it, ch)
                if has(it, 1) and not second:
                    k_squares(it, ch)
                    rsqrt(eng, ch, rms[:, 0:2 * H], ms[:, 0:2 * H], tmp32[:, 0:2 * H])
                if has(it, 2):
                    o2_split(it)
                if has(it, 1):
                    qk_norm()
                eng.wait_ge(z2hi_made, it + 1)
                eng.tensor_tensor(z2_lo[:, :, :].rearrange("p c t -> p (c t)"), pt[0][:, :],
                                  z2_hi[:, :, :].rearrange("p c t -> p (c t)").bitcast(F32), ALU.subtract).then_inc(z2lo_made, 1)
                if isinstance(it, int) and it == 0:
                    weight_split(3)
                    eng.wait_ge(small_in, 4 * 16)
                    eng.tensor_scalar(qk_w[:, 0:1], qk_w[:, 0:1], SCALE, None, ALU.mult).then_inc(scaled, 1)
                    for k in range(E):
                        eng.memset(rank[:, k:k + 1], float(E - k))
                    ch3.link(eng.tensor_copy(sel[:, :, :], ident[0:E, 0:E].unsqueeze(2).broadcast_to([E, E, P])))
                if whole:
                    assert ch.k == PER_STEP
                    count["at"] += (NT - 3) * PER_STEP
                else:
                    count["at"] += ch.k

            RSQRT = 2 + 3 * 3
            PER_STEP = 2 + 2 + (1 + RSQRT) + 2 + 1 + 3 + (2 + RSQRT)

            def w_split(i):
                eng.wait_ge(w_hi_made, i + 1)
                src, hi, lo = split_parts(i)
                eng.tensor_tensor(lo, src, hi.bitcast(F32), ALU.subtract).then_inc(w_lo_made, 1)

            def choose(hf):
                eng.wait_ge(gs_done, hf + 1)
                bc = [P, NH, E]
                ch3.link(eng.tensor_tensor(gs[:, :, :], pg[hf][:, 0:NH * E].rearrange("p (t e) -> p t e", t=NH),
                                           bo2[:, :].unsqueeze(1).broadcast_to(bc), ALU.add))
                ch3.link(eng.tensor_reduce(top[:, :], gs[:, :, :], AX.X, ALU.max))
                ch3.link(eng.tensor_tensor(key[:, :, :], gs[:, :, :], top[:, :].unsqueeze(2).broadcast_to(bc), ALU.is_equal))
                ch3.link(eng.tensor_tensor(key[:, :, :], key[:, :, :], rank[:, :].unsqueeze(1).broadcast_to(bc), ALU.mult))
                ch3.link(eng.tensor_reduce(top[:, :], key[:, :, :], AX.X, ALU.max))
                eng.tensor_tensor(choice[:, :, :], key[:, :, :], top[:, :].unsqueeze(2).broadcast_to(bc),
                                  ALU.is_equal).then_inc(choice_made, 1)

            def choice_copy(hf):
                eng.wait_ge(cT_out, hf + 1)
                if hf:
                    eng.wait_ge(pc_done, E)
                eng.tensor_copy(choice_b[:, :], choice_T.bitcast(F32)).then_inc(cb_out, 1)

            def hidden_rows(k):
                eng.wait_ge(pc_out, k + 1)
                eng.wait_ge(h_done, k + 1)
                need(eng, hlo, k - 1)
                eng.scalar_tensor_tensor(out=h[k % 2], in0=ph(k)[:, :], scalar=b1[:, k % E:k % E + 1],
                                         in1=chosen[k % 2], op0=ALU.add, op1=ALU.mult).then_inc(h_made, 1)
                eng.wait_ge(hhi, k + 1)
                eng.tensor_tensor(h_lo[k % RING], h[k % 2], h_hi[k % RING].bitcast(F32), ALU.subtract).then_inc(hlo, 1)

            def y_take(hf, t):
                k = NH * hf + t
                if t < NH - 1:
                    eng.wait_ge(y_done, (NH - 1) * hf + t + 1)
                else:
                    eng.wait_ge(h_used, E * (hf + 1))
                eng.wait_ge(zn_made, k + 1)
                eng.tensor_tensor(y(k), pa[:, t, :], y(k), ALU.add).then_inc(y_made, 1)

            def y_stats(hf, t):
                eng.wait_ge(y_made, NH * hf + t + 1)
                ch3.link(eng.bn_stats(stats4[:, t, :], y(NH * hf + t)))
                ch3.link(eng.bn_aggr(mv4[:, t, :], stats4[:, t, :]))
                eng.sem_inc(stats_made, 1)

            def y_centre(hf, t):
                k = NH * hf + t
                if k == 0:
                    eng.wait_ge(ln_in, 2 * 16)
                ch3.link(eng.scalar_tensor_tensor(out=y(k), in0=y(k), scalar=mv4[:, t, 0:1], in1=gamma,
                                                  op0=ALU.subtract, op1=ALU.mult))

            def y_deviations():
                ch3.link(eng.tensor_scalar(mv4[:, :, 1], mv4[:, :, 1], LN_EPS, None, ALU.add))
                rsqrt(eng, ch3, rstd4[:, :], mv4[:, :, 1], tmp4[:, :])

            def y_end(hf, t):
                k = NH * hf + t
                eng.wait_ge(xb_made, k + 1)
                eng.scalar_tensor_tensor(out=y(k), in0=y(k), scalar=rstd4[:, t:t + 1], in1=x_nat[:, k, :],
                                         op0=ALU.mult, op1=ALU.add).then_inc(fin, 1)

            steps(eng, body)
            ch = Chain(eng, step, count["at"])
            norms(NT, ch)
            softmax(NT, ch)
            k_squares(NT, ch)
            rsqrt(eng, ch, rms[:, 0:2 * H], ms[:, 0:2 * H], tmp32[:, 0:2 * H])
            o2_split(NT)
            qk_norm()
            w_split(0)
            take_x2(NT + 1)
            eng.wait_ge(ex_in, 6 * 16)
            choose(0)
            softmax(NT + 1, ch)
            choice_copy(0)
            w_split(1)
            o2_split(NT + 1)
            hidden_rows(0)
            w_split(2)
            hidden_rows(1)
            norms(NT + 1, ch, True)
            take_x2(NT + 2)
            eng.wait_ge(b2_split, 1)
            eng.tensor_tensor(b2_lo, b2, b2_hi.bitcast(F32), ALU.subtract).then_inc(b2_split, 1)
            hidden_rows(2)
            norms(NT + 2, ch, True)
            w_split(3)
            hidden_rows(RING)
            w_split(4)
            hidden_rows(RING + 1)
            w_split(5)
            for e_ in range(RING + 2, E):
                hidden_rows(e_)
            eng.wait_ge(xmhi, 2)
            eng.tensor_tensor(xm_lo[:, :, :], O_T[:, :, HT:T], xm_hi[:, :, :].bitcast(F32), ALU.subtract).then_inc(xmlo, 1)
            y_take(0, 0)
            y_take(0, 1)
            y_take(0, 2)
            choose(1)
            y_take(0, 3)
            choice_copy(1)
            for e_ in range(E):
                hidden_rows(E + e_)
                if 0 < e_ <= NH:
                    y_stats(0, e_ - 1)
                    y_centre(0, e_ - 1)
                if e_ == NH + 1:
                    y_deviations()
                    y_end(0, 0)
                    y_end(0, 1)
                if e_ == NH + 2:
                    y_end(0, 2)
                    y_end(0, 3)
            for t in range(NH):
                y_take(1, t)
                y_stats(1, t)
                if t == 2:
                    y_centre(1, t)
            y_centre(1, NH - 1)
            y_deviations()
            for t in (2, 3, 0, 1):
                if t < 2:
                    eng.wait_ge(centred, 2 * t + 2)
                y_end(1, t)


def kernel(**inputs):
    import concourse.bacc as bacc
    from concourse.bass_utils import run_bass_kernel_spmd

    nc = bacc.Bacc("TRN2", target_bir_lowering=False, num_devices=1)
    a = {k: np.asarray(v) for k, v in inputs.items()}

    def rows(w):
        return w.reshape(-1, P, w.shape[1]).transpose(1, 0, 2).reshape(P, -1)

    def cols(b):
        return b.reshape(-1, P).T

    ctx = a["ctx_1024"]
    laid = {
        "x": a["x"].reshape(NT, P, D).transpose(1, 0, 2),
        "ctx": ctx[:, :SM].reshape(NPAIR, 2 * SM, CT, P).transpose(0, 3, 2, 1).reshape(NPAIR, P, CT * 2 * SM),
        "tail": ctx[:, SM].reshape(B, CT, P).transpose(2, 1, 0),
        "mask": a["mask_1x1xSxS2_ff0"].reshape(S, SK),
        "wq": rows(a["L0_xattn_Wq"].T), "wk": rows(a["L0_xattn_Wk"].T), "wv": rows(a["L0_xattn_Wv"].T),
        "w5": np.stack([rows(w) for w in [a["L0_xattn_Wo"].T, *np.split(a["L0_attn_Wqkv"].T, 3, axis=1), a["L0_attn_Wproj"].T]]),
        "bo": a["L0_xattn_bo"], "bqkv": a["L0_attn_bqkv"], "bproj": a["L0_attn_bproj"],
        "qk_w": np.stack([np.tile(a["L0_attn_qn_w"], P // HD), np.tile(a["L0_attn_kn_w"], P // HD)], axis=1),
        "w1": np.stack([rows(w.transpose(1, 0, 2).reshape(D, -1)) for w in np.split(a["L0_ffn_W1"], 3)]),
        "w2": np.stack([w.transpose(1, 0, 2).reshape(DM, -1) for w in np.split(a["L0_ffn_W2"], 3)]),
        "wo1": rows(a["L0_ffn_Wo1"]), "wo2": a["L0_ffn_Wo2"],
        "b1": a["L0_ffn_b1"].T, "bo1": a["L0_ffn_bo1"].reshape(DM, 1), "b2": a["L0_ffn_b2"], "bo2": a["L0_ffn_bo2"],
        "mixw": a["L0_ffn_mix_kernel"].reshape(3, CT, P).transpose(2, 0, 1).reshape(P, 3 * CT),
        "gamma": a["L0_ffn_gamma"], "beta": a["L0_ffn_beta"],
        "bq": cols(a["L0_xattn_bq"]), "bk": cols(a["L0_xattn_bk"]), "bv": cols(a["L0_xattn_bv"]),
    }
    laid = {k: np.ascontiguousarray(v) for k, v in laid.items()}
    io = {k: nc.dram_tensor(k + "_dram", v.shape, mybir.dt.from_np(v.dtype), kind="ExternalInput").ap() for k, v in laid.items()}
    out = nc.dram_tensor("out_dram", (NT, P, D), F32, kind="ExternalOutput").ap()
    build(nc, io, out)
    r = run_bass_kernel_spmd(nc, [{k + "_dram": v for k, v in laid.items()}], core_ids=[0])
    return r.results[0]["out_dram"].reshape(B, S, D)
```
